# Optimizing a Trainium2 kernel written in Bass

```python
import numpy as np
import jax
import jax.numpy as jnp

def _softmax(x, axis=-1):
    return jax.nn.softmax(x, axis=axis)

def _gelu(x):
    return jax.nn.gelu(x, approximate=True)

def _silu(x):
    return jax.nn.silu(x)

def _sigmoid(x):
    return jax.nn.sigmoid(x)

def _layernorm(x, axis=-1, eps=1e-05):
    m = jnp.mean(x, axis=axis, keepdims=True)
    v = jnp.var(x, axis=axis, keepdims=True)
    return (x - m) / jnp.sqrt(v + eps)

def _scatter_add(tgt, idx, src, axis=0):
    return tgt.at[idx].add(src)

def _segment_sum(src, seg, n):
    return jax.ops.segment_sum(src, seg, n)
kernel_name = 'mk_decoder_postln_d4_seqx_r4_945b3a'

def setup_inputs(seed: int=0):
    np.random.seed(seed)
    _w = jnp.asarray

    def _rec_inputs():
        import jax
        import jax.numpy as jnp
        _rk = jax.random.key(seed)
        x = 7.22e-05 + 1 * jax.random.normal(jax.random.fold_in(_rk, 1), (16, 128, 256), jnp.float32)
        _lenS = 128 - jax.random.randint(jax.random.fold_in(_rk, 7), (16,), 0, max(1, 128 // 4) + 1, jnp.int32)
        _lenS2 = 128 - jax.random.randint(jax.random.fold_in(_rk, 8), (16,), 0, max(1, 128 // 4) + 1, jnp.int32)
        _ctx_1024P = jax.random.normal(jax.random.fold_in(_rk, 11), (16, 16, 256), jnp.float32)
        _ctx_1024c = jax.random.dirichlet(jax.random.fold_in(_rk, 511), 0.3 * jnp.ones((16,), jnp.float32), (16, 128))
        _ctx_1024t = jnp.einsum('bsk,bkd->bsd', _ctx_1024c, _ctx_1024P)
        _ctx_1024t = _ctx_1024t * jax.lax.rsqrt(jnp.mean(jnp.square(_ctx_1024t)) + 1e-12) * 0.953939
        ctx_1024 = 4.13588e-05 + 0.999923 * (_ctx_1024t + 0.3 * jax.random.normal(jax.random.fold_in(_rk, 611), (16, 128, 256), jnp.float32))
        return (x, ctx_1024)
    x, ctx_1024 = _rec_inputs()

    def _L0_attn_setup():
        import jax, jax.numpy as jnp
        import numpy as np
        EMBED_DIM = 256
        NUM_HEADS = 16
        HEAD_DIM = EMBED_DIM // NUM_HEADS
        KERNEL_SIZE = 64
        B, L = (2, 512)
        key = jax.random.key(seed)
        ks = jax.random.split(key, 6)
        x = jax.random.normal(ks[0], (B, L, EMBED_DIM), dtype=jnp.float32)
        qkv_w = jax.random.normal(ks[1], (EMBED_DIM, 3 * EMBED_DIM), dtype=jnp.float32) / np.sqrt(EMBED_DIM)
        qkv_b = jnp.zeros((3 * EMBED_DIM,), dtype=jnp.float32)
        out_w = jax.random.normal(ks[2], (EMBED_DIM, EMBED_DIM), dtype=jnp.float32) / np.sqrt(EMBED_DIM)
        out_b = jnp.zeros((EMBED_DIM,), dtype=jnp.float32)
        proj = jax.random.normal(ks[3], (NUM_HEADS, HEAD_DIM, KERNEL_SIZE), dtype=jnp.float32) / np.sqrt(HEAD_DIM)
        return {'x': x, 'qkv_w': qkv_w, 'qkv_b': qkv_b, 'out_w': out_w, 'out_b': out_b, 'proj': proj}
    _L0_attn_all = _L0_attn_setup()
    _L0_attn_in = {k: v for k, v in _L0_attn_all.items() if k in ('qkv_w', 'qkv_b', 'out_w', 'out_b', 'proj')}
    del _L0_attn_all

    def _L0_xattn_setup():
        import jax, jax.numpy as jnp
        import numpy as np
        BETA = 256
        NUM_HEADS = 16
        NORM = (BETA // NUM_HEADS) ** (-0.5)
        key = jax.random.key(seed)
        ks = jax.random.split(key, 6)
        B, N = (4, 512)
        D_in_q = D_in_k = D_in_v = 256
        D_out_k = D_out_v = 256
        q = jax.random.normal(ks[0], (B, N, D_in_q), dtype=jnp.float32)
        k = jax.random.normal(ks[1], (B, N, D_in_k), dtype=jnp.float32)
        v = jax.random.normal(ks[2], (B, N, D_in_v), dtype=jnp.float32)
        Wq = jax.random.normal(ks[3], (D_out_k, D_in_q), dtype=jnp.float32) * D_in_q ** (-0.5)
        Wk = jax.random.normal(ks[4], (D_out_k, D_in_k), dtype=jnp.float32) * D_in_k ** (-0.5)
        Wv = jax.random.normal(ks[5], (D_out_v, D_in_v), dtype=jnp.float32) * D_in_v ** (-0.5)
        return {'q': q, 'k': k, 'v': v, 'Wq': Wq, 'Wk': Wk, 'Wv': Wv}
    _L0_xattn_all = _L0_xattn_setup()
    _L0_xattn_in = {k: v for k, v in _L0_xattn_all.items() if k in ('Wq', 'Wk', 'Wv')}
    del _L0_xattn_all

    def _L0_ffn_setup():
        import jax, jax.numpy as jnp
        import numpy as np
        S, B, H = (512, 1, 256)
        N_HEADS = 16
        HEAD_DIM = H // N_HEADS
        E, K, F = (8, 2, 512)
        EPS = 1e-05

        def layernorm(x, w, b):
            mu = jnp.mean(x, axis=-1, keepdims=True)
            var = jnp.mean(jnp.square(x - mu), axis=-1, keepdims=True)
            return (x - mu) * jax.lax.rsqrt(var + EPS) * w + b
        key = jax.random.key(seed)
        ks = jax.random.split(key, 8)
        std = 0.02
        return {'x': jax.random.normal(ks[0], (S, B, H), dtype=jnp.float32), 'ln1_w': jnp.ones((H,), jnp.float32), 'ln1_b': jnp.zeros((H,), jnp.float32), 'in_proj_w': jax.random.normal(ks[1], (3 * H, H), jnp.float32) * std, 'in_proj_b': jnp.zeros((3 * H,), jnp.float32), 'out_proj_w': jax.random.normal(ks[2], (H, H), jnp.float32) * std, 'out_proj_b': jnp.zeros((H,), jnp.float32), 'ln2_w': jnp.ones((H,), jnp.float32), 'ln2_b': jnp.zeros((H,), jnp.float32), 'router_w': jax.random.normal(ks[3], (E, H), jnp.float32) * std, 'w1': jax.random.normal(ks[4], (E, H, F), jnp.float32) * std, 'w2': jax.random.normal(ks[5], (E, F, H), jnp.float32) * std}
    _L0_ffn_all = _L0_ffn_setup()
    _L0_ffn_in = {k: v for k, v in _L0_ffn_all.items() if k in ('ln1_w', 'ln1_b', 'in_proj_w', 'in_proj_b', 'out_proj_w', 'out_proj_b', 'ln2_w', 'ln2_b', 'router_w', 'w1', 'w2')}
    del _L0_ffn_all

    def _L1_attn_setup():
        import jax, jax.numpy as jnp
        import numpy as np
        D_MODEL = 256
        N_HEADS = 4
        N_KV_HEADS = 2
        HEAD_DIM = D_MODEL // N_HEADS
        N_REP = N_HEADS // N_KV_HEADS
        EPS_RMS = 1e-06
        EPS_NORM = 1e-12

        def _rmsnorm(x, w):
            var = jnp.mean(jnp.square(x), axis=-1, keepdims=True)
            return x * jax.lax.rsqrt(var + EPS_RMS) * w

        def _l2norm(x):
            n = jnp.sqrt(jnp.sum(jnp.square(x), axis=-1, keepdims=True))
            return x / jnp.maximum(n, EPS_NORM)
        key = jax.random.key(seed)
        ks = jax.random.split(key, 8)
        B, L = (2, 1024)
        s = 0.02
        return {'x': jax.random.normal(ks[0], (B, L, D_MODEL), dtype=jnp.float32), 'norm_w': jnp.ones((D_MODEL,), dtype=jnp.float32), 'Wq': jax.random.normal(ks[1], (D_MODEL, N_HEADS * HEAD_DIM), dtype=jnp.float32) * s, 'Wk': jax.random.normal(ks[2], (D_MODEL, N_KV_HEADS * HEAD_DIM), dtype=jnp.float32) * s, 'Wv': jax.random.normal(ks[3], (D_MODEL, N_KV_HEADS * HEAD_DIM), dtype=jnp.float32) * s, 'Wo': jax.random.normal(ks[4], (N_HEADS * HEAD_DIM, D_MODEL), dtype=jnp.float32) * s, 'gate': jnp.asarray(0.1, dtype=jnp.float32), 'log_temperature': jnp.asarray(np.log(10.0), dtype=jnp.float32)}
    _L1_attn_all = _L1_attn_setup()
    _L1_attn_in = {k: v for k, v in _L1_attn_all.items() if k in ('norm_w', 'Wq', 'Wk', 'Wv', 'Wo', 'gate', 'log_temperature')}
    del _L1_attn_all

    def _L1_xattn_setup():
        import jax, jax.numpy as jnp
        import numpy as np
        B_SZ, T_LEN, C_DIM = (4, 1024, 256)

        def _wkv_scan(ek, v, ew):

            def step(carry, xt):
                A, Bd = carry
                ekt, vt = xt
                out = (A, Bd)
                A2 = ew * A + ekt * vt
                B2 = ew * Bd + ekt
                return ((A2, B2), out)
            init = (jnp.zeros_like(ek[:, 0]), jnp.zeros_like(ek[:, 0]))
            xs = (jnp.moveaxis(ek, 1, 0), jnp.moveaxis(v, 1, 0))
            _, (A, Bd) = jax.lax.scan(step, init, xs)
            return (jnp.moveaxis(A, 0, 1), jnp.moveaxis(Bd, 0, 1))

        def _birwkv(r, k, v, w, u):
            wc = w.reshape(-1)
            uc = u.reshape(-1)
            ew = jnp.exp(wc)
            ek = jnp.exp(k)
            Af, Bf = _wkv_scan(ek, v, ew)
            Ab, Bb = _wkv_scan(ek[:, ::-1], v[:, ::-1], ew)
            Ab = Ab[:, ::-1]
            Bb = Bb[:, ::-1]
            cur = jnp.exp(uc + k)
            wkv = (Af + Ab + cur * v) / (Bf + Bb + cur)
            return jax.nn.sigmoid(r) * wkv
        key = jax.random.key(seed)
        k1, k2, k3, k4, k5 = jax.random.split(key, 5)
        r = jax.random.normal(k1, (B_SZ, T_LEN, C_DIM), dtype=jnp.float32)
        k = jax.random.normal(k2, (B_SZ, T_LEN, C_DIM), dtype=jnp.float32)
        v = jax.random.normal(k3, (B_SZ, T_LEN, C_DIM), dtype=jnp.float32)
        w = -(0.3 + jax.random.uniform(k4, (1, 1, C_DIM), dtype=jnp.float32))
        u = jax.random.normal(k5, (1, 1, C_DIM), dtype=jnp.float32) * 0.1
        return {'r': r, 'k': k, 'v': v, 'w': w, 'u': u}
    _L1_xattn_all = _L1_xattn_setup()
    _L1_xattn_in = {k: v for k, v in _L1_xattn_all.items() if k in ('w', 'u')}
    del _L1_xattn_all

    def _L1_ffn_setup():
        import jax, jax.numpy as jnp
        import numpy as np
        B, T, D, F, E = (4, 512, 256, 1024, 8)
        key = jax.random.key(seed)
        k = jax.random.split(key, 7)
        x = jax.random.normal(k[0], (B, T, D), dtype=jnp.float32)
        wr = jax.random.normal(k[1], (D,), dtype=jnp.float32)
        br = jnp.zeros((), dtype=jnp.float32)
        W1 = jax.random.normal(k[2], (E, D, F), dtype=jnp.float32) * 0.02
        b1 = jnp.zeros((E, F), dtype=jnp.float32)
        W2 = jax.random.normal(k[3], (E, F, D), dtype=jnp.float32) * 0.02
        b2 = jnp.zeros((E, D), dtype=jnp.float32)
        return {'x': x, 'wr': wr, 'br': br, 'W1': W1, 'b1': b1, 'W2': W2, 'b2': b2}
    _L1_ffn_all = _L1_ffn_setup()
    _L1_ffn_in = {k: v for k, v in _L1_ffn_all.items() if k in ('wr', 'br', 'W1', 'b1', 'W2', 'b2')}
    del _L1_ffn_all

    def _L2_attn_setup():
        import jax, jax.numpy as jnp
        import numpy as np
        from jax import lax
        B, N, C, RED = (8, 512, 256, 4)
        GN_EPS = 1e-05

        def _conv1d(x, w):
            return lax.conv_general_dilated(x, w, (1,), [(1, 1)], dimension_numbers=('NCH', 'OIH', 'NCH'))

        def _ode_func(A, conv1_w, gn_g, gn_b, conv2_w, conv2_b):
            h = _conv1d(A[:, None, :], conv1_w)
            b, _, n = h.shape
            hg = h.reshape(b, 2, 2, n)
            mu = hg.mean((2, 3), keepdims=True)
            var = hg.var((2, 3), keepdims=True)
            h = ((hg - mu) * lax.rsqrt(var + GN_EPS)).reshape(b, 4, n)
            h = jax.nn.relu(h * gn_g[None, :, None] + gn_b[None, :, None])
            y = _conv1d(h, conv2_w) + conv2_b[None, :, None]
            return y[:, 0, :]
        key = jax.random.key(seed)
        ks = jax.random.split(key, 8)
        s = lambda k, shp, sc: jax.random.normal(k, shp, jnp.float32) * sc
        return dict(x=jax.random.normal(ks[0], (B, N, C), jnp.float32), qkv_w=s(ks[1], (C, 3 * C), 0.02), c1=jnp.float32(0.01 ** 2), c2=jnp.float32(0.03 ** 2), conv1_w=s(ks[2], (4, 1, 3), 0.3), gn_g=jnp.ones(4, jnp.float32), gn_b=jnp.zeros(4, jnp.float32), conv2_w=s(ks[3], (1, 4, 3), 0.3), conv2_b=jnp.zeros(1, jnp.float32), ch_w1=s(ks[4], (C, C // RED), 0.02), ch_b1=jnp.zeros(C // RED, jnp.float32), ch_w2=s(ks[5], (C // RED, C), 0.02), ch_b2=jnp.zeros(C, jnp.float32), proj_w=s(ks[6], (C, C), 0.02), proj_b=jnp.zeros(C, jnp.float32))
    _L2_attn_all = _L2_attn_setup()
    _L2_attn_in = {k: v for k, v in _L2_attn_all.items() if k in ('qkv_w', 'c1', 'c2', 'conv1_w', 'gn_g', 'gn_b', 'conv2_w', 'conv2_b', 'ch_w1', 'ch_b1', 'ch_w2', 'ch_b2', 'proj_w', 'proj_b')}
    del _L2_attn_all

    def _L2_xattn_setup():
        import jax, jax.numpy as jnp
        import numpy as np
        EMBED_DIM = 256
        NUM_HEADS = 16
        HEAD_DIM = EMBED_DIM // NUM_HEADS

        def _split_heads(x):
            B, S, D = x.shape
            return x.reshape(B, S, NUM_HEADS, HEAD_DIM).transpose(0, 2, 1, 3)
        key = jax.random.key(seed)
        ks = jax.random.split(key, 11)
        B, S, D = (4, 512, EMBED_DIM)
        s = 1.0 / np.sqrt(D)
        return {'query': jax.random.normal(ks[0], (B, S, D), jnp.float32), 'key': jax.random.normal(ks[1], (B, S, D), jnp.float32), 'value': jax.random.normal(ks[2], (B, S, D), jnp.float32), 'Wq': jax.random.normal(ks[3], (D, D), jnp.float32) * s, 'bq': jnp.zeros((D,), jnp.float32), 'Wk': jax.random.normal(ks[4], (D, D), jnp.float32) * s, 'bk': jnp.zeros((D,), jnp.float32), 'Wv': jax.random.normal(ks[5], (D, D), jnp.float32) * s, 'bv': jnp.zeros((D,), jnp.float32), 'Wo': jax.random.normal(ks[6], (D, D), jnp.float32) * s, 'bo': jnp.zeros((D,), jnp.float32)}
    _L2_xattn_all = _L2_xattn_setup()
    _L2_xattn_in = {k: v for k, v in _L2_xattn_all.items() if k in ('Wq', 'bq', 'Wk', 'bk', 'Wv', 'bv', 'Wo', 'bo')}
    del _L2_xattn_all

    def _L2_ffn_setup():
        import jax, jax.numpy as jnp
        import numpy as np
        D_MODEL = 256
        H_SHARED = 512
        H_ROUTED = 256
        N_EXPERTS = 8
        TOP_K = 2
        key = jax.random.key(seed)
        ks = jax.random.split(key, 8)
        B, T = (2, 512)
        sc_d = 1.0 / np.sqrt(D_MODEL)
        sc_hs = 1.0 / np.sqrt(H_SHARED)
        sc_hr = 1.0 / np.sqrt(H_ROUTED)
        return {'x': jax.random.normal(ks[0], (B, T, D_MODEL), dtype=jnp.float32), 'router_w': jax.random.normal(ks[1], (N_EXPERTS, D_MODEL), dtype=jnp.float32) * sc_d, 'router_bias': jnp.zeros((N_EXPERTS,), dtype=jnp.float32), 'sw1': jax.random.normal(ks[2], (D_MODEL, H_SHARED), dtype=jnp.float32) * sc_d, 'sw3': jax.random.normal(ks[3], (D_MODEL, H_SHARED), dtype=jnp.float32) * sc_d, 'sw2': jax.random.normal(ks[4], (H_SHARED, D_MODEL), dtype=jnp.float32) * sc_hs, 'ew1': jax.random.normal(ks[5], (N_EXPERTS, D_MODEL, H_ROUTED), dtype=jnp.float32) * sc_d, 'ew2': jax.random.normal(ks[6], (N_EXPERTS, H_ROUTED, D_MODEL), dtype=jnp.float32) * sc_hr}
    _L2_ffn_all = _L2_ffn_setup()
    _L2_ffn_in = {k: v for k, v in _L2_ffn_all.items() if k in ('router_w', 'router_bias', 'sw1', 'sw3', 'sw2', 'ew1', 'ew2')}
    del _L2_ffn_all

    def _L3_attn_setup():
        import math
        import jax, jax.numpy as jnp
        import numpy as np
        D_MODEL = 256
        D_STATE = 16
        D_CONV = 4
        EXPAND = 2
        D_INNER = D_MODEL * EXPAND
        B_SZ = 2
        L_SEQ = 512
        DT_MIN = 0.001
        DT_MAX = 0.1

        def _silu(v):
            return v * jax.nn.sigmoid(v)

        def _mamba(x, in_proj_w, conv_w, conv_b, x_proj_w, dt_proj_w, dt_proj_b, A_log, D, out_proj_w):
            xz = jnp.einsum('bld,ed->ble', x, in_proj_w)
            x_in, z = jnp.split(xz, 2, axis=-1)
            xc = jnp.swapaxes(x_in, 1, 2)
            xc = jax.lax.conv_general_dilated(xc, conv_w, window_strides=(1,), padding=[(D_CONV - 1, 0)], dimension_numbers=('NCH', 'OIH', 'NCH'), feature_group_count=D_INNER)
            xc = xc + conv_b[None, :, None]
            x_in = _silu(jnp.swapaxes(xc, 1, 2))
            dbc = jnp.einsum('bld,ed->ble', x_in, x_proj_w)
            delta_in = dbc[..., :D_INNER]
            Bp = dbc[..., D_INNER:D_INNER + D_STATE]
            Cp = dbc[..., D_INNER + D_STATE:]
            delta = jax.nn.softplus(jnp.einsum('bld,ed->ble', delta_in, dt_proj_w) + dt_proj_b)
            A = -jnp.exp(A_log)

            def step(h, inp):
                dt, bt, ct, xt = inp
                dA = jnp.exp(dt[:, :, None] * A[None])
                h = dA * h + dt[:, :, None] * bt[:, None, :] * xt[:, :, None]
                y = jnp.einsum('bds,bs->bd', h, ct) + D * xt
                return (h, y)
            tm = lambda a: jnp.swapaxes(a, 0, 1)
            h0 = jnp.zeros((x.shape[0], D_INNER, D_STATE), x.dtype)
            _, y = jax.lax.scan(step, h0, (tm(delta), tm(Bp), tm(Cp), tm(x_in)))
            y = jnp.swapaxes(y, 0, 1)
            return jnp.einsum('ble,de->bld', y * _silu(z), out_proj_w)
        key = jax.random.key(seed)
        ks = jax.random.split(key, 8)

        def lin(k, out_f, in_f):
            return jax.random.normal(k, (out_f, in_f), jnp.float32) / np.sqrt(in_f)
        x = jax.random.normal(ks[0], (B_SZ, L_SEQ, D_MODEL), jnp.float32)
        in_proj_w = lin(ks[1], 2 * D_INNER, D_MODEL)
        conv_w = jax.random.normal(ks[2], (D_INNER, 1, D_CONV), jnp.float32) / np.sqrt(D_CONV)
        conv_b = jnp.zeros((D_INNER,), jnp.float32)
        x_proj_w = lin(ks[3], 2 * D_STATE + D_INNER, D_INNER)
        dt_proj_w = lin(ks[4], D_INNER, D_INNER)
        dt = jnp.exp(jax.random.uniform(ks[5], (D_INNER,), jnp.float32) * (math.log(DT_MAX) - math.log(DT_MIN)) + math.log(DT_MIN))
        dt_proj_b = dt + jnp.log(-jnp.expm1(-dt))
        A_log = jnp.log(jnp.tile(jnp.arange(1, D_STATE + 1, dtype=jnp.float32), (D_INNER, 1)))
        D = jnp.ones((D_INNER,), jnp.float32)
        out_proj_w = lin(ks[6], D_MODEL, D_INNER)
        return dict(x=x, in_proj_w=in_proj_w, conv_w=conv_w, conv_b=conv_b, x_proj_w=x_proj_w, dt_proj_w=dt_proj_w, dt_proj_b=dt_proj_b, A_log=A_log, D=D, out_proj_w=out_proj_w)
    _L3_attn_all = _L3_attn_setup()
    _L3_attn_in = {k: v for k, v in _L3_attn_all.items() if k in ('in_proj_w', 'conv_w', 'conv_b', 'x_proj_w', 'dt_proj_w', 'dt_proj_b', 'A_log', 'D', 'out_proj_w')}
    del _L3_attn_all

    def _L3_xattn_setup():
        import jax, jax.numpy as jnp
        import numpy as np
        from math import sqrt
        key = jax.random.key(seed)
        kq, kk, kv = jax.random.split(key, 3)
        B, S, D = (8, 1024, 256)
        q = jax.random.normal(kq, (B, S, D), dtype=jnp.float32)
        k = jax.random.normal(kk, (B, S, D), dtype=jnp.float32)
        v = jax.random.normal(kv, (B, S, D), dtype=jnp.float32)
        return {'q': q, 'k': k, 'v': v}
    _L3_xattn_all = _L3_xattn_setup()
    _L3_xattn_in = {k: v for k, v in _L3_xattn_all.items() if k in ()}
    del _L3_xattn_all

    def _L3_ffn_setup():
        import jax, jax.numpy as jnp
        import numpy as np
        import math
        D_IN = 256
        FEATURES = (1024, 1024, 256)
        BATCH, SEQ = (8, 512)

        def _conn_dense(kernel_bool, x):
            w = jnp.where(kernel_bool, jnp.float32(1.0), jnp.float32(-1.0))
            return x @ w
        key = jax.random.key(seed)
        kx, kk0, kk1, kk2 = jax.random.split(key, 4)
        x = jax.random.normal(kx, (BATCH, SEQ, D_IN), dtype=jnp.float32)
        k0 = jax.random.randint(kk0, (2 * D_IN, FEATURES[0]), 0, 2).astype(jnp.bool_)
        k1 = jax.random.randint(kk1, (FEATURES[0], FEATURES[1]), 0, 2).astype(jnp.bool_)
        k2 = jax.random.randint(kk2, (FEATURES[1], FEATURES[2]), 0, 2).astype(jnp.bool_)
        s0 = jnp.asarray(1.0 / math.sqrt(2 * D_IN), dtype=jnp.float32)
        s1 = jnp.asarray(1.0 / math.sqrt(FEATURES[0]), dtype=jnp.float32)
        s2 = jnp.asarray(1.0 / math.sqrt(FEATURES[1]), dtype=jnp.float32)
        return {'x': x, 'k0': k0, 'k1': k1, 'k2': k2, 's0': s0, 's1': s1, 's2': s2}
    _L3_ffn_all = _L3_ffn_setup()
    _L3_ffn_in = {k: v for k, v in _L3_ffn_all.items() if k in ('k0', 'k1', 'k2', 's0', 's1', 's2')}
    del _L3_ffn_all
    return {'x': x, 'ctx_1024': ctx_1024, 'L0_attn_qkv_w': _L0_attn_in['qkv_w'], 'L0_attn_qkv_b': _L0_attn_in['qkv_b'], 'L0_attn_out_w': _L0_attn_in['out_w'], 'L0_attn_out_b': _L0_attn_in['out_b'], 'L0_attn_proj': _L0_attn_in['proj'], 'L0_xattn_Wq': _L0_xattn_in['Wq'], 'L0_xattn_Wk': _L0_xattn_in['Wk'], 'L0_xattn_Wv': _L0_xattn_in['Wv'], 'L0_ffn_ln1_w': _L0_ffn_in['ln1_w'], 'L0_ffn_ln1_b': _L0_ffn_in['ln1_b'], 'L0_ffn_in_proj_w': _L0_ffn_in['in_proj_w'], 'L0_ffn_in_proj_b': _L0_ffn_in['in_proj_b'], 'L0_ffn_out_proj_w': _L0_ffn_in['out_proj_w'], 'L0_ffn_out_proj_b': _L0_ffn_in['out_proj_b'], 'L0_ffn_ln2_w': _L0_ffn_in['ln2_w'], 'L0_ffn_ln2_b': _L0_ffn_in['ln2_b'], 'L0_ffn_router_w': _L0_ffn_in['router_w'], 'L0_ffn_w1': _L0_ffn_in['w1'], 'L0_ffn_w2': _L0_ffn_in['w2'], 'L1_attn_norm_w': _L1_attn_in['norm_w'], 'L1_attn_Wq': _L1_attn_in['Wq'], 'L1_attn_Wk': _L1_attn_in['Wk'], 'L1_attn_Wv': _L1_attn_in['Wv'], 'L1_attn_Wo': _L1_attn_in['Wo'], 'L1_attn_gate': _L1_attn_in['gate'], 'L1_attn_log_temperature': _L1_attn_in['log_temperature'], 'L1_xattn_w': _L1_xattn_in['w'], 'L1_xattn_u': _L1_xattn_in['u'], 'L1_ffn_wr': _L1_ffn_in['wr'], 'L1_ffn_br': _L1_ffn_in['br'], 'L1_ffn_W1': _L1_ffn_in['W1'], 'L1_ffn_b1': _L1_ffn_in['b1'], 'L1_ffn_W2': _L1_ffn_in['W2'], 'L1_ffn_b2': _L1_ffn_in['b2'], 'L2_attn_qkv_w': _L2_attn_in['qkv_w'], 'L2_attn_c1': _L2_attn_in['c1'], 'L2_attn_c2': _L2_attn_in['c2'], 'L2_attn_conv1_w': _L2_attn_in['conv1_w'], 'L2_attn_gn_g': _L2_attn_in['gn_g'], 'L2_attn_gn_b': _L2_attn_in['gn_b'], 'L2_attn_conv2_w': _L2_attn_in['conv2_w'], 'L2_attn_conv2_b': _L2_attn_in['conv2_b'], 'L2_attn_ch_w1': _L2_attn_in['ch_w1'], 'L2_attn_ch_b1': _L2_attn_in['ch_b1'], 'L2_attn_ch_w2': _L2_attn_in['ch_w2'], 'L2_attn_ch_b2': _L2_attn_in['ch_b2'], 'L2_attn_proj_w': _L2_attn_in['proj_w'], 'L2_attn_proj_b': _L2_attn_in['proj_b'], 'L2_xattn_Wq': _L2_xattn_in['Wq'], 'L2_xattn_bq': _L2_xattn_in['bq'], 'L2_xattn_Wk': _L2_xattn_in['Wk'], 'L2_xattn_bk': _L2_xattn_in['bk'], 'L2_xattn_Wv': _L2_xattn_in['Wv'], 'L2_xattn_bv': _L2_xattn_in['bv'], 'L2_xattn_Wo': _L2_xattn_in['Wo'], 'L2_xattn_bo': _L2_xattn_in['bo'], 'L2_ffn_router_w': _L2_ffn_in['router_w'], 'L2_ffn_router_bias': _L2_ffn_in['router_bias'], 'L2_ffn_sw1': _L2_ffn_in['sw1'], 'L2_ffn_sw3': _L2_ffn_in['sw3'], 'L2_ffn_sw2': _L2_ffn_in['sw2'], 'L2_ffn_ew1': _L2_ffn_in['ew1'], 'L2_ffn_ew2': _L2_ffn_in['ew2'], 'L3_attn_in_proj_w': _L3_attn_in['in_proj_w'], 'L3_attn_conv_w': _L3_attn_in['conv_w'], 'L3_attn_conv_b': _L3_attn_in['conv_b'], 'L3_attn_x_proj_w': _L3_attn_in['x_proj_w'], 'L3_attn_dt_proj_w': _L3_attn_in['dt_proj_w'], 'L3_attn_dt_proj_b': _L3_attn_in['dt_proj_b'], 'L3_attn_A_log': _L3_attn_in['A_log'], 'L3_attn_D': _L3_attn_in['D'], 'L3_attn_out_proj_w': _L3_attn_in['out_proj_w'], 'L3_ffn_k0': _L3_ffn_in['k0'], 'L3_ffn_k1': _L3_ffn_in['k1'], 'L3_ffn_k2': _L3_ffn_in['k2'], 'L3_ffn_s0': _L3_ffn_in['s0'], 'L3_ffn_s1': _L3_ffn_in['s1'], 'L3_ffn_s2': _L3_ffn_in['s2']}

def reference(x, ctx_1024, L0_attn_qkv_w, L0_attn_qkv_b, L0_attn_out_w, L0_attn_out_b, L0_attn_proj, L0_xattn_Wq, L0_xattn_Wk, L0_xattn_Wv, L0_ffn_ln1_w, L0_ffn_ln1_b, L0_ffn_in_proj_w, L0_ffn_in_proj_b, L0_ffn_out_proj_w, L0_ffn_out_proj_b, L0_ffn_ln2_w, L0_ffn_ln2_b, L0_ffn_router_w, L0_ffn_w1, L0_ffn_w2, L1_attn_norm_w, L1_attn_Wq, L1_attn_Wk, L1_attn_Wv, L1_attn_Wo, L1_attn_gate, L1_attn_log_temperature, L1_xattn_w, L1_xattn_u, L1_ffn_wr, L1_ffn_br, L1_ffn_W1, L1_ffn_b1, L1_ffn_W2, L1_ffn_b2, L2_attn_qkv_w, L2_attn_c1, L2_attn_c2, L2_attn_conv1_w, L2_attn_gn_g, L2_attn_gn_b, L2_attn_conv2_w, L2_attn_conv2_b, L2_attn_ch_w1, L2_attn_ch_b1, L2_attn_ch_w2, L2_attn_ch_b2, L2_attn_proj_w, L2_attn_proj_b, L2_xattn_Wq, L2_xattn_bq, L2_xattn_Wk, L2_xattn_bk, L2_xattn_Wv, L2_xattn_bv, L2_xattn_Wo, L2_xattn_bo, L2_ffn_router_w, L2_ffn_router_bias, L2_ffn_sw1, L2_ffn_sw3, L2_ffn_sw2, L2_ffn_ew1, L2_ffn_ew2, L3_attn_in_proj_w, L3_attn_conv_w, L3_attn_conv_b, L3_attn_x_proj_w, L3_attn_dt_proj_w, L3_attn_dt_proj_b, L3_attn_A_log, L3_attn_D, L3_attn_out_proj_w, L3_ffn_k0, L3_ffn_k1, L3_ffn_k2, L3_ffn_s0, L3_ffn_s1, L3_ffn_s2):
    import jax
    import jax.numpy as jnp

    def _L0_attn_ref(x, qkv_w, qkv_b, out_w, out_b, proj):
        import jax, jax.numpy as jnp
        import numpy as np
        EMBED_DIM = 256
        NUM_HEADS = 16
        HEAD_DIM = EMBED_DIM // NUM_HEADS
        KERNEL_SIZE = 64
        B, L = (2, 512)
        Bn, Ln, E = x.shape
        H, D, M = proj.shape
        qkv = x @ qkv_w + qkv_b
        q, k, v = jnp.split(qkv, 3, axis=-1)
        q = q.reshape(Bn, Ln, H, D).transpose(0, 2, 1, 3)
        k = k.reshape(Bn, Ln, H, D).transpose(0, 2, 1, 3)
        v = v.reshape(Bn, Ln, H, D).transpose(0, 2, 1, 3)
        q_prime = jax.nn.relu(jnp.einsum('bhld,hdm->bhlm', q, proj))
        k_prime = jax.nn.relu(jnp.einsum('bhld,hdm->bhlm', k, proj))
        kv_prod = jnp.einsum('bhlm,bhld->bhlmd', k_prime, v)
        kv_cumsum = jnp.cumsum(kv_prod, axis=2)
        context = jnp.einsum('bhlm,bhlmd->bhld', q_prime, kv_cumsum)
        k_cumsum = jnp.cumsum(k_prime, axis=2)
        norm = jnp.einsum('bhlm,bhlm->bhl', q_prime, k_cumsum)
        out = context / (norm[..., None] + 1e-06)
        out = out.transpose(0, 2, 1, 3).reshape(Bn, Ln, E)
        return out @ out_w + out_b

    def _L0_xattn_ref(q, k, v, Wq, Wk, Wv):
        import jax, jax.numpy as jnp
        import numpy as np
        BETA = 256
        NUM_HEADS = 16
        NORM = (BETA // NUM_HEADS) ** (-0.5)
        qp = jax.nn.relu(jnp.einsum('bnd,od->bno', q, Wq))
        kp = jax.nn.relu(jnp.einsum('bnd,od->bno', k, Wk))
        vp = jax.nn.relu(jnp.einsum('bnd,od->bno', v, Wv))
        B, N, D = qp.shape
        dh = D // NUM_HEADS
        qh = qp.reshape(B, N, NUM_HEADS, dh)
        kh = kp.reshape(B, N, NUM_HEADS, dh)
        vh = vp.reshape(B, N, NUM_HEADS, vp.shape[-1] // NUM_HEADS)
        E = NORM * jnp.einsum('bqhd,bkhd->bhqk', qh, kh)
        A = jax.nn.softmax(E, axis=-1)
        out = jnp.einsum('bhqk,bkhd->bqhd', A, vh)
        return out.reshape(B, N, -1)

    def _L0_ffn_ref(x, ln1_w, ln1_b, in_proj_w, in_proj_b, out_proj_w, out_proj_b, ln2_w, ln2_b, router_w, w1, w2):
        import jax, jax.numpy as jnp
        import numpy as np
        S, B, H = (512, 1, 256)
        N_HEADS = 16
        HEAD_DIM = H // N_HEADS
        E, K, F = (8, 2, 512)
        EPS = 1e-05

        def layernorm(x, w, b):
            mu = jnp.mean(x, axis=-1, keepdims=True)
            var = jnp.mean(jnp.square(x - mu), axis=-1, keepdims=True)
            return (x - mu) * jax.lax.rsqrt(var + EPS) * w + b
        s, b, h = x.shape
        hn = layernorm(x, ln1_w, ln1_b)
        qkv = hn @ in_proj_w.T + in_proj_b
        q, k, v = jnp.split(qkv, 3, axis=-1)
        q = q.reshape(s, b, N_HEADS, HEAD_DIM)
        k = k.reshape(s, b, N_HEADS, HEAD_DIM)
        v = v.reshape(s, b, N_HEADS, HEAD_DIM)
        scores = jnp.einsum('sbnd,tbnd->bnst', q, k) / np.sqrt(HEAD_DIM)
        causal = jnp.tril(jnp.ones((s, s), bool))
        scores = jnp.where(causal[None, None], scores, -jnp.inf)
        probs = jax.nn.softmax(scores, axis=-1)
        attn = jnp.einsum('bnst,tbnd->sbnd', probs, v).reshape(s, b, h)
        attn = attn @ out_proj_w.T + out_proj_b
        x1 = x + attn
        hn2 = layernorm(x1, ln2_w, ln2_b).reshape(s * b, h)
        logits = hn2 @ router_w.T
        rp = jax.nn.softmax(logits, axis=-1)
        topw, topi = jax.lax.top_k(rp, K)
        gates = jnp.sum(jax.nn.one_hot(topi, E, dtype=hn2.dtype) * topw[..., None], axis=1)
        hmid = jax.nn.gelu(jnp.einsum('th,ehf->tef', hn2, w1), approximate=False)
        y = jnp.einsum('tef,efh->th', hmid * gates[:, :, None], w2)
        return x1 + y.reshape(s, b, h)

    def _L1_attn_ref(x, norm_w, Wq, Wk, Wv, Wo, gate, log_temperature):
        import jax, jax.numpy as jnp
        import numpy as np
        D_MODEL = 256
        N_HEADS = 4
        N_KV_HEADS = 2
        HEAD_DIM = D_MODEL // N_HEADS
        N_REP = N_HEADS // N_KV_HEADS
        EPS_RMS = 1e-06
        EPS_NORM = 1e-12

        def _rmsnorm(x, w):
            var = jnp.mean(jnp.square(x), axis=-1, keepdims=True)
            return x * jax.lax.rsqrt(var + EPS_RMS) * w

        def _l2norm(x):
            n = jnp.sqrt(jnp.sum(jnp.square(x), axis=-1, keepdims=True))
            return x / jnp.maximum(n, EPS_NORM)
        B, L, D = x.shape
        h = _rmsnorm(x, norm_w)
        q = (h @ Wq).reshape(B, L, N_HEADS, HEAD_DIM).transpose(0, 2, 1, 3)
        k = (h @ Wk).reshape(B, L, N_KV_HEADS, HEAD_DIM).transpose(0, 2, 1, 3)
        v = (h @ Wv).reshape(B, L, N_KV_HEADS, HEAD_DIM).transpose(0, 2, 1, 3)
        if N_REP > 1:
            k = jnp.repeat(k, N_REP, axis=1)
            v = jnp.repeat(v, N_REP, axis=1)
        q = _l2norm(q)
        k = _l2norm(k)
        scale = jnp.exp(log_temperature)
        attn = jnp.einsum('bhqd,bhkd->bhqk', q, k) * scale
        causal = jnp.tril(jnp.ones((L, L), dtype=bool))
        attn = jnp.where(causal, attn, -jnp.inf)
        attn = jax.nn.softmax(attn, axis=-1)
        out = jnp.einsum('bhqk,bhkd->bhqd', attn, v).transpose(0, 2, 1, 3).reshape(B, L, D)
        out = out @ Wo
        return x + gate * out

    def _L1_xattn_ref(r, k, v, w, u):
        import jax, jax.numpy as jnp
        import numpy as np
        B_SZ, T_LEN, C_DIM = (4, 1024, 256)

        def _wkv_scan(ek, v, ew):

            def step(carry, xt):
                A, Bd = carry
                ekt, vt = xt
                out = (A, Bd)
                A2 = ew * A + ekt * vt
                B2 = ew * Bd + ekt
                return ((A2, B2), out)
            init = (jnp.zeros_like(ek[:, 0]), jnp.zeros_like(ek[:, 0]))
            xs = (jnp.moveaxis(ek, 1, 0), jnp.moveaxis(v, 1, 0))
            _, (A, Bd) = jax.lax.scan(step, init, xs)
            return (jnp.moveaxis(A, 0, 1), jnp.moveaxis(Bd, 0, 1))

        def _birwkv(r, k, v, w, u):
            wc = w.reshape(-1)
            uc = u.reshape(-1)
            ew = jnp.exp(wc)
            ek = jnp.exp(k)
            Af, Bf = _wkv_scan(ek, v, ew)
            Ab, Bb = _wkv_scan(ek[:, ::-1], v[:, ::-1], ew)
            Ab = Ab[:, ::-1]
            Bb = Bb[:, ::-1]
            cur = jnp.exp(uc + k)
            wkv = (Af + Ab + cur * v) / (Bf + Bb + cur)
            return jax.nn.sigmoid(r) * wkv
        return _birwkv(r, k, v, w, u)

    def _L1_ffn_ref(x, wr, br, W1, b1, W2, b2):
        import jax, jax.numpy as jnp
        import numpy as np
        B, T, D, F, E = (4, 512, 256, 1024, 8)
        keys = jnp.einsum('btd,d->bt', x, wr) + br
        expert_idx = jnp.mod(jnp.floor(keys).astype(jnp.int32), W1.shape[0])
        out = jnp.zeros_like(x)
        for e in range(W1.shape[0]):
            h = jax.nn.relu(jnp.einsum('btd,df->btf', x, W1[e]) + b1[e])
            y = jnp.einsum('btf,fd->btd', h, W2[e]) + b2[e]
            out = jnp.where((expert_idx == e)[..., None], y, out)
        return out

    def _L2_attn_ref(x, qkv_w, c1, c2, conv1_w, gn_g, gn_b, conv2_w, conv2_b, ch_w1, ch_b1, ch_w2, ch_b2, proj_w, proj_b):
        import jax, jax.numpy as jnp
        import numpy as np
        from jax import lax
        B, N, C, RED = (8, 512, 256, 4)
        GN_EPS = 1e-05

        def _conv1d(x, w):
            return lax.conv_general_dilated(x, w, (1,), [(1, 1)], dimension_numbers=('NCH', 'OIH', 'NCH'))

        def _ode_func(A, conv1_w, gn_g, gn_b, conv2_w, conv2_b):
            h = _conv1d(A[:, None, :], conv1_w)
            b, _, n = h.shape
            hg = h.reshape(b, 2, 2, n)
            mu = hg.mean((2, 3), keepdims=True)
            var = hg.var((2, 3), keepdims=True)
            h = ((hg - mu) * lax.rsqrt(var + GN_EPS)).reshape(b, 4, n)
            h = jax.nn.relu(h * gn_g[None, :, None] + gn_b[None, :, None])
            y = _conv1d(h, conv2_w) + conv2_b[None, :, None]
            return y[:, 0, :]
        Bx, Nx, Cx = x.shape
        qkv = (x @ qkv_w).reshape(Bx, Nx, 3, Cx)
        q, k, v = (qkv[..., 0, :], qkv[..., 1, :], qkv[..., 2, :])
        mu_q = q.mean(-1, keepdims=True)
        mu_k = k.mean(-1, keepdims=True)
        dq, dk = (q - mu_q, k - mu_k)
        inv_cm1 = 1.0 / (Cx - 1)
        sigma_qk = (dq * dk).sum(-1, keepdims=True) * inv_cm1
        sigma_q2 = (dq * dq).sum(-1, keepdims=True) * inv_cm1
        sigma_k2 = (dk * dk).sum(-1, keepdims=True) * inv_cm1
        num = (2 * mu_q * mu_k + c1) * (2 * sigma_qk + c2)
        den = (mu_q ** 2 + mu_k ** 2 + c1) * (sigma_q2 + sigma_k2 + c2)
        attn_base = ((num / (den + 1e-07)) ** 2)[..., 0]
        steps = 2
        ts = jnp.linspace(0.0, 1.0, steps)
        dts = ts[1:] - ts[:-1]

        def step(A, dt):
            return (A + dt * _ode_func(A, conv1_w, gn_g, gn_b, conv2_w, conv2_b), None)
        A, _ = lax.scan(step, attn_base, dts)
        final_a = jax.nn.sigmoid(A)
        weights = jax.nn.softmax(final_a, axis=1)
        m = x.mean(axis=1, keepdims=True)
        ch_w = jax.nn.sigmoid(jax.nn.relu(m @ ch_w1 + ch_b1) @ ch_w2 + ch_b2)
        out_low = weights[..., None] * v * ch_w
        return out_low @ proj_w + proj_b

    def _L2_xattn_ref(query, key, value, Wq, bq, Wk, bk, Wv, bv, Wo, bo):
        import jax, jax.numpy as jnp
        import numpy as np
        EMBED_DIM = 256
        NUM_HEADS = 16
        HEAD_DIM = EMBED_DIM // NUM_HEADS

        def _split_heads(x):
            B, S, D = x.shape
            return x.reshape(B, S, NUM_HEADS, HEAD_DIM).transpose(0, 2, 1, 3)
        q = _split_heads(query @ Wq + bq)
        k = _split_heads(key @ Wk + bk)
        v = _split_heads(value @ Wv + bv)
        scores = jnp.einsum('bhqd,bhkd->bhqk', q, k) / np.sqrt(HEAD_DIM).astype(np.float32)
        attn = jax.nn.softmax(scores, axis=-1)
        ctx = jnp.einsum('bhqk,bhkd->bhqd', attn, v)
        B, H, S, hd = ctx.shape
        ctx = ctx.transpose(0, 2, 1, 3).reshape(B, S, H * hd)
        return ctx @ Wo + bo

    def _L2_ffn_ref(x, router_w, router_bias, sw1, sw3, sw2, ew1, ew2):
        import jax, jax.numpy as jnp
        import numpy as np
        D_MODEL = 256
        H_SHARED = 512
        H_ROUTED = 256
        N_EXPERTS = 8
        TOP_K = 2
        B, T, C = x.shape
        xf = x.reshape(-1, C)
        shared_out = jax.nn.silu(xf @ sw1) * (xf @ sw3) @ sw2
        s = jax.nn.sigmoid((xf @ router_w.T).astype(jnp.float32))
        sel_scores = s + router_bias.astype(jnp.float32)
        _, topk_idx = jax.lax.top_k(sel_scores, TOP_K)
        s_sel = jnp.take_along_axis(s, topk_idx, axis=1)
        denom = s_sel.sum(axis=1, keepdims=True)
        gates = jnp.where(denom > 1e-09, s_sel / (denom + 1e-09), 1.0 / TOP_K).astype(x.dtype)
        one_hot = jax.nn.one_hot(topk_idx, N_EXPERTS, dtype=x.dtype)
        comb = jnp.einsum('nke,nk->ne', one_hot, gates)
        h = jax.nn.gelu(jnp.einsum('nd,edh->neh', xf, ew1), approximate=False)
        y = jnp.einsum('neh,ehd->ned', h, ew2)
        routed_out = jnp.einsum('ned,ne->nd', y, comb)
        return (shared_out + routed_out).reshape(B, T, C)

    def _L3_attn_ref(x, in_proj_w, conv_w, conv_b, x_proj_w, dt_proj_w, dt_proj_b, A_log, D, out_proj_w):
        import math
        import jax, jax.numpy as jnp
        import numpy as np
        D_MODEL = 256
        D_STATE = 16
        D_CONV = 4
        EXPAND = 2
        D_INNER = D_MODEL * EXPAND
        B_SZ = 2
        L_SEQ = 512
        DT_MIN = 0.001
        DT_MAX = 0.1

        def _silu(v):
            return v * jax.nn.sigmoid(v)

        def _mamba(x, in_proj_w, conv_w, conv_b, x_proj_w, dt_proj_w, dt_proj_b, A_log, D, out_proj_w):
            xz = jnp.einsum('bld,ed->ble', x, in_proj_w)
            x_in, z = jnp.split(xz, 2, axis=-1)
            xc = jnp.swapaxes(x_in, 1, 2)
            xc = jax.lax.conv_general_dilated(xc, conv_w, window_strides=(1,), padding=[(D_CONV - 1, 0)], dimension_numbers=('NCH', 'OIH', 'NCH'), feature_group_count=D_INNER)
            xc = xc + conv_b[None, :, None]
            x_in = _silu(jnp.swapaxes(xc, 1, 2))
            dbc = jnp.einsum('bld,ed->ble', x_in, x_proj_w)
            delta_in = dbc[..., :D_INNER]
            Bp = dbc[..., D_INNER:D_INNER + D_STATE]
            Cp = dbc[..., D_INNER + D_STATE:]
            delta = jax.nn.softplus(jnp.einsum('bld,ed->ble', delta_in, dt_proj_w) + dt_proj_b)
            A = -jnp.exp(A_log)

            def step(h, inp):
                dt, bt, ct, xt = inp
                dA = jnp.exp(dt[:, :, None] * A[None])
                h = dA * h + dt[:, :, None] * bt[:, None, :] * xt[:, :, None]
                y = jnp.einsum('bds,bs->bd', h, ct) + D * xt
                return (h, y)
            tm = lambda a: jnp.swapaxes(a, 0, 1)
            h0 = jnp.zeros((x.shape[0], D_INNER, D_STATE), x.dtype)
            _, y = jax.lax.scan(step, h0, (tm(delta), tm(Bp), tm(Cp), tm(x_in)))
            y = jnp.swapaxes(y, 0, 1)
            return jnp.einsum('ble,de->bld', y * _silu(z), out_proj_w)
        return _mamba(x, in_proj_w, conv_w, conv_b, x_proj_w, dt_proj_w, dt_proj_b, A_log, D, out_proj_w)

    def _L3_xattn_ref(q, k, v):
        import jax, jax.numpy as jnp
        import numpy as np
        from math import sqrt
        S = q.shape[1]
        scale = 1.0 / sqrt(S)
        qn = q * scale
        kn = k * scale
        kv_mat = jnp.einsum('bsd,bse->bde', kn, v)
        out = jnp.einsum('bsd,bde->bse', qn, kv_mat)
        return out

    def _L3_ffn_ref(x, k0, k1, k2, s0, s1, s2):
        import jax, jax.numpy as jnp
        import numpy as np
        import math
        D_IN = 256
        FEATURES = (1024, 1024, 256)
        BATCH, SEQ = (8, 512)

        def _conn_dense(kernel_bool, x):
            w = jnp.where(kernel_bool, jnp.float32(1.0), jnp.float32(-1.0))
            return x @ w
        h = jnp.concatenate([x, -x], axis=-1)
        h = s0 * _conn_dense(k0, h)
        h = jax.nn.relu(h) * 2
        h = s1 * _conn_dense(k1, h)
        h = jax.nn.relu(h) * 2
        h = s2 * _conn_dense(k2, h)
        return h
    x = _layernorm(x + _L0_attn_ref(x, L0_attn_qkv_w, L0_attn_qkv_b, L0_attn_out_w, L0_attn_out_b, L0_attn_proj), axis=-1)
    x = _layernorm(x + _L0_xattn_ref(x, ctx_1024, ctx_1024, L0_xattn_Wq, L0_xattn_Wk, L0_xattn_Wv), axis=-1)
    x = _layernorm(x + _L0_ffn_ref(x, L0_ffn_ln1_w, L0_ffn_ln1_b, L0_ffn_in_proj_w, L0_ffn_in_proj_b, L0_ffn_out_proj_w, L0_ffn_out_proj_b, L0_ffn_ln2_w, L0_ffn_ln2_b, L0_ffn_router_w, L0_ffn_w1, L0_ffn_w2), axis=-1)
    x = _layernorm(x + _L1_attn_ref(x, L1_attn_norm_w, L1_attn_Wq, L1_attn_Wk, L1_attn_Wv, L1_attn_Wo, L1_attn_gate, L1_attn_log_temperature), axis=-1)
    x = _layernorm(x + _L1_xattn_ref(x, ctx_1024, ctx_1024, L1_xattn_w, L1_xattn_u), axis=-1)
    x = _layernorm(x + _L1_ffn_ref(x, L1_ffn_wr, L1_ffn_br, L1_ffn_W1, L1_ffn_b1, L1_ffn_W2, L1_ffn_b2), axis=-1)
    x = _layernorm(x + _L2_attn_ref(x, L2_attn_qkv_w, L2_attn_c1, L2_attn_c2, L2_attn_conv1_w, L2_attn_gn_g, L2_attn_gn_b, L2_attn_conv2_w, L2_attn_conv2_b, L2_attn_ch_w1, L2_attn_ch_b1, L2_attn_ch_w2, L2_attn_ch_b2, L2_attn_proj_w, L2_attn_proj_b), axis=-1)
    x = _layernorm(x + _L2_xattn_ref(x, ctx_1024, ctx_1024, L2_xattn_Wq, L2_xattn_bq, L2_xattn_Wk, L2_xattn_bk, L2_xattn_Wv, L2_xattn_bv, L2_xattn_Wo, L2_xattn_bo), axis=-1)
    x = _layernorm(x + _L2_ffn_ref(x, L2_ffn_router_w, L2_ffn_router_bias, L2_ffn_sw1, L2_ffn_sw3, L2_ffn_sw2, L2_ffn_ew1, L2_ffn_ew2), axis=-1)
    x = _layernorm(x + _L3_attn_ref(x, L3_attn_in_proj_w, L3_attn_conv_w, L3_attn_conv_b, L3_attn_x_proj_w, L3_attn_dt_proj_w, L3_attn_dt_proj_b, L3_attn_A_log, L3_attn_D, L3_attn_out_proj_w), axis=-1)
    x = _layernorm(x + _L3_xattn_ref(x, ctx_1024, ctx_1024), axis=-1)
    x = _layernorm(x + _L3_ffn_ref(x, L3_ffn_k0, L3_ffn_k1, L3_ffn_k2, L3_ffn_s0, L3_ffn_s1, L3_ffn_s2), axis=-1)
    return x

_drawn_inputs = setup_inputs


def setup_inputs(seed=0):
    import zlib

    import numpy as np

    out = dict(_drawn_inputs(seed))
    spreads = {'L0_attn_qkv_b': (0.0, 0.1),
     'L0_attn_out_b': (0.0, 0.1),
     'L0_ffn_ln1_w': (1.0, 0.2),
     'L0_ffn_ln1_b': (0.0, 0.315),
     'L0_ffn_in_proj_b': (0.0, 0.1),
     'L0_ffn_out_proj_b': (0.0, 0.1),
     'L0_ffn_ln2_w': (1.0, 0.2),
     'L0_ffn_ln2_b': (0.0, 0.336),
     'L1_attn_norm_w': (1.0, 0.6),
     'L1_ffn_b1': (0.0, 0.1),
     'L1_ffn_b2': (0.0, 0.1),
     'L2_attn_gn_g': (1.0, 0.6),
     'L2_attn_gn_b': (0.0, 0.8),
     'L2_attn_ch_b1': (0.0, 0.8),
     'L2_attn_ch_b2': (0.0, 0.8),
     'L2_attn_proj_b': (0.0, 0.1),
     'L2_xattn_bq': (0.0, 0.296),
     'L2_xattn_bk': (0.0, 0.8),
     'L2_xattn_bv': (0.0, 0.1),
     'L2_xattn_bo': (0.0, 0.1),
     'L2_ffn_router_bias': (0.0, 0.1),
     'L3_attn_conv_b': (0.0, 0.375),
     'L3_attn_D': (1.0, 0.2)}
    factors = {'L1_attn_Wq': 4.86,
     'L1_attn_Wk': 2.981,
     'L2_attn_qkv_w': 8.0,
     'L2_attn_conv1_w': 8.0,
     'L2_attn_conv2_w': 8.0,
     'L2_attn_ch_w1': 8.0,
     'L2_attn_ch_w2': 8.0,
     'L2_attn_proj_w': 8.0,
     'L3_attn_dt_proj_w': 3.99,
     'L3_attn_dt_proj_b': 2.873,
     'L3_attn_A_log': 2.801}
    for name, (base, spread) in spreads.items():
        noise = np.random.default_rng([zlib.crc32(name.encode()), seed]).standard_normal(out[name].shape)
        drawn = base * np.exp(spread * noise) if base else spread * noise
        out[name] = jnp.asarray(drawn.astype(out[name].dtype))
    for name, factor in factors.items():
        out[name] = (out[name] * factor).astype(out[name].dtype)
    return out
```

```python
from contextlib import ExitStack

import concourse.bass as bass
from concourse import mybir

F32 = mybir.dt.float32
BF16 = mybir.dt.bfloat16
I32 = mybir.dt.int32
U8 = mybir.dt.uint8
ALU = mybir.AluOpType
ACT = mybir.ActivationFunctionType
AX_X = mybir.AxisListType.X

P = 128
NB = 4
D = 256
FT = D // P
T = NB * P
NH, DH = 16, 16
SLOT = 32
SHIFT_ROW = 16
EPS = 1e-5
BIG = float(2.0 ** 100)
EXPERTS = 8
SEQUENCES = 16
PAIR_DONE = [2, 2, 4, 4]


class Chain:

    def __init__(self, eng, sem):
        self.eng, self.sem, self.n = eng, sem, 0

    def step(self, ins):
        self.n += 1
        ins.then_inc(self.sem, 1)

    def settle(self):
        self.eng.wait_ge(self.sem, self.n)

    def __call__(self, ins):
        self.step(ins)
        self.settle()


class Net:

    def __init__(self, nc, cx, params, cols, consts):
        self.nc, self.cx, self.params, self.cols = nc, cx, params, cols

        def sb(name, shape, dt=F32):
            return cx.enter_context(nc.sbuf_tensor(name, shape, dt))

        self.x = sb("x_tokens", [P, NB, D])
        self.xT = sb("x_features", [P, FT, T])
        self.ctx = sb("ctx_tokens", [P, NB, D])
        self.ctxT = sb("ctx_features", [P, FT, T])
        self.r = sb("residual_sum", [P, NB, D])
        self.stats = sb("ln_stats", [P, NB, 6])
        self.mv = sb("ln_mean_var", [P, NB, 2])
        self.var = sb("ln_var_eps", [P, NB])
        self.rvar = sb("ln_inverse_var", [P, NB])
        self.rstd = sb("ln_rstd", [P, NB])
        self.ident = sb("identity", [P, P])
        self.identb = sb("identity_bf16", [P, P], BF16)
        self.mates_qk = sb("mates_bias_qk", [P, 4, P], BF16)
        self.mates_kq = sb("mates_bias_kq", [P, 4, P], BF16)
        self.keep_kq = sb("causal_keep_kq", [P, P])
        self.causal_qk = sb("causal_bias_qk", [P, 4, P], BF16)
        self.causal_kq = sb("causal_bias_kq", [P, 4, P], BF16)
        self.inside = sb("inside_places", [P, NB * (P + 2)])
        self.before = sb("earlier_expert", [P, EXPERTS * EXPERTS])
        self.negmax = [sb(f"negmax_slots{i}", [P, NH, SLOT]) for i in range(2)]
        self.v1 = sb("values_and_one", [P, NB, NH, DH + 1])
        self.w_room = [sb(f"weights{i}", [P, max(cols["room"])]) for i in range(2)]
        self.e_room = sb("expert_weights", [P, cols["expert_room"]])
        self.banks = [cx.enter_context(nc.psum_tensor(f"bank{i}", [P, 512], F32)) for i in range(8)]
        self.pool = [cx.enter_context(nc.semaphore(f"signal{i}")) for i in range(40)]
        self.consts = consts

    def scratch(self, sub):
        return lambda name, shape, dt=F32: sub.enter_context(
            self.nc.sbuf_tensor(f"{self.stage}_{name}", shape, dt))

    def signals(self, n):
        assert n <= len(self.pool)
        return self.pool[:n]

    def end_sublayer(self):
        nums = [s.num for s in self.pool]
        self.nc.all_engine_barrier(sems_to_clear=range(min(nums), max(nums) + 1))

    def weights(self, sub):
        self.stage = sub
        at, out = 0, {}
        for name, n in self.cols[sub]:
            out[name] = self.w_room[SUBLAYERS.index(sub) % 2][:, at:at + n]
            at += n
        return out


def tiles(ap, k):
    return ap.rearrange("p (k n) -> p k n", k=k)


def seq(b):
    return slice(b * P, (b + 1) * P)



def transposes(pe, net, src, banks, done):
    for f in range(FT):
        for b in range(NB):
            mm = pe.transpose(net.banks[banks[f]][:, seq(b)], src[:, b, f * P:(f + 1) * P], net.ident[:])
        mm.then_inc(done, 1)


def project(pe, out, w, src, m, start=True, stop=True):
    k = w.shape[1]
    for f in range(k):
        mm = pe.matmul(out, w[:, f, m * P:(m + 1) * P], src[:, f, :], start=start and f == 0,
                       stop=stop and f == k - 1)
    return mm


def project_tokens(pe, out, srcT, b, w, start=True, stop=True):
    k = w.shape[1]
    for f in range(k):
        mm = pe.matmul(out, srcT[:, f, seq(b)], w[:, f, :], start=start and f == 0,
                       stop=stop and f == k - 1)
    return mm


def half(net, banks, b):
    return net.banks[banks[b // 2]][:, (b % 2) * D:(b % 2 + 1) * D]


def layer_norm_rstd_dve(dve, net, chain, r, var_ready):
    nc = net.nc
    for b in range(NB):
        chain.step(nc.vector.bn_stats(net.stats[:, b, :], r[:, b, :]))
    chain.settle()
    for b in range(NB):
        chain.step(nc.vector.bn_aggr(net.mv[:, b, :], net.stats[:, b, :]))
    chain.settle()
    chain(nc.vector.tensor_scalar(net.var[:], net.mv[:, :, 1], EPS, None, ALU.add))
    nc.vector.reciprocal(net.rvar[:], net.var[:]).then_inc(var_ready, 1)


def root_act(act, net, var_ready, rstd_ready, n=1):
    act.wait_ge(var_ready, n)
    net.nc.scalar.activation(net.rstd[:], net.rvar[:], ACT.Sqrt).then_inc(rstd_ready, 1)


def residual_norm_dve(dve, net, chain, base, y, y_ready, y_counts, var_ready, rstd_ready):
    nc = net.nc
    for b in range(NB):
        if y_counts[b]:
            dve.wait_ge(y_ready, y_counts[b])
        chain.step(nc.vector.tensor_tensor(net.r[:, b, :], base[:, b, :], y(b), ALU.add))
    chain.settle()
    layer_norm_rstd_dve(dve, net, chain, net.r, var_ready)
    dve.wait_ge(rstd_ready, 1)
    for b in range(NB):
        chain.step(nc.vector.tensor_scalar(net.x[:, b, :], net.r[:, b, :], net.mv[:, b, 0:1],
                                           net.rstd[:, b:b + 1], ALU.subtract, ALU.mult))
    chain.settle()



class Heads16:

    SCORES, SHIFTED, MAXT, CONTEXT = (0, 1), (2, 3), 4, (5, 6)

    def __init__(self, net, sub, signals, masked, scale):
        self.net, self.masked, self.scale = net, masked, scale
        (self.scores_ready, self.max_ready, self.negmax_ready, self.negmaxT_ready,
         self.shift_ready, self.shifted_ready, self.exp_ready, self.sums_ready,
         self.context_ready) = signals
        nc = net.nc

        sb = net.scratch(sub)

        self.qT = sb("q_slots", [P, 4, T])
        self.kT = sb("k_slots", [P, 4, T])
        self.probs = [sb(f"probs{i}", [P, 4, 4, P]) for i in range(2)]
        self.mx = [sb(f"score_max{i}", [P, 4, 4]) for i in range(2)]
        self.rec = [sb(f"inverse_sum{i}", [P, NH]) for i in range(2)]
        self.context = sb("context", [P, NB, D])

    def run_pe(self, pe):
        net = self.net

        def four_tiles(out_banks, lhs, rhs, b, u, mask, done):
            if self.masked:
                for s in range(2):
                    pe.matmul(net.banks[out_banks[s]][:], net.identb[:],
                              mask[:].rearrange("p a k -> p (a k)"), start=True, stop=True)
            for t in range(4):
                for s in range(2):
                    at = SLOT * (2 * u + s)
                    mm = pe.matmul(net.banks[out_banks[s]][:, seq(t)], lhs[at:at + SLOT, t, seq(b)],
                                   rhs[at:at + SLOT, t, seq(b)], start=not self.masked, stop=True,
                                   skip_group_check=True, tile_position=(at, 0))
                    if t == 3:
                        mm.then_inc(done, 1)

        def scores(b, u):
            n = 2 * b + u
            if n:
                pe.wait_ge(self.max_ready, 2 * n)
            four_tiles(self.SCORES, self.qT, self.kT, b, u, net.mates_qk, self.scores_ready)

        def negmax_transposes(b):
            pe.wait_ge(self.negmax_ready, b + 1)
            if b:
                pe.wait_ge(self.shift_ready, b)
            for t in range(4):
                mm = pe.transpose(net.banks[self.MAXT][:, seq(t)],
                                  net.negmax[b % 2][:, 4 * t:4 * t + 4, :].rearrange("p h s -> p (h s)"),
                                  net.ident[:])
            mm.then_inc(self.negmaxT_ready, 1)

        def shifted(b, u):
            n = 2 * b + u
            pe.wait_ge(self.shift_ready, b + 1)
            if n:
                pe.wait_ge(self.exp_ready, 2 * n)
            four_tiles(self.SHIFTED, self.kT, self.qT, b, u, net.mates_kq, self.shifted_ready)

        def context(b):
            pe.wait_ge(self.exp_ready, 4 * (b + 1))
            if b >= 2:
                pe.wait_ge(self.context_ready, b - 1)
            for h in range(NH):
                mm = pe.matmul(net.banks[self.CONTEXT[b % 2]][:, h * (DH + 1):(h + 1) * (DH + 1)],
                               self.probs[b % 2][:, h % 4, h // 4, :], net.v1[:, b, h, :], start=True, stop=True)
            mm.then_inc(self.sums_ready, 1)

        scores(0, 0)
        scores(0, 1)
        for b in range(NB):
            if b + 1 < NB:
                scores(b + 1, 0)
            negmax_transposes(b)
            shifted(b, 0)
            if b + 1 < NB:
                scores(b + 1, 1)
            shifted(b, 1)
            if b:
                context(b - 1)
        context(NB - 1)

    def run_act(self, act):
        for b in range(NB):
            for s in range(4):
                act.wait_ge(self.shifted_ready, 4 * b + s + 1)
                if b >= 2 and s == 0:
                    act.wait_ge(self.sums_ready, b - 1)
                self.net.nc.scalar.activation(
                    self.probs[b % 2][:, s, :, :].rearrange("p t q -> p (t q)"),
                    self.net.banks[self.SHIFTED[s % 2]][:], ACT.Exp,
                    scale=self.scale).then_inc(self.exp_ready, 1)

    def run_dve(self, dve, chain):
        net, nc = self.net, self.net.nc

        def maxima(b, u):
            if u == 0 and b >= 2:
                dve.wait_ge(self.negmax_ready, b - 1)
            for s in (2 * u, 2 * u + 1):
                dve.wait_ge(self.scores_ready, 4 * b + s + 1)
                nc.vector.reduce_max(self.mx[b % 2][:, :, s],
                                     net.banks[self.SCORES[s % 2]][:].rearrange("p (t k) -> p t k", t=4),
                                     AX_X).then_inc(self.max_ready, 1)

        def negate(b):
            dve.wait_ge(self.max_ready, 4 * (b + 1))
            if b >= 2:
                dve.wait_ge(self.negmaxT_ready, b - 1)
            nc.vector.tensor_scalar(net.negmax[b % 2][:, :, SHIFT_ROW],
                                    self.mx[b % 2][:].rearrange("p t s -> p (t s)"), -1.0, None,
                                    ALU.mult).then_inc(self.negmax_ready, 1)

        def shift(b):
            dve.wait_ge(self.negmaxT_ready, b + 1)
            dve.wait_ge(self.scores_ready, 4 * (b + 1))
            nc.vector.tensor_tensor(self.qT[:, :, seq(b)], self.qT[:, :, seq(b)],
                                    net.banks[self.MAXT][:].rearrange("p (t q) -> p t q", t=4),
                                    ALU.add).then_inc(self.shift_ready, 1)

        def normalise(b):
            dve.wait_ge(self.sums_ready, b + 1)
            got = net.banks[self.CONTEXT[b % 2]][:, 0:NH * (DH + 1)].rearrange("p (h d) -> p h d", h=NH)
            chain(nc.vector.reciprocal(self.rec[b % 2][:], got[:, :, DH]))
            nc.vector.tensor_tensor(self.context[:, b, :].rearrange("p (h d) -> p h d", h=NH),
                                    got[:, :, 0:DH],
                                    self.rec[b % 2][:].unsqueeze(2).broadcast_to([P, NH, DH]),
                                    ALU.mult).then_inc(self.context_ready, 1)

        maxima(0, 0)
        maxima(0, 1)
        negate(0)
        for b in range(NB):
            if b + 1 < NB:
                maxima(b + 1, 0)
            shift(b)
            if b + 1 < NB:
                maxima(b + 1, 1)
                negate(b + 1)
            if b:
                normalise(b - 1)
        normalise(NB - 1)



def l0_attn(net, prefetch):
    nc = net.nc
    w = net.weights("l0_attn")
    wqk, wv, wo = tiles(w["wqk"], FT), tiles(w["wv"], FT), tiles(w["wo"], FT)
    proj = tiles(w["proj"], 8)
    with ExitStack() as sub:
        sb = net.scratch(sub)

        qk = sb("qk", [P, 4, T])
        prime = net.e_room[:, 0:16 * T].rearrange("p (t m n) -> p t m n", t=2, m=8)
        scores = [sb(f"scores{i}", [P, 2, 8, P]) for i in range(2)]
        den = sb("denominator", [P, NH])
        context = sb("context", [P, NB, D])
        contextT = sb("contextT", [P, FT, T])
        xb = sb("x_plus_bias", [P, NB, D])
        (xT_in_psum, xT0_ready, xT1_ready, qk_in_psum, qk_ready, v_in_psum, v_ready, prime_in_psum,
         qprime_ready, kprime_ready, scores_in_psum, scores_ready, sums_ready, context_ready,
         cT_in_psum, cT0_ready, cT1_ready, y_ready, xb_ready, var_ready, rstd_ready,
         dve_steps) = net.signals(22)
        with nc.Block() as block:
            @block.sync
            def _(sp):
                prefetch(sp)

            @block.tensor
            def _(pe):
                pe.wait_ge(net.ready["l0_attn"], 16)
                transposes(pe, net, net.x, (0, 1), xT_in_psum)
                pe.wait_ge(xT0_ready, 1)
                pe.wait_ge(xT1_ready, 1)
                for m in range(4):
                    project(pe, net.banks[2 + m][:], wqk, net.xT, m).then_inc(qk_in_psum, 1)
                for b in range(NB):
                    project_tokens(pe, half(net, (6, 7), b), net.xT, b, wv).then_inc(v_in_psum, 1)
                pe.wait_ge(qk_ready, 4)
                for j in range(16):
                    pair, t = j // 2, j % 2
                    if j >= 4:
                        pe.wait_ge((qprime_ready, kprime_ready)[t], pair - 1)
                    pe.matmul(net.banks[2 + j % 4][:], proj[:, pair, :], qk[:, 2 * t + pair // 4, :],
                              start=True, stop=True).then_inc(prime_in_psum, 1)
                pe.wait_ge(qprime_ready, 8)
                pe.wait_ge(kprime_ready, 8)
                pe.wait_ge(v_ready, NB)

                def score(b):
                    for u in range(2):
                        n = 2 * b + u
                        if n >= 2:
                            pe.wait_ge(scores_ready, 2 * (n - 1))
                        for i in range(4):
                            for j in range(2):
                                rows = slice(64 * j, 64 * j + 64)
                                mm = pe.matmul(net.banks[2 * (n % 2) + j][:, seq(i)],
                                               prime[rows, 1, 4 * u + i, seq(b)],
                                               prime[rows, 0, 4 * u + i, seq(b)], start=True, stop=True,
                                               tile_position=(64 * j, 0))
                                if i == 3:
                                    mm.then_inc(scores_in_psum, 1)

                def context_of(b):
                    pe.wait_ge(scores_ready, 4 * (b + 1))
                    if b >= 2:
                        pe.wait_ge(context_ready, b - 1)
                    for h in range(NH):
                        mm = pe.matmul(net.banks[6 + b % 2][:, h * (DH + 1):(h + 1) * (DH + 1)],
                                       scores[b % 2][:, h % 2, h // 2, :], net.v1[:, b, h, :], start=True, stop=True)
                    mm.then_inc(sums_ready, 1)

                for b in range(NB):
                    score(b)
                    if b:
                        context_of(b - 1)
                context_of(NB - 1)
                pe.wait_ge(context_ready, NB)
                transposes(pe, net, context, (2, 3), cT_in_psum)
                pe.wait_ge(cT0_ready, 1)
                pe.wait_ge(cT1_ready, 1)
                for b in range(NB):
                    project_tokens(pe, half(net, (4, 5), b), contextT, b, wo).then_inc(y_ready, 1)

            @block.scalar
            def _(act):
                act.wait_ge(net.ready["l0_attn"], 16)
                act.wait_ge(xT_in_psum, 1)
                nc.scalar.copy(net.xT[:, 0, :], net.banks[0][:]).then_inc(xT0_ready, 1)
                for m in range(4):
                    act.wait_ge(qk_in_psum, m + 1)
                    nc.scalar.activation(qk[:, m, :], net.banks[2 + m][:], ACT.Identity,
                                         bias=w["bqk"][:, m:m + 1]).then_inc(qk_ready, 1)
                for pair in range(8):
                    act.wait_ge(prime_in_psum, 2 * pair + 1)
                    nc.scalar.activation(prime[:, 0, pair, :], net.banks[2 + (2 * pair) % 4][:],
                                         ACT.Relu).then_inc(qprime_ready, 1)
                act.wait_ge(cT_in_psum, 1)
                nc.scalar.copy(contextT[:, 0, :], net.banks[2][:]).then_inc(cT0_ready, 1)
                root_act(act, net, var_ready, rstd_ready)

            @block.vector
            def _(dve):
                chain = Chain(dve, dve_steps)
                dve.wait_ge(net.ready["l0_attn"], 16)
                dve.wait_ge(xT_in_psum, 2)
                nc.vector.tensor_copy(net.xT[:, 1, :], net.banks[1][:]).then_inc(xT1_ready, 1)
                for b in range(NB):
                    dve.wait_ge(v_in_psum, PAIR_DONE[b])
                    nc.vector.tensor_tensor(net.v1[:, b, :, 0:DH],
                                            half(net, (6, 7), b).rearrange("p (h d) -> p h d", h=NH),
                                            w["bv"].rearrange("p (h d) -> p h d", h=NH),
                                            ALU.add).then_inc(v_ready, 1)
                for pair in range(8):
                    dve.wait_ge(prime_in_psum, 2 * pair + 2)
                    nc.vector.tensor_scalar(prime[:, 1, pair, :], net.banks[2 + (2 * pair + 1) % 4][:], 0.0,
                                            None, ALU.max).then_inc(kprime_ready, 1)

                def mask(b):
                    if b >= 2:
                        dve.wait_ge(sums_ready, b - 1)
                    for n in (2 * b, 2 * b + 1):
                        for j in range(2):
                            dve.wait_ge(scores_in_psum, 2 * n + j + 1)
                            pairs = slice(4 * (n % 2), 4 * (n % 2) + 4)
                            nc.vector.tensor_tensor(scores[b % 2][:, j, pairs, :],
                                                    net.banks[2 * (n % 2) + j][:].rearrange(
                                                        "p (h q) -> p h q", h=4),
                                                    net.keep_kq[:].unsqueeze(1).broadcast_to([P, 4, P]),
                                                    ALU.mult).then_inc(scores_ready, 1)

                def divide(b):
                    dve.wait_ge(sums_ready, b + 1)
                    got = net.banks[6 + b % 2][:, 0:NH * (DH + 1)].rearrange("p (h d) -> p h d", h=NH)
                    chain(nc.vector.tensor_scalar(den[:], got[:, :, DH], 1e-6, None, ALU.add))
                    chain(nc.vector.reciprocal(den[:], den[:]))
                    nc.vector.tensor_tensor(context[:, b, :].rearrange("p (h d) -> p h d", h=NH),
                                            got[:, :, 0:DH], den[:].unsqueeze(2).broadcast_to([P, NH, DH]),
                                            ALU.mult).then_inc(context_ready, 1)
                    dve.wait_ge(context_ready, b + 1)

                for b in range(NB):
                    mask(b)
                    if b:
                        divide(b - 1)
                divide(NB - 1)
                dve.wait_ge(cT_in_psum, 2)
                nc.vector.tensor_copy(contextT[:, 1, :], net.banks[3][:]).then_inc(cT1_ready, 1)
                dve.wait_ge(xb_ready, 1)
                residual_norm_dve(dve, net, chain, xb, lambda b: half(net, (4, 5), b), y_ready,
                                  PAIR_DONE, var_ready, rstd_ready)

            @block.gpsimd
            def _(pool):
                pool.wait_ge(net.ready["l0_attn"], 16)
                nc.gpsimd.tensor_tensor(xb[:], net.x[:], w["bo"].unsqueeze(1).broadcast_to([P, NB, D]),
                                        ALU.add).then_inc(xb_ready, 1)
    net.end_sublayer()



def l0_xattn(net, prefetch):
    nc = net.nc
    w = net.weights("l0_xattn")
    wq, wk, wv = (tiles(w[n], FT) for n in ("wq", "wk", "wv"))
    with ExitStack() as sub:
        sig = net.signals(24)
        (xT_in_psum, xT0_ready, xT1_ready, qk_in_psum, q_ready, k_ready, v_in_psum, v_ready,
         var_ready, rstd_ready, dve_steps) = sig[9:20]
        heads = Heads16(net, sub, sig[:9], masked=False, scale=DH ** -0.5)
        with nc.Block() as block:
            @block.sync
            def _(sp):
                prefetch(sp)

            @block.tensor
            def _(pe):
                pe.wait_ge(net.ready["l0_xattn"], 16)
                transposes(pe, net, net.x, (0, 1), xT_in_psum)
                for m in range(4):
                    project(pe, net.banks[2 + m][:], wk, net.ctxT, m).then_inc(qk_in_psum, 1)
                for b in range(NB):
                    project_tokens(pe, half(net, (6, 7), b), net.ctxT, b, wv).then_inc(v_in_psum, 1)
                pe.wait_ge(xT0_ready, 1)
                pe.wait_ge(xT1_ready, 1)
                for m in range(4):
                    pe.wait_ge(k_ready, m + 1)
                    project(pe, net.banks[2 + m][:], wq, net.xT, m).then_inc(qk_in_psum, 1)
                pe.wait_ge(q_ready, 4)
                pe.wait_ge(v_ready, NB)
                heads.run_pe(pe)

            @block.scalar
            def _(act):
                act.wait_ge(net.ready["l0_xattn"], 16)
                act.wait_ge(xT_in_psum, 1)
                nc.scalar.copy(net.xT[:, 0, :], net.banks[0][:]).then_inc(xT0_ready, 1)
                for m in range(4):
                    act.wait_ge(qk_in_psum, m + 1)
                    nc.scalar.activation(heads.kT[:, m, :], net.banks[2 + m][:], ACT.Relu,
                                         bias=w["one_rows"][:, 0:1]).then_inc(k_ready, 1)
                for m in range(4):
                    act.wait_ge(qk_in_psum, m + 5)
                    nc.scalar.activation(heads.qT[:, m, :], net.banks[2 + m][:],
                                         ACT.Relu).then_inc(q_ready, 1)
                heads.run_act(act)
                root_act(act, net, var_ready, rstd_ready)

            @block.vector
            def _(dve):
                chain = Chain(dve, dve_steps)
                dve.wait_ge(xT_in_psum, 2)
                nc.vector.tensor_copy(net.xT[:, 1, :], net.banks[1][:]).then_inc(xT1_ready, 1)
                for b in range(NB):
                    dve.wait_ge(v_in_psum, PAIR_DONE[b])
                    nc.vector.tensor_scalar(net.v1[:, b, :, 0:DH],
                                            half(net, (6, 7), b).rearrange("p (h d) -> p h d", h=NH),
                                            0.0, None, ALU.max).then_inc(v_ready, 1)
                heads.run_dve(dve, chain)
                residual_norm_dve(dve, net, chain, net.x, lambda b: heads.context[:, b, :],
                                  heads.context_ready, [1, 2, 3, 4], var_ready, rstd_ready)
    net.end_sublayer()



class OutputProjection:

    Y = (2, 3)

    def __init__(self, net, sub, heads, wo, signals):
        self.net, self.heads, self.wo = net, heads, wo
        self.cT_in_psum, self.cT0_ready, self.cT1_ready, self.y_ready = signals
        self.contextT = net.scratch(sub)("contextT", [P, FT, T])

    def run_pe(self, pe):
        pe.wait_ge(self.heads.context_ready, NB)
        transposes(pe, self.net, self.heads.context, (0, 1), self.cT_in_psum)
        pe.wait_ge(self.cT0_ready, 1)
        pe.wait_ge(self.cT1_ready, 1)
        for b in range(NB):
            project_tokens(pe, half(self.net, self.Y, b), self.contextT, b, self.wo).then_inc(self.y_ready, 1)

    def run_act(self, act):
        act.wait_ge(self.cT_in_psum, 1)
        self.net.nc.scalar.copy(self.contextT[:, 0, :], self.net.banks[0][:]).then_inc(self.cT0_ready, 1)

    def run_dve(self, dve):
        dve.wait_ge(self.cT_in_psum, 2)
        self.net.nc.vector.tensor_copy(self.contextT[:, 1, :],
                                       self.net.banks[1][:]).then_inc(self.cT1_ready, 1)



def l0_ffn_attention(net, prefetch):
    nc = net.nc
    w = net.weights("l0_ffn_attention")
    wq, wk, wv, wo = (tiles(w[n], FT) for n in ("wq", "wk", "wv", "wo"))
    with ExitStack() as sub:
        sig = net.signals(39)
        (h_ready, hT_in_psum, hT0_ready, hT1_ready, qk_in_psum, q_ready, k_ready, v_in_psum, v_ready,
         xb_ready, x1_ready, base_ready, h2_ready, h2T_in_psum, h2T_ready, var_ready, rstd_ready,
         dve_steps) = sig[13:31]
        heads = Heads16(net, sub, sig[:9], masked=True, scale=DH ** -0.5)
        back = OutputProjection(net, sub, heads, wo, sig[9:13])
        normed = net.scratch(sub)("normed", [P, NB, D])
        xb = net.scratch(sub)("x_plus_bias", [P, NB, D])
        with nc.Block() as block:
            @block.sync
            def _(sp):
                prefetch(sp)

            @block.tensor
            def _(pe):
                pe.wait_ge(net.ready["l0_ffn_attention"], 16)
                pe.wait_ge(h_ready, 1)
                transposes(pe, net, normed, (0, 1), hT_in_psum)
                pe.wait_ge(hT0_ready, 1)
                pe.wait_ge(hT1_ready, 1)
                for m in range(4):
                    project(pe, net.banks[2 + m][:], wk, net.xT, m).then_inc(qk_in_psum, 1)
                for b in range(NB):
                    project_tokens(pe, half(net, (6, 7), b), net.xT, b, wv).then_inc(v_in_psum, 1)
                for m in range(4):
                    pe.wait_ge(k_ready, m + 1)
                    project(pe, net.banks[2 + m][:], wq, net.xT, m).then_inc(qk_in_psum, 1)
                pe.wait_ge(q_ready, 4)
                pe.wait_ge(v_ready, NB)
                heads.run_pe(pe)
                back.run_pe(pe)
                pe.wait_ge(h2_ready, 1)
                transposes(pe, net, normed, (0, 1), h2T_in_psum)

            @block.scalar
            def _(act):
                act.wait_ge(net.ready["l0_ffn_attention"], 16)
                root_act(act, net, var_ready, rstd_ready, 1)
                act.wait_ge(hT_in_psum, 1)
                nc.scalar.activation(net.xT[:, 0, :], net.banks[0][:], ACT.Identity,
                                     scale=w["ln1_w"][:, 0:1],
                                     bias=w["ln1_b"][:, 0:1]).then_inc(hT0_ready, 1)
                for m in range(4):
                    act.wait_ge(qk_in_psum, m + 1)
                    nc.scalar.activation(heads.kT[:, m, :], net.banks[2 + m][:], ACT.Identity,
                                         bias=w["bk"][:, m:m + 1]).then_inc(k_ready, 1)
                for m in range(4):
                    act.wait_ge(qk_in_psum, m + 5)
                    nc.scalar.activation(heads.qT[:, m, :], net.banks[2 + m][:], ACT.Identity,
                                         bias=w["bq"][:, m:m + 1]).then_inc(q_ready, 1)
                heads.run_act(act)
                back.run_act(act)
                root_act(act, net, var_ready, rstd_ready, 2)
                act.wait_ge(h2T_in_psum, 1)
                nc.scalar.activation(net.xT[:, 0, :], net.banks[0][:], ACT.Identity,
                                     scale=w["ln2_w"][:, 0:1],
                                     bias=w["ln2_b"][:, 0:1]).then_inc(h2T_ready, 1)

            @block.vector
            def _(dve):
                chain = Chain(dve, dve_steps)

                def norm(src, n, done):
                    layer_norm_rstd_dve(dve, net, chain, src, var_ready)
                    dve.wait_ge(rstd_ready, n)
                    for b in range(NB):
                        chain.step(nc.vector.tensor_scalar(normed[:, b, :], src[:, b, :],
                                                           net.mv[:, b, 0:1], net.rstd[:, b:b + 1],
                                                           ALU.subtract, ALU.mult))
                    chain.settle()
                    nc.vector.engine_nop().then_inc(done, 1)

                dve.wait_ge(net.ready["l0_ffn_attention"], 16)
                norm(net.x, 1, h_ready)
                dve.wait_ge(hT_in_psum, 2)
                nc.vector.tensor_scalar(net.xT[:, 1, :], net.banks[1][:], w["ln1_w"][:, 1:2],
                                        w["ln1_b"][:, 1:2], ALU.mult, ALU.add).then_inc(hT1_ready, 1)
                for b in range(NB):
                    dve.wait_ge(v_in_psum, PAIR_DONE[b])
                    nc.vector.tensor_tensor(net.v1[:, b, :, 0:DH],
                                            half(net, (6, 7), b).rearrange("p (h d) -> p h d", h=NH),
                                            w["bv"].rearrange("p (h d) -> p h d", h=NH),
                                            ALU.add).then_inc(v_ready, 1)
                heads.run_dve(dve, chain)
                back.run_dve(dve)
                dve.wait_ge(xb_ready, 1)
                for b in range(NB):
                    dve.wait_ge(back.y_ready, PAIR_DONE[b])
                    nc.vector.tensor_tensor(net.r[:, b, :], xb[:, b, :], half(net, back.Y, b),
                                            ALU.add).then_inc(x1_ready, 1)
                dve.wait_ge(x1_ready, NB)
                norm(net.r, 2, h2_ready)
                dve.wait_ge(h2T_in_psum, 2)
                nc.vector.tensor_scalar(net.xT[:, 1, :], net.banks[1][:], w["ln2_w"][:, 1:2],
                                        w["ln2_b"][:, 1:2], ALU.mult, ALU.add).then_inc(h2T_ready, 1)

            @block.gpsimd
            def _(pool):
                pool.wait_ge(net.ready["l0_ffn_attention"], 16)
                nc.gpsimd.tensor_tensor(xb[:], net.x[:], w["bo"].unsqueeze(1).broadcast_to([P, NB, D]),
                                        ALU.add).then_inc(xb_ready, 1)
                pool.wait_ge(x1_ready, NB)
                nc.gpsimd.tensor_tensor(net.x[:], net.x[:], net.r[:], ALU.add).then_inc(base_ready, 1)
                pool.wait_ge(base_ready, 1)
    net.end_sublayer()



class Experts:

    HIDDEN, OUT = (1, 2, 3), ((4, 5), (6, 7))

    def __init__(self, net, sub, name, signals, n_hidden, func, bias=None, slots=EXPERTS):
        self.net, self.n, self.func, self.bias, self.slots = net, n_hidden, func, bias, slots
        (self.hidden_in_psum, self.hidden_ready, self.out_in_psum, self.out_taken) = signals
        self.hidden = [net.scratch(sub)(f"hidden{i}", [P, n_hidden, T])
                       for i in range(2)]
        loop = next(part for part in LOOPS if name in part)
        self.loads = 16 * (1 + [s for s in loop if s in RUN and s in EXPERT_NETS].index(name))

    def w1(self, e):
        at = (e % self.slots) * self.n * 2 * D
        return tiles(self.net.e_room[:, at:at + self.n * D], FT)

    def w2(self, e):
        at = (e % self.slots) * self.n * 2 * D + self.n * D
        return tiles(self.net.e_room[:, at:at + self.n * D], self.n)

    def run_pe(self, pe, before_out=None):
        net = self.net

        def hidden(e):
            pe.wait_ge(net.expert_ready[e], self.loads)
            for m in range(self.n):
                n = e * self.n + m
                if n >= 3:
                    pe.wait_ge(self.hidden_ready, n - 2)
                project(pe, net.banks[self.HIDDEN[n % 3]][:], self.w1(e), net.xT,
                        m).then_inc(self.hidden_in_psum, 1)

        def out(e):
            pe.wait_ge(self.hidden_ready, self.n * (e + 1))
            if e >= 2:
                pe.wait_ge(self.out_taken, NB * (e - 1))
            for b in range(NB):
                project_tokens(pe, half(net, self.OUT[e % 2], b), self.hidden[e % 2], b,
                               self.w2(e)).then_inc(self.out_in_psum, 1)

        hidden(0)
        for e in range(EXPERTS):
            if e + 1 < EXPERTS:
                hidden(e + 1)
            if e == 0 and before_out:
                before_out()
            out(e)

    def run_act(self, act):
        for e in range(EXPERTS):
            if e >= 2:
                act.wait_ge(self.out_in_psum, NB * (e - 1))
            for m in range(self.n):
                n = e * self.n + m
                act.wait_ge(self.hidden_in_psum, n + 1)
                kw = {"bias": self.bias[:, n:n + 1]} if self.bias is not None else {}
                self.net.nc.scalar.activation(self.hidden[e % 2][:, m, :],
                                              self.net.banks[self.HIDDEN[n % 3]][:], self.func,
                                              **kw).then_inc(self.hidden_ready, 1)

    def run_dve(self, dve, gates, base):
        net = self.net
        for e in range(EXPERTS):
            for b in range(NB):
                dve.wait_ge(self.out_in_psum, NB * e + PAIR_DONE[b])
                if e:
                    dve.wait_ge(self.out_taken, NB * (e - 1) + b + 1)
                net.nc.vector.scalar_tensor_tensor(
                    out=net.r[:, b, :], in0=half(net, self.OUT[e % 2], b), scalar=gates[:, b, e:e + 1],
                    in1=base[:, b, :] if e == 0 else net.r[:, b, :], op0=ALU.mult,
                    op1=ALU.add).then_inc(self.out_taken, 1)


def finish_norm_dve(dve, net, chain, var_ready, rstd_ready):
    layer_norm_rstd_dve(dve, net, chain, net.r, var_ready)
    dve.wait_ge(rstd_ready, 1)
    for b in range(NB):
        chain.step(net.nc.vector.tensor_scalar(net.x[:, b, :], net.r[:, b, :], net.mv[:, b, 0:1],
                                               net.rstd[:, b:b + 1], ALU.subtract, ALU.mult))
    chain.settle()


def top2_dve(net, chain, key, chosen, greater, equal, rank):
    nc = net.nc
    shape = [P, NB, EXPERTS, EXPERTS]
    other = key[:].unsqueeze(2).broadcast_to(shape)
    own = key[:].unsqueeze(3).broadcast_to(shape)
    chain.step(nc.vector.tensor_tensor(greater[:], other, own, ALU.is_gt))
    chain(nc.vector.tensor_tensor(equal[:], other, own, ALU.is_equal))
    chain(nc.vector.tensor_tensor(equal[:].rearrange("p b e o -> p b (e o)"),
                                  equal[:].rearrange("p b e o -> p b (e o)"),
                                  net.before[:].unsqueeze(1).broadcast_to([P, NB, EXPERTS * EXPERTS]),
                                  ALU.mult))
    chain(nc.vector.tensor_tensor(greater[:], greater[:], equal[:], ALU.add))
    chain(nc.vector.reduce_sum(rank[:], greater[:], AX_X))
    chain(nc.vector.tensor_scalar(chosen[:], rank[:], 2.0, None, ALU.is_lt))


def load_experts(sub):
    def load(net, sp):
        per = EXPERT_COLS[sub]
        for e in range(min(EXPERTS, EXPERT_ROOM // per)):
            sp.dma_start(net.e_room[:, e * per:(e + 1) * per],
                         net.params[sub + "_experts"][:, e * per:(e + 1) * per]).then_inc(
                             net.expert_ready[e], 16)
    return load



def l0_ffn_experts(net, prefetch):
    nc = net.nc
    w = net.weights("l0_ffn_experts")
    router = tiles(w["router"], FT)
    with ExitStack() as sub:
        sb = net.scratch(sub)

        (logits_in_psum, shifted_ready, exp_ready, var_ready, rstd_ready,
         dve_steps) = net.signals(10)[4:]
        experts = Experts(net, sub, "l0_ffn_experts", net.signals(4), 4, ACT.Gelu)
        mx, total = sb("logit_max", [P, NB]), sb("exp_sum", [P, NB])
        prob, gates, chosen, rank = (sb(n, [P, NB, EXPERTS]) for n in ("prob", "gates", "chosen", "rank"))
        greater, equal = (sb(n, [P, NB, EXPERTS, EXPERTS]) for n in ("greater", "equal"))
        logits = net.banks[0][:, 0:NB * EXPERTS].rearrange("p (b e) -> p b e", b=NB)
        with nc.Block() as block:
            @block.sync
            def _(sp):
                prefetch(sp)

            @block.tensor
            def _(pe):
                pe.wait_ge(net.ready["l0_ffn_experts"], 16)
                for b in range(NB):
                    mm = project_tokens(pe, logits[:, b, :], net.xT, b, router)
                mm.then_inc(logits_in_psum, 1)
                experts.run_pe(pe)

            @block.scalar
            def _(act):
                act.wait_ge(shifted_ready, 1)
                nc.scalar.activation(prob[:], prob[:], ACT.Exp).then_inc(exp_ready, 1)
                experts.run_act(act)
                root_act(act, net, var_ready, rstd_ready)

            @block.vector
            def _(dve):
                chain = Chain(dve, dve_steps)
                wide = [P, NB, EXPERTS]
                dve.wait_ge(logits_in_psum, 1)
                chain(nc.vector.reduce_max(mx[:], logits, AX_X))
                nc.vector.tensor_tensor(prob[:], logits, mx[:].unsqueeze(2).broadcast_to(wide),
                                        ALU.subtract).then_inc(shifted_ready, 1)
                dve.wait_ge(exp_ready, 1)
                chain(nc.vector.reduce_sum(total[:], prob[:], AX_X))
                chain(nc.vector.reciprocal(total[:], total[:]))
                chain(nc.vector.tensor_tensor(prob[:], prob[:], total[:].unsqueeze(2).broadcast_to(wide),
                                              ALU.mult))
                top2_dve(net, chain, prob, chosen, greater, equal, rank)
                chain(nc.vector.tensor_tensor(gates[:], prob[:], chosen[:], ALU.mult))
                experts.run_dve(dve, gates, net.x)
                dve.wait_ge(experts.out_taken, NB * EXPERTS)
                finish_norm_dve(dve, net, chain, var_ready, rstd_ready)
    net.end_sublayer()



Q_HEADS, KV_HEADS, HD = 4, 2, 64


def l1_attn(net, prefetch):
    nc = net.nc
    w = net.weights("l1_attn")
    wq, wkv, wo = (tiles(w[n], FT) for n in ("wq", "wkv", "wo"))
    with ExitStack() as sub:
        sb = net.scratch(sub)
        normed = sb("normed", [P, NB, D])
        doubled = sb("x_twice", [P, NB, D])
        msq, unit, temp = sb("mean_square", [P, NB]), sb("inverse_length", [P, NB, 6]), sb("temperature", [P, 1])
        squares = sb("squares", [P, NB, 6, HD])
        qk = sb("unit_qk", [P, NB, 6, HD])
        v = sb("values", [P, NB, KV_HEADS, HD + 1])
        qkT = sb("unit_qkT", [P, 3, T])
        mx = sb("score_max", [P, NB, 2, 2])
        negT = sb("negmaxT", [P, P])
        probs = sb("probs", [P, 2, NB, 2, P])
        rec = sb("inverse_sum", [P, NB, Q_HEADS])
        context = sb("context", [P, NB, D])
        contextT = sb("contextT", [P, FT, T])
        (var_ready, rstd_ready, h_ready, hT_in_psum, hT0_ready, hT1_ready, qkv_in_psum, squares_ready,
         v_ready, ones_ready, length_ready, root_ready, unit_ready, unitT_in_psum, unitT_ready,
         unitT_ready_dve, scores_ready, max_ready, neg_ready, negT_in_psum, negT_ready, shifted_ready,
         exp_ready, sums_ready, context_ready, cT_in_psum, cT0_ready, cT1_ready, y_ready, temp_ready,
         doubled_ready, out_var_ready, out_rstd_ready, dve_steps) = net.signals(34)
        HT, QKV, UNIT_T, SCORES, NEG_T = (0, 1), (2, 3, 4, 5), (6, 7, 0), ((2, 3), (4, 5)), 1
        SHIFTED, SUMS, CT, Y = ((6, 7), (2, 3)), (4, 5, 0, 1), (6, 7), (2, 3)
        with nc.Block() as block:
            @block.sync
            def _(sp):
                prefetch(sp)

            @block.tensor
            def _(pe):
                pe.wait_ge(net.ready["l1_attn"], 16)
                pe.wait_ge(h_ready, 1)
                transposes(pe, net, normed, HT, hT_in_psum)
                pe.wait_ge(hT0_ready, 1)
                pe.wait_ge(hT1_ready, 1)
                for b in range(NB):
                    bank = net.banks[QKV[b]]
                    project_tokens(pe, bank[:, 0:D], net.xT, b, wq)
                    project_tokens(pe, bank[:, D:2 * D], net.xT, b, wkv).then_inc(qkv_in_psum, 1)
                for k, bank in enumerate(UNIT_T):
                    pe.wait_ge(unit_ready, NB)
                    for b in range(NB):
                        mm = pe.transpose(net.banks[bank][:, seq(b)],
                                          qk[:, b, 2 * k:2 * k + 2, :].rearrange("p h d -> p (h d)"),
                                          net.ident[:])
                    mm.then_inc(unitT_in_psum, 1)
                pe.wait_ge(unitT_ready, 2)
                pe.wait_ge(unitT_ready_dve, 1)
                pe.wait_ge(v_ready, NB)

                def four(out_banks, u, lhs_tile, rhs_tile, mask, done, shift):
                    for j in range(2):
                        pe.matmul(net.banks[out_banks[j]][:], net.identb[:],
                                  mask[:].rearrange("p a k -> p (a k)"), start=True, stop=True)
                    for a in range(4):
                        b, i = 2 * u + a // 2, a % 2
                        if shift:
                            for j in range(2):
                                r = 4 * b + 2 * i + j
                                pe.matmul(net.banks[out_banks[j]][:, seq(a)],
                                          net.ident[0:16, r:r + 1].broadcast_to([16, P]), negT[0:16, :],
                                          start=False, stop=True, skip_group_check=True)
                    for a in range(4):
                        b, i = 2 * u + a // 2, a % 2
                        for j in range(2):
                            rows = slice(HD * j, HD * (j + 1))
                            lt, rt = (i if x == "q" else 2 for x in (lhs_tile, rhs_tile))
                            mm = pe.matmul(net.banks[out_banks[j]][:, seq(a)], qkT[rows, lt, seq(b)],
                                           qkT[rows, rt, seq(b)], start=False, stop=True,
                                           skip_group_check=True, tile_position=(HD * j, 0))
                            if a == 3:
                                mm.then_inc(done, 1)

                for u in range(2):
                    four(SCORES[u], u, "q", "k", net.causal_qk, scores_ready, False)
                pe.wait_ge(neg_ready, 1)
                pe.transpose(net.banks[NEG_T][0:16, 0:P], mx[:].rearrange("p b i j -> p (b i j)"),
                             net.ident[:]).then_inc(negT_in_psum, 1)
                pe.wait_ge(negT_ready, 1)
                for u in range(2):
                    four(SHIFTED[u], u, "k", "q", net.causal_kq, shifted_ready, True)
                pe.wait_ge(ones_ready, 1)
                for b in range(NB):
                    if b % 2 == 0:
                        pe.wait_ge(exp_ready, 2 * (b // 2 + 1))
                    for h in range(Q_HEADS):
                        mm = pe.matmul(net.banks[SUMS[b]][:, h * (HD + 1):(h + 1) * (HD + 1)],
                                       probs[:, h // 2, b, h % 2, :], v[:, b, h // 2, :], start=True, stop=True)
                    mm.then_inc(sums_ready, 1)
                pe.wait_ge(context_ready, NB)
                transposes(pe, net, context, CT, cT_in_psum)
                pe.wait_ge(cT0_ready, 1)
                pe.wait_ge(cT1_ready, 1)
                for b in range(NB):
                    project_tokens(pe, half(net, Y, b), contextT, b, wo).then_inc(y_ready, 1)

            @block.scalar
            def _(act):
                act.wait_ge(net.ready["l1_attn"], 16)
                nc.scalar.activation(temp[:], w["log_temperature"], ACT.Exp).then_inc(temp_ready, 1)
                root_act(act, net, var_ready, rstd_ready)
                act.wait_ge(hT_in_psum, 1)
                nc.scalar.activation(net.xT[:, 0, :], net.banks[HT[0]][:], ACT.Copy,
                                     scale=w["norm_w"][:, 0:1]).then_inc(hT0_ready, 1)
                for b in range(NB):
                    act.wait_ge(qkv_in_psum, b + 1)
                    nc.scalar.activation(squares[:, b, :, :].rearrange("p h d -> p (h d)"),
                                         net.banks[QKV[b]][:, 0:6 * HD], ACT.Square).then_inc(squares_ready, 1)
                act.wait_ge(length_ready, 1)
                nc.scalar.activation(unit[:], unit[:], ACT.Sqrt).then_inc(root_ready, 1)
                for k in range(2):
                    act.wait_ge(unitT_in_psum, k + 1)
                    nc.scalar.copy(qkT[:, k, :], net.banks[UNIT_T[k]][:]).then_inc(unitT_ready, 1)
                act.wait_ge(temp_ready, 1)
                for u in range(2):
                    for j in range(2):
                        act.wait_ge(shifted_ready, 2 * u + j + 1)
                        nc.scalar.activation(
                            probs[:, j, 2 * u:2 * u + 2, :, :].rearrange("p b i q -> p (b i q)"),
                            net.banks[SHIFTED[u][j]][:], ACT.Exp, scale=temp[:, 0:1]).then_inc(exp_ready, 1)
                act.wait_ge(cT_in_psum, 1)
                nc.scalar.copy(contextT[:, 0, :], net.banks[CT[0]][:]).then_inc(cT0_ready, 1)
                root_act(act, net, out_var_ready, out_rstd_ready)

            @block.vector
            def _(dve):
                chain = Chain(dve, dve_steps)
                dve.wait_ge(net.ready["l1_attn"], 16)
                for b in range(NB):
                    chain.step(nc.vector.bn_stats(net.stats[:, b, :], net.x[:, b, :]))
                chain.settle()
                for b in range(NB):
                    chain.step(nc.vector.bn_aggr(net.mv[:, b, :], net.stats[:, b, :]))
                chain.settle()
                chain(nc.vector.tensor_tensor(msq[:], net.mv[:, :, 0], net.mv[:, :, 0], ALU.mult))
                chain(nc.vector.tensor_tensor(msq[:], msq[:], net.mv[:, :, 1], ALU.add))
                chain(nc.vector.tensor_scalar(net.var[:], msq[:], 1e-6, None, ALU.add))
                nc.vector.reciprocal(net.rvar[:], net.var[:]).then_inc(var_ready, 1)
                dve.wait_ge(rstd_ready, 1)
                for b in range(NB):
                    chain.step(nc.vector.tensor_scalar(normed[:, b, :], net.x[:, b, :],
                                                       net.rstd[:, b:b + 1], None, ALU.mult))
                chain.settle()
                nc.vector.engine_nop().then_inc(h_ready, 1)
                dve.wait_ge(hT_in_psum, 2)
                nc.vector.tensor_scalar(net.xT[:, 1, :], net.banks[HT[1]][:], w["norm_w"][:, 1:2], None,
                                        ALU.mult).then_inc(hT1_ready, 1)
                for b in range(NB):
                    dve.wait_ge(squares_ready, b + 1)
                    chain.step(nc.vector.reduce_sum(unit[:, b, :], squares[:, b, :, :], AX_X))
                chain.settle()
                chain(nc.vector.tensor_scalar(unit[:], unit[:], 1e-24, None, ALU.max))
                nc.vector.reciprocal(unit[:], unit[:]).then_inc(length_ready, 1)
                dve.wait_ge(root_ready, 1)
                for b in range(NB):
                    nc.vector.tensor_tensor(qk[:, b, :, :],
                                            net.banks[QKV[b]][:, 0:6 * HD].rearrange("p (h d) -> p h d", h=6),
                                            unit[:, b, :].unsqueeze(2).broadcast_to([P, 6, HD]),
                                            ALU.mult).then_inc(unit_ready, 1)
                dve.wait_ge(ones_ready, 1)
                for b in range(NB):
                    nc.vector.tensor_copy(v[:, b, :, 0:HD],
                                          net.banks[QKV[b]][:, 6 * HD:].rearrange("p (h d) -> p h d", h=2)
                                          ).then_inc(v_ready, 1)
                dve.wait_ge(unitT_in_psum, 3)
                nc.vector.tensor_copy(qkT[:, 2, :], net.banks[UNIT_T[2]][:]).then_inc(unitT_ready_dve, 1)
                for u in range(2):
                    for j in range(2):
                        dve.wait_ge(scores_ready, 2 * u + j + 1)
                        nc.vector.reduce_max(mx[:, 2 * u:2 * u + 2, :, j],
                                             net.banks[SCORES[u][j]][:].rearrange(
                                                 "p (b i k) -> p b i k", b=2, i=2),
                                             AX_X).then_inc(max_ready, 1)
                dve.wait_ge(max_ready, 4)
                nc.vector.tensor_scalar(mx[:], mx[:], -1.0, None, ALU.mult).then_inc(neg_ready, 1)
                dve.wait_ge(negT_in_psum, 1)
                nc.vector.tensor_copy(negT[0:16, :], net.banks[NEG_T][0:16, 0:P]).then_inc(negT_ready, 1)
                for b in range(NB):
                    dve.wait_ge(sums_ready, b + 1)
                    got = net.banks[SUMS[b]][:, 0:Q_HEADS * (HD + 1)].rearrange("p (h d) -> p h d", h=Q_HEADS)
                    chain(nc.vector.reciprocal(rec[:, b, :], got[:, :, HD]))
                    nc.vector.tensor_tensor(context[:, b, :].rearrange("p (h d) -> p h d", h=Q_HEADS),
                                            got[:, :, 0:HD],
                                            rec[:, b, :].unsqueeze(2).broadcast_to([P, Q_HEADS, HD]),
                                            ALU.mult).then_inc(context_ready, 1)
                dve.wait_ge(cT_in_psum, 2)
                nc.vector.tensor_copy(contextT[:, 1, :], net.banks[CT[1]][:]).then_inc(cT1_ready, 1)
                dve.wait_ge(doubled_ready, 1)
                for b in range(NB):
                    dve.wait_ge(y_ready, PAIR_DONE[b])
                    chain.step(nc.vector.scalar_tensor_tensor(
                        out=net.r[:, b, :], in0=half(net, Y, b), scalar=w["gate"], in1=doubled[:, b, :],
                        op0=ALU.mult, op1=ALU.add))
                chain.settle()
                finish_norm_dve(dve, net, chain, out_var_ready, out_rstd_ready)

            @block.gpsimd
            def _(pool):
                nc.gpsimd.memset(v[:], 1.0).then_inc(ones_ready, 1)
                nc.gpsimd.tensor_tensor(doubled[:], net.x[:], net.x[:], ALU.add).then_inc(doubled_ready, 1)
    net.end_sublayer()



PAD = P + 2


def l1_xattn(net, prefetch):
    nc = net.nc
    w = net.weights("l1_xattn")
    with ExitStack() as sub:
        sb = net.scratch(sub)
        decay = sb("decay", [P, FT])
        decays = sb("decays", [P, FT, NB * PAD])
        ek = sb("exp_k", [P, FT, NB, PAD])
        ekv = sb("exp_k_v", [P, FT, NB, PAD])
        cur = sb("exp_u_k", [P, FT, T])
        gate = sb("sigmoid_r", [P, FT, T])
        scans = sb("scans", [P, 4, NB, PAD])
        num, den = sb("numerator", [P, FT, T]), sb("denominator", [P, FT, T])
        (xT_in_psum, gate_ready, decay_ready, zeros_ready, ek_ready, cur_ready, ekv_ready, curv_ready,
         scans_ready, sums_ready, out_ready, out_in_psum, var_ready, rstd_ready,
         dve_steps, pool_steps) = net.signals(16)

        def by_seq(ap):
            return ap.rearrange("p (b t) -> p b t", b=NB)

        with nc.Block() as block:
            @block.sync
            def _(sp):
                prefetch(sp)

            @block.tensor
            def _(pe):
                transposes(pe, net, net.x, (0, 1), xT_in_psum)
                pe.wait_ge(out_ready, 2)
                for half_ in range(2):
                    for b in (2 * half_, 2 * half_ + 1):
                        for f in range(FT):
                            mm = pe.transpose(half(net, (2, 3), b)[:, f * P:(f + 1) * P],
                                              num[:, f, seq(b)], net.ident[:])
                        mm.then_inc(out_in_psum, 1)

            @block.scalar
            def _(act):
                act.wait_ge(net.ready["l1_xattn"], 16)
                nc.scalar.activation(decay[:], w["w"], ACT.Exp).then_inc(decay_ready, 1)
                act.wait_ge(zeros_ready, 1)
                for f in range(FT):
                    nc.scalar.activation(ek[:, f, :, 1:P + 1], by_seq(net.ctxT[:, f, :]),
                                         ACT.Exp).then_inc(ek_ready, 1)
                for f in range(FT):
                    nc.scalar.activation(cur[:, f, :], net.ctxT[:, f, :], ACT.Exp,
                                         bias=w["u"][:, f:f + 1]).then_inc(cur_ready, 1)
                for f in range(FT):
                    act.wait_ge(xT_in_psum, f + 1)
                    nc.scalar.activation(gate[:, f, :], net.banks[f][:], ACT.Sigmoid).then_inc(gate_ready, 1)
                root_act(act, net, var_ready, rstd_ready)

            @block.vector
            def _(dve):
                chain = Chain(dve, dve_steps)
                dve.wait_ge(net.ready["l1_xattn"], 16)
                dve.wait_ge(decay_ready, 1)
                for f in range(FT):
                    chain.step(nc.vector.tensor_scalar(decays[:, f, :], net.inside[:], decay[:, f:f + 1],
                                                       None, ALU.mult))
                chain.settle()
                for f in range(FT):
                    dve.wait_ge(ek_ready, f + 1)
                    dve.wait_ge(ekv_ready, f + 1)
                    if f:
                        dve.wait_ge(scans_ready, 4 * f)
                        dve.wait_ge(sums_ready, 2 * f)
                    for k, (src, back) in enumerate(((ekv, False), (ek, False), (ekv, True), (ek, True))):
                        data = src[:, f, :, :].rearrange("p b t -> p (b t)")
                        mult = decays[:, f, :]
                        dst = scans[:, k, :, :].rearrange("p b t -> p (b t)")
                        if back:
                            data, mult, dst = data[:, ::-1], mult[:, ::-1], dst[:, ::-1]
                        nc.vector.tensor_tensor_scan(dst, mult, data, 0.0, ALU.mult,
                                                     ALU.add).then_inc(scans_ready, 1)
                    dve.wait_ge(scans_ready, 4 * (f + 1))
                    dve.wait_ge(curv_ready, f + 1)
                    for k, (out, own) in enumerate(((num, num), (den, cur))):
                        chain(nc.vector.tensor_tensor(scans[:, k, :, 0:P], scans[:, k, :, 0:P],
                                                      scans[:, 2 + k, :, 2:P + 2], ALU.add))
                        if k == 1:
                            dve.wait_ge(cur_ready, f + 1)
                        nc.vector.tensor_tensor(by_seq(out[:, f, :]), scans[:, k, :, 0:P],
                                                by_seq(own[:, f, :]), ALU.add).then_inc(sums_ready, 1)
                    dve.wait_ge(sums_ready, 2 * (f + 1))
                    dve.wait_ge(gate_ready, f + 1)
                    chain(nc.vector.reciprocal(den[:, f, :], den[:, f, :]))
                    chain(nc.vector.tensor_tensor(num[:, f, :], num[:, f, :], den[:, f, :], ALU.mult))
                    nc.vector.tensor_tensor(num[:, f, :], num[:, f, :], gate[:, f, :],
                                            ALU.mult).then_inc(out_ready, 1)
                residual_norm_dve(dve, net, chain, net.x, lambda b: half(net, (2, 3), b), out_in_psum,
                                  PAIR_DONE, var_ready, rstd_ready)

            @block.gpsimd
            def _(pool):
                nc.gpsimd.memset(ek[:], 0.0).then_inc(pool_steps, 1)
                nc.gpsimd.memset(ekv[:], 0.0).then_inc(pool_steps, 1)
                pool.wait_ge(pool_steps, 2)
                nc.gpsimd.engine_nop().then_inc(zeros_ready, 1)
                for f in range(FT):
                    pool.wait_ge(ek_ready, f + 1)
                    nc.gpsimd.tensor_tensor(ekv[:, f, :, 1:P + 1], ek[:, f, :, 1:P + 1],
                                            by_seq(net.ctxT[:, f, :]), ALU.mult).then_inc(ekv_ready, 1)
                for f in range(FT):
                    pool.wait_ge(cur_ready, f + 1)
                    nc.gpsimd.tensor_tensor(num[:, f, :], cur[:, f, :], net.ctxT[:, f, :],
                                            ALU.mult).then_inc(curv_ready, 1)
    net.end_sublayer()



def floor_dve(nc, chain, out, src, whole, above):
    chain(nc.vector.tensor_copy(whole, src))
    chain(nc.vector.tensor_copy(out, whole))
    chain(nc.vector.tensor_tensor(above, out, src, ALU.is_gt))
    chain(nc.vector.tensor_tensor(out, out, above, ALU.subtract))


def l1_ffn(net, prefetch):
    nc = net.nc
    w = net.weights("l1_ffn")
    b2 = tiles(w["b2"], EXPERTS)
    with ExitStack() as sub:
        sb = net.scratch(sub)
        (xT_in_psum, xT0_ready, xT1_ready, var_ready, rstd_ready, dve_steps) = net.signals(10)[4:]
        experts = Experts(net, sub, "l1_ffn", net.signals(4), 8, ACT.Relu, bias=w["b1"],
                          slots=EXPERT_ROOM // EXPERT_COLS["l1_ffn"])
        keys, octave, fl = (sb(n, [P, NB]) for n in ("keys", "octave", "floor"))
        above, whole = sb("above", [P, NB]), sb("whole", [P, NB], I32)
        gates = sb("gates", [P, NB, EXPERTS])
        with nc.Block() as block:
            @block.sync
            def _(sp):
                for e in range(experts.slots, EXPERTS):
                    sp.wait_ge(experts.out_in_psum, NB * (e - experts.slots + 1))
                    at = (e % experts.slots) * EXPERT_COLS["l1_ffn"]
                    sp.dma_start(net.e_room[:, at:at + EXPERT_COLS["l1_ffn"]],
                                 net.params["l1_ffn_experts"][:, e * EXPERT_COLS["l1_ffn"]:
                                                              (e + 1) * EXPERT_COLS["l1_ffn"]]
                                 ).then_inc(net.expert_ready[e], 16)
                prefetch(sp)

            @block.tensor
            def _(pe):
                transposes(pe, net, net.x, (0, 1), xT_in_psum)
                pe.wait_ge(xT0_ready, 1)
                pe.wait_ge(xT1_ready, 1)
                experts.run_pe(pe)

            @block.scalar
            def _(act):
                act.wait_ge(xT_in_psum, 1)
                nc.scalar.copy(net.xT[:, 0, :], net.banks[0][:]).then_inc(xT0_ready, 1)
                act.wait_ge(net.ready["l1_ffn"], 16)
                experts.run_act(act)
                root_act(act, net, var_ready, rstd_ready)

            @block.vector
            def _(dve):
                chain = Chain(dve, dve_steps)
                dve.wait_ge(net.ready["l1_ffn"], 16)
                dve.wait_ge(xT_in_psum, 2)
                nc.vector.tensor_copy(net.xT[:, 1, :], net.banks[1][:]).then_inc(xT1_ready, 1)
                chain(nc.vector.tensor_tensor(net.r[:], net.x[:], w["wr"].unsqueeze(1).broadcast_to([P, NB, D]),
                                              ALU.mult))
                chain(nc.vector.reduce_sum(keys[:], net.r[:], AX_X))
                chain(nc.vector.tensor_scalar(keys[:], keys[:], w["br"], None, ALU.add))
                floor_dve(nc, chain, fl[:], keys[:], whole[:], above[:])
                chain(nc.vector.tensor_scalar(keys[:], fl[:], 1.0 / EXPERTS, None, ALU.mult))
                floor_dve(nc, chain, octave[:], keys[:], whole[:], above[:])
                chain(nc.vector.tensor_scalar(octave[:], octave[:], float(-EXPERTS), None, ALU.mult))
                chain(nc.vector.tensor_tensor(fl[:], fl[:], octave[:], ALU.add))
                for e in range(EXPERTS):
                    chain.step(nc.vector.tensor_scalar(gates[:, :, e], fl[:], float(e), None, ALU.is_equal))
                chain.settle()
                for e in range(EXPERTS):
                    for b in range(NB):
                        chain.step(nc.vector.scalar_tensor_tensor(
                            out=net.r[:, b, :], in0=b2[:, e, :], scalar=gates[:, b, e:e + 1],
                            in1=net.x[:, b, :] if e == 0 else net.r[:, b, :], op0=ALU.mult, op1=ALU.add))
                    chain.settle()
                experts.run_dve(dve, gates, net.r)
                dve.wait_ge(experts.out_taken, NB * EXPERTS)
                finish_norm_dve(dve, net, chain, var_ready, rstd_ready)
    net.end_sublayer()



CONV = 4
CT_ = CONV * NB


def l2_attn(net, prefetch):
    nc = net.nc
    w = net.weights("l2_attn")
    wqk, wv, wo, ch_w1 = (tiles(w[n], FT) for n in ("wqk", "wv", "wo", "ch_w1"))
    c1, c2, conv2_b = w["c1"], w["c2"], w["conv2_b"]
    ROWS = slice(0, CT_)
    with ExitStack() as sub:
        sb = net.scratch(sub)
        dq, dqk = sb("q_less_mean", [P, NB, D]), sb("products", [P, NB, D])
        qstats, qmv = sb("qk_stats", [P, NB, 2, 6]), sb("qk_mean_var", [P, NB, 2, 2])
        cov = sb("covariance", [P, NB])
        num, den, tmp = (sb(n, [P, NB]) for n in ("numerator", "denominator", "partial"))
        base = sb("attn_base", [P, CONV, NB])
        rows_in = sb("rows", [CT_, P + 2])
        h, hh = sb("conv1", [CT_, P]), sb("conv1_less_mean", [CT_, P])
        act_in = sb("conv2_input", [CT_, P + 2])
        z = sb("conv2", [CT_, P])
        one = {n: sb(n, [CT_, 1]) for n in ("row_sum", "group_mean", "square_sum", "group_var", "scale")}
        final, weight_rows = sb("final", [NB, P]), sb("weight_rows", [NB, P])
        total = sb("exp_sum", [NB, 1])
        weights = sb("token_weights", [P, NB])
        mean = sb("feature_sums", [P, FT, NB])
        ch_h, ch = sb("channel_hidden", [64, NB]), sb("channel_weights", [P, FT, NB])
        vT = sb("weighted_vT", [P, FT, T])
        xb = sb("x_plus_bias", [P, NB, D])
        (xT_in_psum, xT0_ready, xT1_ready, qk_in_psum, dq_ready, qk_taken, base_ready, rows_in_psum, rows_ready,
         sum_ready, mean_in_psum, centred_ready, squares_ready, var_in_psum, gvar_ready, groot_ready,
         scale_ready, relu_ready, z_ready, z_in_psum, final_ready, sig_ready, exp_ready, weight_ready,
         weights_in_psum, v_in_psum, fmean_ready, ch1_in_psum, ch1_ready, ch2_in_psum, ch_ready,
         vT_ready, y_ready, xb_ready, var_ready, rstd_ready, dve_steps, zeros_ready,
         act_steps) = net.signals(39)
        QK, V, SMALL, CHANNEL, Y = (2, 3, 4, 5), (6, 7), 0, 1, (2, 3)
        small, channel = net.banks[SMALL], net.banks[CHANNEL]
        with nc.Block() as block:
            @block.sync
            def _(sp):
                prefetch(sp)

            @block.tensor
            def _(pe):
                pe.wait_ge(net.ready["l2_attn"], 16)
                transposes(pe, net, net.x, (0, 1), xT_in_psum)
                pe.wait_ge(xT0_ready, 1)
                pe.wait_ge(xT1_ready, 1)
                for b in range(NB):
                    project_tokens(pe, net.banks[QK[b]][:], net.xT, b, wqk).then_inc(qk_in_psum, 1)
                for m in range(FT):
                    project(pe, net.banks[V[m]][:], wv, net.xT, m).then_inc(v_in_psum, 1)
                pe.wait_ge(fmean_ready, 1)
                for f in range(FT):
                    mm = pe.matmul(channel[0:64, 0:NB], ch_w1[:, f, :], mean[:, f, :],
                                   start=f == 0, stop=f == FT - 1)
                mm.then_inc(ch1_in_psum, 1)
                pe.wait_ge(ch1_ready, 1)
                for f in range(FT):
                    mm = pe.matmul(channel[:, f * NB:(f + 1) * NB], w["ch_w2"][0:64, f * P:(f + 1) * P],
                                   ch_h[:], start=True, stop=True)
                mm.then_inc(ch2_in_psum, 1)
                pe.wait_ge(base_ready, 1)
                pe.transpose(small[ROWS, 0:P], base[:].rearrange("p c b -> p (c b)"),
                             net.ident[:]).then_inc(rows_in_psum, 1)
                pe.wait_ge(sum_ready, 1)
                pe.wait_ge(rows_ready, 1)
                pe.matmul(small[ROWS, 0:1], w["groups"][ROWS, 0:CT_], one["row_sum"][:],
                          start=True, stop=True).then_inc(mean_in_psum, 1)
                pe.wait_ge(squares_ready, 1)
                pe.wait_ge(centred_ready, 1)
                pe.matmul(small[ROWS, 1:2], w["groups"][ROWS, 0:CT_], one["square_sum"][:],
                          start=True, stop=True).then_inc(var_in_psum, 1)
                pe.wait_ge(z_ready, 1)
                pe.matmul(small[0:NB, 0:P], w["channels"][ROWS, 0:NB], z[:],
                          start=True, stop=True).then_inc(z_in_psum, 1)
                pe.wait_ge(weight_ready, 1)
                pe.transpose(small[:, 0:NB], weight_rows[:], net.ident[0:NB, 0:NB]).then_inc(weights_in_psum, 1)
                pe.wait_ge(vT_ready, FT)
                for b in range(NB):
                    project_tokens(pe, half(net, Y, b), vT, b, wo).then_inc(y_ready, 1)

            @block.scalar
            def _(act):
                act.wait_ge(net.ready["l2_attn"], 16)
                act.wait_ge(xT_in_psum, 1)
                nc.scalar.copy(net.xT[:, 0, :], net.banks[0][:]).then_inc(xT0_ready, 1)
                act.wait_ge(ch1_in_psum, 1)
                nc.scalar.activation(ch_h[:], channel[0:64, 0:NB], ACT.Relu, scale=1.0 / P,
                                     bias=w["ch_b1"][0:64, 0:1]).then_inc(ch1_ready, 1)
                act.wait_ge(ch2_in_psum, 1)
                for f in range(FT):
                    nc.scalar.activation(ch[:, f, :], channel[:, f * NB:(f + 1) * NB], ACT.Sigmoid,
                                         bias=w["ch_b2"][:, f:f + 1]).then_inc(ch_ready, 1)
                act.wait_ge(gvar_ready, 1)
                nc.scalar.activation(one["group_var"][:], one["group_var"][:], ACT.Sqrt).then_inc(groot_ready, 1)
                act.wait_ge(scale_ready, 1)
                act.wait_ge(zeros_ready, 1)
                nc.scalar.activation(act_in[:, 1:P + 1], hh[:], ACT.Relu, scale=one["scale"][:, 0:1],
                                     bias=w["gn_b"][ROWS, 0:1]).then_inc(relu_ready, 1)
                act.wait_ge(final_ready, 1)
                nc.scalar.activation(final[:], final[:], ACT.Sigmoid).then_inc(sig_ready, 1)
                act.wait_ge(sig_ready, 1)
                nc.scalar.activation(weight_rows[:], final[:], ACT.Exp,
                                     accum_out=total[:]).then_inc(exp_ready, 1)
                root_act(act, net, var_ready, rstd_ready)

            @block.vector
            def _(dve):
                chain = Chain(dve, dve_steps)
                tt, ts, stt = nc.vector.tensor_tensor, nc.vector.tensor_scalar, nc.vector.scalar_tensor_tensor
                dve.wait_ge(net.ready["l2_attn"], 16)
                dve.wait_ge(xT_in_psum, 2)
                nc.vector.tensor_copy(net.xT[:, 1, :], net.banks[1][:]).then_inc(xT1_ready, 1)
                dve.wait_ge(xT0_ready, 1)
                dve.wait_ge(xT1_ready, 1)
                nc.vector.reduce_sum(mean[:], net.xT[:].rearrange("p f (b t) -> p f b t", b=NB),
                                     AX_X).then_inc(fmean_ready, 1)
                for b in range(NB):
                    dve.wait_ge(qk_in_psum, b + 1)
                    for s in range(2):
                        chain.step(nc.vector.bn_stats(qstats[:, b, s, :],
                                                      net.banks[QK[b]][:, s * D:(s + 1) * D]))
                    chain.settle()
                    for s in range(2):
                        chain.step(nc.vector.bn_aggr(qmv[:, b, s, :], qstats[:, b, s, :]))
                    chain.settle()
                    chain(ts(dq[:, b, :], net.banks[QK[b]][:, 0:D], qmv[:, b, 0, 0:1], None, ALU.subtract))
                    chain.step(stt(out=dqk[:, b, :], in0=net.banks[QK[b]][:, D:2 * D],
                                   scalar=qmv[:, b, 1, 0:1], in1=dq[:, b, :], op0=ALU.subtract,
                                   op1=ALU.mult, accum_out=cov[:, b:b + 1]))
                chain.settle()
                mq, mk, vq, vk = (qmv[:, :, s, k] for s, k in ((0, 0), (1, 0), (0, 1), (1, 1)))
                chain(tt(num[:], mq, mk, ALU.mult))
                chain(ts(num[:], num[:], 2.0, c1, ALU.mult, ALU.add))
                chain(ts(tmp[:], cov[:], 2.0 / (D - 1), c2, ALU.mult, ALU.add))
                chain(tt(num[:], num[:], tmp[:], ALU.mult))
                chain(tt(den[:], mq, mq, ALU.mult))
                chain(tt(tmp[:], mk, mk, ALU.mult))
                chain(stt(out=den[:], in0=den[:], scalar=c1, in1=tmp[:], op0=ALU.add, op1=ALU.add))
                chain(tt(tmp[:], vq, vk, ALU.add))
                chain(ts(tmp[:], tmp[:], D / (D - 1), c2, ALU.mult, ALU.add))
                chain(tt(den[:], den[:], tmp[:], ALU.mult))
                chain(ts(den[:], den[:], 1e-7, None, ALU.add))
                chain(nc.vector.reciprocal(den[:], den[:]))
                chain(tt(num[:], num[:], den[:], ALU.mult))
                chain(tt(base[:], num[:].unsqueeze(1).broadcast_to([P, CONV, NB]),
                         num[:].unsqueeze(1).broadcast_to([P, CONV, NB]), ALU.mult))
                nc.vector.engine_nop().then_inc(base_ready, 1)
                for f in range(FT):
                    dve.wait_ge(v_in_psum, f + 1)
                    dve.wait_ge(ch_ready, f + 1)
                    tt(vT[:, f, :].rearrange("p (b t) -> p b t", b=NB),
                       net.banks[V[f]][:].rearrange("p (b t) -> p b t", b=NB),
                       ch[:, f, :].unsqueeze(2).broadcast_to([P, NB, P]), ALU.mult).then_inc(vT_ready, 1)
                dve.wait_ge(rows_in_psum, 1)
                dve.wait_ge(zeros_ready, 1)
                nc.vector.tensor_copy(rows_in[:, 1:P + 1], small[ROWS, 0:P]).then_inc(rows_ready, 1)
                dve.wait_ge(rows_ready, 1)
                conv1, conv2 = w["conv1"], w["conv2"]
                chain(ts(h[:], rows_in[:, 0:P], conv1[ROWS, 0:1], None, ALU.mult))
                chain(stt(out=h[:], in0=rows_in[:, 1:P + 1], scalar=conv1[ROWS, 1:2], in1=h[:],
                          op0=ALU.mult, op1=ALU.add))
                chain(stt(out=h[:], in0=rows_in[:, 2:P + 2], scalar=conv1[ROWS, 2:3], in1=h[:],
                          op0=ALU.mult, op1=ALU.add))
                nc.vector.reduce_sum(one["row_sum"][:], h[:], AX_X).then_inc(sum_ready, 1)
                dve.wait_ge(mean_in_psum, 1)
                chain(ts(one["group_mean"][:], small[ROWS, 0:1], 1.0 / (2 * P), None, ALU.mult))
                chain(ts(hh[:], h[:], one["group_mean"][:, 0:1], None, ALU.subtract))
                nc.vector.engine_nop().then_inc(centred_ready, 1)
                chain(tt(h[:], hh[:], hh[:], ALU.mult))
                nc.vector.reduce_sum(one["square_sum"][:], h[:], AX_X).then_inc(squares_ready, 1)
                dve.wait_ge(var_in_psum, 1)
                chain(ts(one["group_var"][:], small[ROWS, 1:2], 1.0 / (2 * P), EPS, ALU.mult, ALU.add))
                nc.vector.reciprocal(one["group_var"][:], one["group_var"][:]).then_inc(gvar_ready, 1)
                dve.wait_ge(groot_ready, 1)
                tt(one["scale"][:], one["group_var"][:], w["gn_g"][ROWS, :], ALU.mult).then_inc(scale_ready, 1)
                dve.wait_ge(relu_ready, 1)
                chain(ts(z[:], act_in[:, 0:P], conv2[ROWS, 0:1], None, ALU.mult))
                chain(stt(out=z[:], in0=act_in[:, 1:P + 1], scalar=conv2[ROWS, 1:2], in1=z[:],
                          op0=ALU.mult, op1=ALU.add))
                stt(out=z[:], in0=act_in[:, 2:P + 2], scalar=conv2[ROWS, 2:3], in1=z[:],
                    op0=ALU.mult, op1=ALU.add).then_inc(z_ready, 1)
                dve.wait_ge(z_in_psum, 1)
                stt(out=final[:], in0=small[0:NB, 0:P], scalar=conv2_b[0:NB, 0:1],
                    in1=rows_in[0:NB, 1:P + 1], op0=ALU.add, op1=ALU.add).then_inc(final_ready, 1)
                dve.wait_ge(exp_ready, 1)
                chain(nc.vector.reciprocal(total[:], total[:]))
                ts(weight_rows[:], weight_rows[:], total[:, 0:1], None, ALU.mult).then_inc(weight_ready, 1)
                dve.wait_ge(weights_in_psum, 1)
                chain(nc.vector.tensor_copy(weights[:], small[:, 0:NB]))
                dve.wait_ge(xb_ready, 1)
                for b in range(NB):
                    dve.wait_ge(y_ready, PAIR_DONE[b])
                    chain.step(stt(out=net.r[:, b, :], in0=half(net, Y, b), scalar=weights[:, b:b + 1],
                                   in1=xb[:, b, :], op0=ALU.mult, op1=ALU.add))
                chain.settle()
                finish_norm_dve(dve, net, chain, var_ready, rstd_ready)

            @block.gpsimd
            def _(pool):
                nc.gpsimd.memset(rows_in[:], 0.0)
                nc.gpsimd.memset(act_in[:], 0.0).then_inc(zeros_ready, 1)
                pool.wait_ge(net.ready["l2_attn"], 16)
                nc.gpsimd.tensor_tensor(xb[:], net.x[:], w["bo"].unsqueeze(1).broadcast_to([P, NB, D]),
                                        ALU.add).then_inc(xb_ready, 1)
    net.end_sublayer()



def l2_xattn(net, prefetch):
    nc = net.nc
    w = net.weights("l2_xattn")
    wq, wk, wv, wo = (tiles(w[n], FT) for n in ("wq", "wk", "wv", "wo"))
    with ExitStack() as sub:
        sig = net.signals(26)
        (xT_in_psum, xT0_ready, xT1_ready, qk_in_psum, q_ready, k_ready, v_in_psum, v_ready, xb_ready,
         var_ready, rstd_ready, dve_steps) = sig[13:25]
        heads = Heads16(net, sub, sig[:9], masked=False, scale=DH ** -0.5)
        back = OutputProjection(net, sub, heads, wo, sig[9:13])
        xb = net.scratch(sub)("x_plus_bias", [P, NB, D])
        with nc.Block() as block:
            @block.sync
            def _(sp):
                prefetch(sp)

            @block.tensor
            def _(pe):
                pe.wait_ge(net.ready["l2_xattn"], 16)
                transposes(pe, net, net.x, (0, 1), xT_in_psum)
                for m in range(4):
                    project(pe, net.banks[2 + m][:], wk, net.ctxT, m).then_inc(qk_in_psum, 1)
                for b in range(NB):
                    project_tokens(pe, half(net, (6, 7), b), net.ctxT, b, wv).then_inc(v_in_psum, 1)
                pe.wait_ge(xT0_ready, 1)
                pe.wait_ge(xT1_ready, 1)
                for m in range(4):
                    pe.wait_ge(k_ready, m + 1)
                    project(pe, net.banks[2 + m][:], wq, net.xT, m).then_inc(qk_in_psum, 1)
                pe.wait_ge(q_ready, 4)
                pe.wait_ge(v_ready, NB)
                heads.run_pe(pe)
                back.run_pe(pe)

            @block.scalar
            def _(act):
                act.wait_ge(net.ready["l2_xattn"], 16)
                act.wait_ge(xT_in_psum, 1)
                nc.scalar.copy(net.xT[:, 0, :], net.banks[0][:]).then_inc(xT0_ready, 1)
                for m in range(4):
                    act.wait_ge(qk_in_psum, m + 1)
                    nc.scalar.activation(heads.kT[:, m, :], net.banks[2 + m][:], ACT.Identity,
                                         bias=w["bk"][:, m:m + 1]).then_inc(k_ready, 1)
                for m in range(4):
                    act.wait_ge(qk_in_psum, m + 5)
                    nc.scalar.activation(heads.qT[:, m, :], net.banks[2 + m][:], ACT.Identity,
                                         bias=w["bq"][:, m:m + 1]).then_inc(q_ready, 1)
                heads.run_act(act)
                back.run_act(act)
                root_act(act, net, var_ready, rstd_ready)

            @block.vector
            def _(dve):
                chain = Chain(dve, dve_steps)
                dve.wait_ge(net.ready["l2_xattn"], 16)
                dve.wait_ge(xT_in_psum, 2)
                nc.vector.tensor_copy(net.xT[:, 1, :], net.banks[1][:]).then_inc(xT1_ready, 1)
                for b in range(NB):
                    dve.wait_ge(v_in_psum, PAIR_DONE[b])
                    nc.vector.tensor_tensor(net.v1[:, b, :, 0:DH],
                                            half(net, (6, 7), b).rearrange("p (h d) -> p h d", h=NH),
                                            w["bv"].rearrange("p (h d) -> p h d", h=NH),
                                            ALU.add).then_inc(v_ready, 1)
                heads.run_dve(dve, chain)
                back.run_dve(dve)
                dve.wait_ge(xb_ready, 1)
                residual_norm_dve(dve, net, chain, xb, lambda b: half(net, back.Y, b), back.y_ready,
                                  PAIR_DONE, var_ready, rstd_ready)

            @block.gpsimd
            def _(pool):
                pool.wait_ge(net.ready["l2_xattn"], 16)
                nc.gpsimd.tensor_tensor(xb[:], net.x[:], w["bo"].unsqueeze(1).broadcast_to([P, NB, D]),
                                        ALU.add).then_inc(xb_ready, 1)
    net.end_sublayer()



def l2_ffn(net, prefetch):
    nc = net.nc
    w = net.weights("l2_ffn")
    router, sw1, sw3, sw2 = tiles(w["router"], FT), tiles(w["sw1"], FT), tiles(w["sw3"], FT), tiles(w["sw2"], 4)
    with ExitStack() as sub:
        sb = net.scratch(sub)
        (xT_in_psum, xT0_ready, xT1_ready, logits_in_psum, sigmoid_ready, gate_in_psum, silu_ready,
         up_in_psum, swiglu_ready, shared_in_psum, shared_taken, var_ready, rstd_ready,
         dve_steps) = net.signals(18)[4:]
        experts = Experts(net, sub, "l2_ffn", net.signals(4), 2, ACT.Gelu)
        s, gates, chosen, rank = (sb(n, [P, NB, EXPERTS]) for n in ("sigmoid", "gates", "chosen", "rank"))
        greater, equal = (sb(n, [P, NB, EXPERTS, EXPERTS]) for n in ("greater", "equal"))
        total, usable, spare = (sb(n, [P, NB]) for n in ("gate_sum", "usable", "spare"))
        silu, swiglu = sb("silu", [P, 4, T]), sb("swiglu", [P, 4, T])
        logits = net.banks[0][:, 0:NB * EXPERTS].rearrange("p (b e) -> p b e", b=NB)
        GATE, UP, SHARED = (2, 3), (4, 5), (6, 7)
        with nc.Block() as block:
            @block.sync
            def _(sp):
                prefetch(sp)

            @block.tensor
            def _(pe):
                pe.wait_ge(net.ready["l2_ffn"], 16)
                transposes(pe, net, net.x, (0, 1), xT_in_psum)
                pe.wait_ge(xT0_ready, 1)
                pe.wait_ge(xT1_ready, 1)
                for b in range(NB):
                    mm = project_tokens(pe, logits[:, b, :], net.xT, b, router)
                mm.then_inc(logits_in_psum, 1)
                for m in range(4):
                    if m >= 2:
                        pe.wait_ge(swiglu_ready, m - 1)
                    project(pe, net.banks[GATE[m % 2]][:], sw1, net.xT, m).then_inc(gate_in_psum, 1)
                    project(pe, net.banks[UP[m % 2]][:], sw3, net.xT, m).then_inc(up_in_psum, 1)
                pe.wait_ge(swiglu_ready, 4)
                for b in range(NB):
                    project_tokens(pe, half(net, SHARED, b), swiglu, b, sw2).then_inc(shared_in_psum, 1)
                experts.run_pe(pe, before_out=lambda: pe.wait_ge(shared_taken, NB))

            @block.scalar
            def _(act):
                act.wait_ge(xT_in_psum, 1)
                nc.scalar.copy(net.xT[:, 0, :], net.banks[0][:]).then_inc(xT0_ready, 1)
                act.wait_ge(logits_in_psum, 1)
                nc.scalar.activation(s[:], logits, ACT.Sigmoid).then_inc(sigmoid_ready, 1)
                for m in range(4):
                    act.wait_ge(gate_in_psum, m + 1)
                    nc.scalar.activation(silu[:, m, :], net.banks[GATE[m % 2]][:],
                                         ACT.Silu).then_inc(silu_ready, 1)
                experts.run_act(act)
                root_act(act, net, var_ready, rstd_ready)

            @block.vector
            def _(dve):
                chain = Chain(dve, dve_steps)
                tt, ts = nc.vector.tensor_tensor, nc.vector.tensor_scalar
                wide = [P, NB, EXPERTS]
                dve.wait_ge(net.ready["l2_ffn"], 16)
                dve.wait_ge(xT_in_psum, 2)
                nc.vector.tensor_copy(net.xT[:, 1, :], net.banks[1][:]).then_inc(xT1_ready, 1)
                for m in range(4):
                    dve.wait_ge(silu_ready, m + 1)
                    dve.wait_ge(up_in_psum, m + 1)
                    tt(swiglu[:, m, :], silu[:, m, :], net.banks[UP[m % 2]][:], ALU.mult).then_inc(swiglu_ready, 1)
                dve.wait_ge(sigmoid_ready, 1)
                chain(tt(rank[:], s[:], w["router_bias"].unsqueeze(1).broadcast_to(wide), ALU.add))
                chain(nc.vector.tensor_copy(gates[:], rank[:]))
                top2_dve(net, chain, gates, chosen, greater, equal, rank)
                chain(tt(gates[:], s[:], chosen[:], ALU.mult))
                chain(nc.vector.reduce_sum(total[:], gates[:], AX_X))
                chain(ts(usable[:], total[:], 1e-9, None, ALU.is_gt))
                chain(ts(total[:], total[:], 1e-9, None, ALU.add))
                chain(nc.vector.reciprocal(total[:], total[:]))
                chain(tt(total[:], total[:], usable[:], ALU.mult))
                chain(tt(gates[:], gates[:], total[:].unsqueeze(2).broadcast_to(wide), ALU.mult))
                chain(ts(spare[:], usable[:], -0.5, 0.5, ALU.mult, ALU.add))
                chain(tt(chosen[:], chosen[:], spare[:].unsqueeze(2).broadcast_to(wide), ALU.mult))
                chain(tt(gates[:], gates[:], chosen[:], ALU.add))
                for b in range(NB):
                    dve.wait_ge(shared_in_psum, PAIR_DONE[b])
                    tt(net.r[:, b, :], net.x[:, b, :], half(net, SHARED, b), ALU.add).then_inc(shared_taken, 1)
                dve.wait_ge(shared_taken, NB)
                experts.run_dve(dve, gates, net.r)
                dve.wait_ge(experts.out_taken, NB * EXPERTS)
                finish_norm_dve(dve, net, chain, var_ready, rstd_ready)
    net.end_sublayer()



DI, STATES, TAPS = 512, 16, 4
DT_ = DI // P


def l3_attn(net, prefetch):
    nc = net.nc
    w = net.weights("l3_attn")
    w_in, w_x, w_dt, w_out = tiles(w["w_in"], FT), tiles(w["w_x"], DT_), tiles(w["w_dt"], DT_), tiles(w["w_out"], DT_)
    conv_w = w["conv_w"].rearrange("p (m k) -> p m k", m=DT_)
    with ExitStack() as sub:
        sb = net.scratch(sub)
        u = sb("conv_silu", [P, DT_, T])
        zs = sb("silu_z", [P, DT_, T])
        dt = sb("step", [P, DT_, T])
        dtu = sb("step_times_input", [P, DT_, T])
        bc = sb("b_and_c", [2 * STATES, T])
        a = sb("minus_exp_a_log", [P, DT_ * STATES])
        c_row = [sb(f"c_on_all_rows{i}", [P, T]) for i in range(2)]
        room = net.e_room
        padded = room[:, 0:DT_ * NB * (P + 3)].rearrange("p (m b t) -> p m b t", m=DT_, b=NB)
        at = DT_ * NB * (P + 3)
        conv, delta, ex, one_ex, lost, positive = (
            room[:, at + k * DT_ * T:at + (k + 1) * DT_ * T].rearrange("p (m t) -> p m t", m=DT_)
            for k in range(6))
        ring = [room[:, k * DT_ * T:(k + 1) * DT_ * T].rearrange("p (m t) -> p m t", m=DT_)
                for k in range(8)]
        decay, drive, state, out = ring[0:2], ring[2:4], ring[4:6], ring[6:8]
        (xT_in_psum, xT0_ready, xT1_ready, zeros_ready, in_in_psum, in_taken, conv_ready, u_ready,
         x_in_psum, delta_ready, bc_ready, dt_in_psum, positive_ready, exp_ready, one_ready, log_ready,
         lost_ready, dt_ready, a_ready, b_in_psum, c_in_psum, drive_ready,
         c_ready, decay_ready, state_ready, out_ready, summed, yz_ready, y_ready, var_ready,
         rstd_ready, dve_steps, act_steps) = net.signals(33)
        with nc.Block() as block:
            @block.sync
            def _(sp):
                prefetch(sp)

            @block.tensor
            def _(pe):
                pe.wait_ge(net.ready["l3_attn"], 16)
                transposes(pe, net, net.x, (0, 1), xT_in_psum)
                pe.wait_ge(xT0_ready, 1)
                pe.wait_ge(xT1_ready, 1)
                for m in range(2 * DT_):
                    if m >= 4:
                        pe.wait_ge(in_taken, m - 3)
                    project(pe, net.banks[2 + m % 4][:], w_in, net.xT, m).then_inc(in_in_psum, 1)
                pe.wait_ge(in_taken, 2 * DT_)
                pe.wait_ge(u_ready, DT_)
                for m in range(DT_):
                    project(pe, net.banks[2 + m][:], w_x, u, m).then_inc(x_in_psum, 1)
                for k in range(DT_):
                    mm = pe.matmul(net.banks[6][0:2 * STATES, :], w_x[:, k, DI:DI + 2 * STATES], u[:, k, :],
                                   start=k == 0, stop=k == DT_ - 1)
                mm.then_inc(x_in_psum, 1)
                pe.wait_ge(delta_ready, DT_)
                for m in range(DT_):
                    project(pe, net.banks[2 + m][:], w_dt, delta, m).then_inc(dt_in_psum, 1)
                pe.wait_ge(bc_ready, 1)
                pe.wait_ge(positive_ready, DT_)
                pe.wait_ge(exp_ready, DT_)

                def add_up(s):
                    pe.wait_ge(out_ready, s + 1)
                    for m in range(DT_):
                        mm = pe.matmul(net.banks[m][:], net.ident[:], out[s % 2][:, m, :],
                                       start=s == 0, stop=s == STATES - 1)
                    mm.then_inc(summed, 1)

                for s in range(STATES):
                    if s >= 2:
                        pe.wait_ge(drive_ready, s - 1)
                        pe.wait_ge(c_ready, s - 1)
                    for bank, col, done in ((4, s, b_in_psum), (6, STATES + s, c_in_psum)):
                        pe.matmul(net.banks[bank + s % 2][:],
                                  net.ident[0:2 * STATES, col:col + 1].broadcast_to([2 * STATES, P]),
                                  bc[:], start=True, stop=True).then_inc(done, 1)
                    if s:
                        add_up(s - 1)
                add_up(STATES - 1)
                pe.wait_ge(yz_ready, DT_)
                for b in range(NB):
                    project_tokens(pe, half(net, (4, 5), b), dtu, b, w_out).then_inc(y_ready, 1)

            @block.scalar
            def _(act):
                chain = Chain(act, act_steps)
                act.wait_ge(net.ready["l3_attn"], 16)
                chain(nc.scalar.activation(a[:], w["a_log"], ACT.Exp))
                nc.scalar.mul(a[:], a[:], -1.0).then_inc(a_ready, 1)
                act.wait_ge(xT_in_psum, 1)
                nc.scalar.copy(net.xT[:, 0, :], net.banks[0][:]).then_inc(xT0_ready, 1)
                act.wait_ge(zeros_ready, 1)
                for m in range(DT_):
                    act.wait_ge(in_in_psum, m + 1)
                    nc.scalar.copy(padded[:, m, :, 3:P + 3],
                                   net.banks[2 + m][:].rearrange("p (b t) -> p b t", b=NB)).then_inc(in_taken, 1)
                for m in range(DT_):
                    act.wait_ge(in_in_psum, DT_ + m + 1)
                    nc.scalar.activation(zs[:, m, :], net.banks[2 + m][:], ACT.Silu).then_inc(in_taken, 1)
                for m in range(DT_):
                    act.wait_ge(conv_ready, m + 1)
                    nc.scalar.activation(u[:, m, :], conv[:, m, :], ACT.Silu,
                                         bias=w["conv_b"][:, m:m + 1]).then_inc(u_ready, 1)
                for m in range(DT_):
                    act.wait_ge(x_in_psum, m + 1)
                    nc.scalar.copy(delta[:, m, :], net.banks[2 + m][:]).then_inc(delta_ready, 1)
                for m in range(DT_):
                    act.wait_ge(dt_in_psum, m + 1)
                    chain(nc.scalar.activation(ex[:, m, :], net.banks[2 + m][:], ACT.Abs,
                                               bias=w["dt_b"][:, m:m + 1]))
                    nc.scalar.activation(ex[:, m, :], ex[:, m, :], ACT.Exp, scale=-1.0).then_inc(exp_ready, 1)
                act.wait_ge(one_ready, 1)
                nc.scalar.activation(dt[:], one_ex, ACT.Ln).then_inc(log_ready, 1)
                act.wait_ge(dt_ready, 1)
                act.wait_ge(a_ready, 1)
                for s in range(STATES):
                    if s >= 2:
                        act.wait_ge(state_ready, s - 1)
                        act.wait_ge(out_ready, s - 1)
                    for m in range(DT_):
                        nc.scalar.activation(decay[s % 2][:, m, :], dt[:, m, :], ACT.Exp,
                                             scale=a[:, m * STATES + s:m * STATES + s + 1]).then_inc(decay_ready, 1)
                    act.wait_ge(c_in_psum, s + 1)
                    nc.scalar.copy(c_row[s % 2][:], net.banks[6 + s % 2][:]).then_inc(c_ready, 1)
                root_act(act, net, var_ready, rstd_ready)

            @block.vector
            def _(dve):
                chain = Chain(dve, dve_steps)
                tt, ts, stt = nc.vector.tensor_tensor, nc.vector.tensor_scalar, nc.vector.scalar_tensor_tensor
                dve.wait_ge(net.ready["l3_attn"], 16)
                dve.wait_ge(xT_in_psum, 2)
                nc.vector.tensor_copy(net.xT[:, 1, :], net.banks[1][:]).then_inc(xT1_ready, 1)
                for m in range(DT_):
                    dve.wait_ge(in_taken, m + 1)
                    acc = conv[:, m, :].rearrange("p (b t) -> p b t", b=NB)
                    chain(ts(acc, padded[:, m, :, 0:P], conv_w[:, m, 0:1], None, ALU.mult))
                    for k in range(1, TAPS):
                        ins = stt(out=acc, in0=padded[:, m, :, k:k + P], scalar=conv_w[:, m, k:k + 1],
                                  in1=acc, op0=ALU.mult, op1=ALU.add)
                        if k < TAPS - 1:
                            chain(ins)
                    ins.then_inc(conv_ready, 1)
                dve.wait_ge(x_in_psum, DT_ + 1)
                nc.vector.tensor_copy(bc[:], net.banks[6][0:2 * STATES, :]).then_inc(bc_ready, 1)
                for m in range(DT_):
                    dve.wait_ge(dt_in_psum, m + 1)
                    dve.wait_ge(exp_ready, m + 1)
                    ts(positive[:, m, :], net.banks[2 + m][:], w["dt_b"][:, m:m + 1], 0.0, ALU.add,
                       ALU.max).then_inc(positive_ready, 1)
                dve.wait_ge(log_ready, 1)
                dve.wait_ge(positive_ready, DT_)
                dve.wait_ge(lost_ready, 1)
                chain(tt(dt[:], dt[:], positive, ALU.add))
                chain(tt(dt[:], dt[:], lost, ALU.subtract))
                nc.vector.engine_nop().then_inc(dt_ready, 1)
                chain(tt(dtu[:], dt[:], u[:], ALU.mult))
                for s in range(STATES):
                    dve.wait_ge(b_in_psum, s + 1)
                    if s >= 2:
                        dve.wait_ge(state_ready, s - 1)
                    tt(drive[s % 2], dtu[:],
                       net.banks[4 + s % 2][:].unsqueeze(1).broadcast_to([P, DT_, T]),
                       ALU.mult).then_inc(drive_ready, 1)
                    dve.wait_ge(decay_ready, DT_ * (s + 1))
                    chain(nc.vector.memset(decay[s % 2].rearrange("p m (b t) -> p (m b) t", b=NB)[:, :, 0],
                                           0.0))
                    dve.wait_ge(drive_ready, s + 1)
                    if s >= 2:
                        dve.wait_ge(out_ready, s - 1)
                    nc.vector.tensor_tensor_scan(state[s % 2].rearrange("p m t -> p (m t)"),
                                                 decay[s % 2].rearrange("p m t -> p (m t)"),
                                                 drive[s % 2].rearrange("p m t -> p (m t)"),
                                                 0.0, ALU.mult, ALU.add).then_inc(state_ready, 1)
                dve.wait_ge(summed, STATES)
                for m in range(DT_):
                    chain(stt(out=u[:, m, :], in0=u[:, m, :], scalar=w["d"][:, m:m + 1],
                              in1=net.banks[m][:], op0=ALU.mult, op1=ALU.add))
                    tt(dtu[:, m, :], u[:, m, :], zs[:, m, :], ALU.mult).then_inc(yz_ready, 1)
                residual_norm_dve(dve, net, chain, net.x, lambda b: half(net, (4, 5), b), y_ready,
                                  PAIR_DONE, var_ready, rstd_ready)

            @block.gpsimd
            def _(pool):
                nc.gpsimd.memset(padded, 0.0).then_inc(zeros_ready, 1)
                pool.wait_ge(exp_ready, DT_)
                nc.gpsimd.tensor_scalar(one_ex, ex, 1.0, None, ALU.add).then_inc(one_ready, 1)
                pool.wait_ge(one_ready, 1)
                nc.gpsimd.tensor_scalar(lost, one_ex, -1.0, None, ALU.add).then_inc(one_ready, 1)
                pool.wait_ge(one_ready, 2)
                nc.gpsimd.tensor_tensor(lost, lost, ex, ALU.subtract).then_inc(lost_ready, 1)
                for s in range(STATES):
                    pool.wait_ge(state_ready, s + 1)
                    pool.wait_ge(c_ready, s + 1)
                    if s >= 2:
                        pool.wait_ge(summed, s - 1)
                    nc.gpsimd.tensor_tensor(out[s % 2], state[s % 2],
                                            c_row[s % 2][:].unsqueeze(1).broadcast_to([P, DT_, T]),
                                            ALU.mult).then_inc(out_ready, 1)
    net.end_sublayer()



def l3_xattn(net, prefetch):
    nc = net.nc
    net.stage = "l3_xattn"
    with ExitStack() as sub:
        kv = net.scratch(sub)("kv", [P, NB, FT, D])
        (xT_in_psum, xT0_ready, xT1_ready, kv_in_psum, kv_ready, y_ready, var_ready, rstd_ready,
         dve_steps) = net.signals(9)
        with nc.Block() as block:
            @block.sync
            def _(sp):
                prefetch(sp)

            @block.tensor
            def _(pe):
                for b in range(NB):
                    for m in range(FT):
                        mm = pe.matmul(net.banks[2 + b][:, m * D:(m + 1) * D], net.ctx[:, b, m * P:(m + 1) * P],
                                       net.ctx[:, b, :], start=True, stop=True)
                    mm.then_inc(kv_in_psum, 1)
                transposes(pe, net, net.x, (0, 1), xT_in_psum)
                pe.wait_ge(xT0_ready, 1)
                pe.wait_ge(xT1_ready, 1)
                for b in range(NB):
                    pe.wait_ge(kv_ready, b + 1)
                    project_tokens(pe, half(net, (6, 7), b), net.xT, b, kv[:, b, :, :]).then_inc(y_ready, 1)

            @block.scalar
            def _(act):
                for b in range(NB):
                    act.wait_ge(kv_in_psum, b + 1)
                    nc.scalar.activation(kv[:, b, :, :].rearrange("p f d -> p (f d)"), net.banks[2 + b][:],
                                         ACT.Copy, scale=1.0 / P).then_inc(kv_ready, 1)
                act.wait_ge(xT_in_psum, 1)
                nc.scalar.copy(net.xT[:, 0, :], net.banks[0][:]).then_inc(xT0_ready, 1)
                root_act(act, net, var_ready, rstd_ready)

            @block.vector
            def _(dve):
                chain = Chain(dve, dve_steps)
                dve.wait_ge(xT_in_psum, 2)
                nc.vector.tensor_copy(net.xT[:, 1, :], net.banks[1][:]).then_inc(xT1_ready, 1)
                residual_norm_dve(dve, net, chain, net.x, lambda b: half(net, (6, 7), b), y_ready,
                                  PAIR_DONE, var_ready, rstd_ready)
    net.end_sublayer()



BITS = 4 * 1024 + 8 * 1024 + 8 * D
BITS_AT = (2 * 1024 + 8 * 1024 + 8 * D)


def load_bits(net, sp):
    room = net.e_room[:, BITS_AT:BITS_AT + BITS // 4].bitcast(I32)
    sp.dma_start(room, net.params["l3_ffn_bits"]).then_inc(net.expert_ready[0], 16)


def l3_ffn(net, prefetch):
    nc = net.nc
    w = net.weights("l3_ffn")
    with ExitStack() as sub:
        sb = net.scratch(sub)
        scale = sb("scales", [P, 2])
        h0, h1 = sb("hidden0", [P, 8, T]), sb("hidden1", [P, 8, T])
        room = net.e_room
        w0 = tiles(room[:, 0:2048], 2)
        w1 = tiles(room[:, 2048:2048 + 8192], 8)
        w2 = tiles(room[:, 2048 + 8192:BITS_AT], 8)
        bits = room[:, BITS_AT:BITS_AT + BITS // 4].bitcast(U8)
        k0, k1, k2 = tiles(bits[:, 0:4096], 4), tiles(bits[:, 4096:4096 + 8192], 8), tiles(bits[:, 4096 + 8192:BITS], 8)
        (xT_in_psum, xT0_ready, xT1_ready, w0_ready, w1_ready, w2_ready, scale_ready, h0_in_psum,
         h0_ready, h1_in_psum, h1_ready, y_ready, var_ready, rstd_ready, dve_steps) = net.signals(15)
        loads = 16 * (1 + sum(s in EXPERT_NETS for s in LAST_LOOP if s in RUN))
        with nc.Block() as block:
            @block.sync
            def _(sp):
                prefetch(sp)

            @block.tensor
            def _(pe):
                transposes(pe, net, net.x, (0, 1), xT_in_psum)
                pe.wait_ge(xT0_ready, 1)
                pe.wait_ge(xT1_ready, 1)
                pe.wait_ge(w0_ready, 1)
                for m in range(8):
                    if m >= 4:
                        pe.wait_ge(h0_ready, m - 3)
                    project(pe, net.banks[2 + m % 4][:], w0, net.xT, m).then_inc(h0_in_psum, 1)
                pe.wait_ge(h0_ready, 8)
                pe.wait_ge(w1_ready, 8)
                for m in range(8):
                    if m >= 4:
                        pe.wait_ge(h1_ready, m - 3)
                    project(pe, net.banks[2 + m % 4][:], w1, h0, m).then_inc(h1_in_psum, 1)
                pe.wait_ge(h1_ready, 8)
                pe.wait_ge(w2_ready, 1)
                for b in range(NB):
                    project_tokens(pe, half(net, (6, 7), b), h1, b, w2).then_inc(y_ready, 1)

            @block.scalar
            def _(act):
                act.wait_ge(xT_in_psum, 1)
                nc.scalar.copy(net.xT[:, 0, :], net.banks[0][:]).then_inc(xT0_ready, 1)
                act.wait_ge(scale_ready, 1)
                for m in range(8):
                    act.wait_ge(h0_in_psum, m + 1)
                    nc.scalar.activation(h0[:, m, :], net.banks[2 + m % 4][:], ACT.Relu,
                                         scale=scale[:, 0:1]).then_inc(h0_ready, 1)
                for m in range(8):
                    act.wait_ge(h1_in_psum, m + 1)
                    nc.scalar.activation(h1[:, m, :], net.banks[2 + m % 4][:], ACT.Relu,
                                         scale=scale[:, 1:2]).then_inc(h1_ready, 1)
                root_act(act, net, var_ready, rstd_ready)

            @block.vector
            def _(dve):
                chain = Chain(dve, dve_steps)
                dve.wait_ge(xT_in_psum, 2)
                nc.vector.tensor_copy(net.xT[:, 1, :], net.banks[1][:]).then_inc(xT1_ready, 1)
                dve.wait_ge(net.expert_ready[0], loads)
                nc.vector.tensor_tensor(w0, k0[:, 0:2, :], k0[:, 2:4, :], ALU.subtract).then_inc(w0_ready, 1)
                dve.wait_ge(net.ready["l3_ffn"], 16)
                chain(nc.vector.tensor_scalar(scale[:, 0:1], w["s0"], 4.0, None, ALU.mult))
                nc.vector.tensor_scalar(scale[:, 1:2], w["s1"], 2.0, None, ALU.mult).then_inc(scale_ready, 1)
                for k in range(8):
                    nc.vector.tensor_scalar(w1[:, k, :], k1[:, k, :], 2.0, -1.0, ALU.mult,
                                            ALU.add).then_inc(w1_ready, 1)
                for b in range(NB):
                    dve.wait_ge(y_ready, PAIR_DONE[b])
                    chain.step(nc.vector.scalar_tensor_tensor(
                        out=net.r[:, b, :], in0=half(net, (6, 7), b), scalar=w["s2"], in1=net.x[:, b, :],
                        op0=ALU.mult, op1=ALU.add))
                chain.settle()
                finish_norm_dve(dve, net, chain, var_ready, rstd_ready)

            @block.gpsimd
            def _(pool):
                pool.wait_ge(net.expert_ready[0], loads)
                nc.gpsimd.tensor_scalar(w2, k2, 2.0, -1.0, ALU.mult, ALU.add).then_inc(w2_ready, 1)
    net.end_sublayer()


EXPERT_COLS = {"l0_ffn_experts": 2048, "l1_ffn": 4096, "l2_ffn": 1024}
EXPERT_NETS = tuple(EXPERT_COLS)
EXPERT_LOADS = {s: load_experts(s) for s in EXPERT_NETS}
EXPERT_LOADS["l3_ffn"] = load_bits
EXPERT_ROOM = 16384
BODIES = {"l0_attn": l0_attn, "l0_xattn": l0_xattn, "l0_ffn_attention": l0_ffn_attention,
          "l0_ffn_experts": l0_ffn_experts,
          "l1_attn": l1_attn, "l1_xattn": l1_xattn, "l1_ffn": l1_ffn,
          "l2_attn": l2_attn, "l2_xattn": l2_xattn, "l2_ffn": l2_ffn,
          "l3_attn": l3_attn, "l3_xattn": l3_xattn, "l3_ffn": l3_ffn}
RUN = list(BODIES)


def expert_parameters(i):
    import numpy as np

    def blocks(w1, w2):
        return np.concatenate([p for e in range(EXPERTS) for p in (rows(w1[e]), rows(w2[e]))], axis=1)

    bits = [rows(i[f"L3_ffn_k{k}"].view(np.uint8)) for k in range(3)]
    return {"l3_ffn_bits": np.concatenate(bits, axis=1).view(np.int32),
            "l0_ffn_experts_experts": blocks(i["L0_ffn_w1"], i["L0_ffn_w2"]),
            "l1_ffn_experts": blocks(i["L1_ffn_W1"], i["L1_ffn_W2"]),
            "l2_ffn_experts": blocks(i["L2_ffn_ew1"], i["L2_ffn_ew2"])}



SUBLAYERS = ["l0_attn", "l0_xattn", "l0_ffn_attention", "l0_ffn_experts", "l1_attn", "l1_xattn", "l1_ffn",
             "l2_attn", "l2_xattn", "l2_ffn", "l3_attn", "l3_xattn", "l3_ffn"]
LOOPS = [SUBLAYERS[:2], SUBLAYERS[2:4], SUBLAYERS[4:]]
LAST_LOOP = LOOPS[2]
ACROSS = ("l0_ffn_attention", "l0_ffn_experts")
GROUPS = 4


def decoder(nc, x, ctx, out, params, cols, consts):
    with ExitStack() as cx:
        net = Net(nc, cx, params, cols, consts)
        io_done = cx.enter_context(nc.semaphore("io_done"))
        constants_ready = cx.enter_context(nc.semaphore("constants_ready"))
        ctxT_in_psum = cx.enter_context(nc.semaphore("ctxT_in_psum"))
        ctxT_ready = cx.enter_context(nc.semaphore("ctxT_ready"))
        net.ready = {s: cx.enter_context(nc.semaphore(f"{s}_weights_ready")) for s in SUBLAYERS}
        net.expert_ready = [cx.enter_context(nc.semaphore(f"expert{e}_weights_ready"))
                            for e in range(EXPERTS)]
        net.out_stored = cx.enter_context(nc.semaphore("out_stored"))
        between = [nc.dram_tensor(f"stream{i}", x.shape, F32).ap() for i in range(2)]

        def load_weights(sp, sub):
            n = sum(c for _, c in cols.get(sub, []))
            if not n:
                return
            room = net.w_room[SUBLAYERS.index(sub) % 2]
            sp.dma_start(room[:, 0:n], params[sub]).then_inc(net.ready[sub], 16)

        with nc.Block() as block:
            @block.sync
            def _(sp):
                for name, dst in (("ident", net.ident), ("identb", net.identb),
                                  ("mates_qk", net.mates_qk), ("mates_kq", net.mates_kq),
                                  ("keep_kq", net.keep_kq), ("before", net.before),
                                  ("causal_qk", net.causal_qk), ("causal_kq", net.causal_kq),
                                  ("inside", net.inside)):
                    sp.dma_start(dst[:].rearrange("p a k -> p (a k)") if len(dst.shape) == 3 else dst[:],
                                 consts[name]).then_inc(constants_ready, 16)
                sp.wait_ge(constants_ready, 16 * 9)

            @block.gpsimd
            def _(pool):
                for buf in net.negmax:
                    nc.gpsimd.memset(buf[:], 0.0)
                nc.gpsimd.memset(net.v1[:], 1.0)

        loops = [names for names in ([n for n in part if n in RUN] for part in LOOPS) if names]
        for k, names in enumerate(loops):
            src = x if k == 0 else between[k - 1]
            dst = out if k == len(loops) - 1 else between[k]
            group_loop(net, names, src, dst, ctx, load_weights, io_done, ctxT_in_psum, ctxT_ready)


def group_loop(net, names, src, dst, ctx, load_weights, io_done, ctxT_in_psum, ctxT_ready):
    nc = net.nc
    across = names[0] in ACROSS
    ctx_g = ctx.rearrange("(g b) t d -> g t b d", b=NB)

    def group_views(a, g):
        if across:
            v = a.rearrange("s (g b p) d -> g b p s d", b=NB, p=P // SEQUENCES)[g]
        else:
            v = a.rearrange("(g b) t d -> g b t d", b=NB)[g]
        return [v[b] for b in range(NB)]

    with nc.Fori(0, GROUPS) as g:
        with nc.Block() as block:
            @block.sync
            def _(sp):
                if not across:
                    sp.dma_start(net.ctx[:], ctx_g[g]).then_inc(io_done, 16)
                for b, view in enumerate(group_views(src, g)):
                    sp.dma_start(net.x[:, b, :], view).then_inc(io_done, 16)
                load_weights(sp, names[0])
                if names[0] in EXPERT_LOADS:
                    EXPERT_LOADS[names[0]](net, sp)
                sp.wait_ge(io_done, 16 * (NB + (not across)))

            @block.tensor
            def _(pe):
                if not across:
                    pe.wait_ge(io_done, 16 * (NB + 1))
                    transposes(pe, net, net.ctx, (0, 1), ctxT_in_psum)

            @block.scalar
            def _(act):
                if not across:
                    act.wait_ge(ctxT_in_psum, 1)
                    nc.scalar.copy(net.ctxT[:, 0, :], net.banks[0][:]).then_inc(ctxT_ready, 1)

            @block.vector
            def _(dve):
                if not across:
                    dve.wait_ge(ctxT_in_psum, 2)
                    nc.vector.tensor_copy(net.ctxT[:, 1, :], net.banks[1][:]).then_inc(ctxT_ready, 1)

        for i, name in enumerate(names):
            def prefetch(sp, i=i):
                if i + 1 < len(names):
                    load_weights(sp, names[i + 1])
                    if names[i + 1] in EXPERT_LOADS:
                        EXPERT_LOADS[names[i + 1]](net, sp)
            BODIES[name](net, prefetch)

        with nc.Block() as block:
            @block.sync
            def _(sp):
                for b, view in enumerate(group_views(dst, g)):
                    sp.dma_start(view, net.x[:, b, :]).then_inc(net.out_stored, 16)
                sp.wait_ge(net.out_stored, 16 * NB)
        nums = [s.num for s in [io_done, ctxT_in_psum, ctxT_ready, net.out_stored,
                                *net.ready.values(), *net.expert_ready]]
        nc.all_engine_barrier(sems_to_clear=range(min(nums), max(nums) + 1))



def rows(a):
    import numpy as np
    k, n = a.shape
    return np.ascontiguousarray(a.reshape(k // P, P, n).transpose(1, 0, 2)).reshape(P, -1)


def spread(v):
    import numpy as np
    v = np.asarray(v).reshape(1, -1)
    return np.broadcast_to(v, (P, v.shape[1]))


def column(v):
    return v.reshape(-1, P).T


def slots(a, row=0.0):
    import numpy as np
    out = np.zeros((*a.shape[:-1], NH, SLOT), a.dtype)
    out[..., 0:DH] = a.reshape(*a.shape[:-1], NH, DH)
    out[..., SHIFT_ROW] = row
    return out.reshape(*a.shape[:-1], NH * SLOT)


def parameters(i):
    import numpy as np
    proj = np.zeros((8, P, P), np.float32)
    for h in range(NH):
        at = (h % 8) * DH
        proj[h // 2, at:at + DH, (h % 2) * 64:(h % 2) * 64 + 64] = i["L0_attn_proj"][h]
    out = {
        "l0_attn": [
            ("wqk", rows(i["L0_attn_qkv_w"][:, :2 * D])), ("wv", rows(i["L0_attn_qkv_w"][:, 2 * D:])),
            ("wo", rows(i["L0_attn_out_w"])), ("bqk", column(i["L0_attn_qkv_b"][:2 * D])),
            ("bv", spread(i["L0_attn_qkv_b"][2 * D:])), ("bo", spread(i["L0_attn_out_b"])),
            ("proj", proj.transpose(1, 0, 2).reshape(P, -1))],
        "l0_xattn": [
            ("wq", rows(slots(i["L0_xattn_Wq"].T))), ("wk", rows(slots(i["L0_xattn_Wk"].T))),
            ("wv", rows(i["L0_xattn_Wv"].T)),
            ("one_rows", column(slots(np.zeros(D, np.float32), 1.0)))],
    }
    i0 = {k[len("L0_ffn_"):]: v for k, v in i.items() if k.startswith("L0_ffn_")}
    w0, b0 = i0["in_proj_w"], i0["in_proj_b"]
    out["l0_ffn_attention"] = [
        ("wq", rows(slots(w0[:D].T))), ("wk", rows(slots(w0[D:2 * D].T))), ("wv", rows(w0[2 * D:].T)),
        ("wo", rows(i0["out_proj_w"].T)), ("bq", column(slots(b0[:D]))), ("bk", column(slots(b0[D:2 * D], 1.0))),
        ("bv", spread(b0[2 * D:])), ("bo", spread(i0["out_proj_b"])),
        ("ln1_w", column(i0["ln1_w"])), ("ln1_b", column(i0["ln1_b"])),
        ("ln2_w", column(i0["ln2_w"])), ("ln2_b", column(i0["ln2_b"]))]
    out["l0_ffn_experts"] = [("router", rows(i0["router_w"].T))]
    order = [0, 2, 1, 3]
    wq = i["L1_attn_Wq"].reshape(D, Q_HEADS, HD)[:, order].reshape(D, D)
    out["l1_attn"] = [
        ("wq", rows(wq)), ("wkv", rows(np.concatenate([i["L1_attn_Wk"], i["L1_attn_Wv"]], axis=1))),
        ("wo", rows(i["L1_attn_Wo"])), ("norm_w", column(i["L1_attn_norm_w"])),
        ("gate", spread(i["L1_attn_gate"])), ("log_temperature", spread(i["L1_attn_log_temperature"]))]
    out["l1_xattn"] = [("w", column(i["L1_xattn_w"].reshape(-1))), ("u", column(i["L1_xattn_u"].reshape(-1)))]
    out["l1_ffn"] = [
        ("wr", spread(i["L1_ffn_wr"])), ("br", spread(i["L1_ffn_br"])),
        ("b1", column(i["L1_ffn_b1"].reshape(-1))), ("b2", spread(i["L1_ffn_b2"].reshape(-1)))]
    i2 = {k[len("L2_attn_"):]: v for k, v in i.items() if k.startswith("L2_attn_")}

    def down(a):
        full = np.zeros((P, a.shape[1]), np.float32)
        full[:a.shape[0]] = a
        return full

    channel = np.repeat(np.arange(CONV), NB)
    sequence = np.tile(np.arange(NB), CONV)
    groups = (sequence[:, None] == sequence) & (channel[:, None] // 2 == channel // 2)
    out["l2_attn"] = [
        ("wqk", rows(i2["qkv_w"][:, :2 * D])), ("wv", rows(i2["qkv_w"][:, 2 * D:])),
        ("wo", rows(i2["proj_w"])), ("bo", spread(i2["proj_b"])), ("c1", spread(i2["c1"])),
        ("c2", spread(i2["c2"])), ("conv2_b", spread(i2["conv2_b"])), ("ch_w1", rows(i2["ch_w1"])),
        ("ch_w2", down(i2["ch_w2"])), ("ch_b1", down(i2["ch_b1"].reshape(-1, 1))),
        ("ch_b2", column(i2["ch_b2"])), ("groups", down(groups.astype(np.float32))),
        ("channels", down((sequence[:, None] == np.arange(NB)).astype(np.float32))),
        ("conv1", down(i2["conv1_w"].reshape(CONV, 3)[channel])),
        ("conv2", down(i2["conv2_w"].reshape(CONV, 3)[channel])),
        ("gn_g", down(i2["gn_g"][channel].reshape(-1, 1))), ("gn_b", down(i2["gn_b"][channel].reshape(-1, 1)))]
    out["l2_xattn"] = [
        ("wq", rows(slots(i["L2_xattn_Wq"]))), ("wk", rows(slots(i["L2_xattn_Wk"]))),
        ("wv", rows(i["L2_xattn_Wv"])), ("wo", rows(i["L2_xattn_Wo"])),
        ("bq", column(slots(i["L2_xattn_bq"]))), ("bk", column(slots(i["L2_xattn_bk"], 1.0))),
        ("bv", spread(i["L2_xattn_bv"])), ("bo", spread(i["L2_xattn_bo"]))]
    out["l2_ffn"] = [
        ("router", rows(i["L2_ffn_router_w"].T)), ("router_bias", spread(i["L2_ffn_router_bias"])),
        ("sw1", rows(i["L2_ffn_sw1"])), ("sw3", rows(i["L2_ffn_sw3"])), ("sw2", rows(i["L2_ffn_sw2"]))]
    i3 = {k[len("L3_attn_"):]: v for k, v in i.items() if k.startswith("L3_attn_")}

    def by_tile(a):
        return a.reshape(-1, P, a.shape[1]).transpose(1, 0, 2).reshape(P, -1)

    out["l3_attn"] = [
        ("w_in", rows(i3["in_proj_w"].T)), ("w_x", rows(i3["x_proj_w"].T)), ("w_dt", rows(i3["dt_proj_w"].T)),
        ("w_out", rows(i3["out_proj_w"].T)), ("conv_w", by_tile(i3["conv_w"][:, 0, :])),
        ("conv_b", column(i3["conv_b"])), ("dt_b", column(i3["dt_proj_b"])),
        ("a_log", by_tile(i3["A_log"])), ("d", column(i3["D"]))]
    out["l3_ffn"] = [(s, spread(i["L3_ffn_" + s])) for s in ("s0", "s1", "s2")]
    return out


def kernel(**inputs):
    import ml_dtypes
    import numpy as np
    import concourse.bacc as bacc
    from concourse.bass_utils import run_bass_kernel_spmd

    inputs = {k: np.asarray(v) for k, v in inputs.items()}
    nc = bacc.Bacc("TRN2", target_bir_lowering=False, num_devices=1)
    arrays = {}

    def dram(name, a):
        a = np.ascontiguousarray(a)
        arrays[name] = a
        return nc.dram_tensor(name, a.shape, mybir.dt.from_np(a.dtype), kind="ExternalInput").ap()

    pieces = parameters(inputs)
    experts = expert_parameters(inputs)
    cols = {s: [(n, a.shape[1]) for n, a in p] for s, p in pieces.items()}
    cols["room"] = [sum(c for _, c in cols[s]) for s in pieces]
    cols["expert_room"] = EXPERT_ROOM
    params = {s: dram(s, np.concatenate([a for _, a in p], axis=1)) for s, p in pieces.items()}
    params.update({s: dram(s, a) for s, a in experts.items()})
    key, query = np.arange(P)[:, None], np.arange(P)[None, :]
    later = np.where(key <= query, 0.0, -BIG)
    mates = (key <= query) & (key // SEQUENCES == query // SEQUENCES)
    below = np.where(mates, 0.0, -BIG)
    consts = {n: dram(n, a) for n, a in {
        "ident": np.eye(P, dtype=np.float32), "identb": np.eye(P).astype(ml_dtypes.bfloat16),
        "mates_qk": np.tile(below.T, 4).astype(ml_dtypes.bfloat16),
        "mates_kq": np.tile(below, 4).astype(ml_dtypes.bfloat16),
        "causal_qk": np.tile(later.T, 4).astype(ml_dtypes.bfloat16),
        "causal_kq": np.tile(later, 4).astype(ml_dtypes.bfloat16),
        "inside": np.tile(np.pad(np.ones(P, np.float32), 1), (P, NB)),
        "before": np.tile(np.tril(np.ones((EXPERTS, EXPERTS), np.float32), -1).reshape(1, -1), (P, 1)),
        "keep_kq": (key <= query).astype(np.float32)}.items()}
    x, ctx = dram("x", inputs["x"]), dram("ctx", inputs["ctx_1024"])
    out = nc.dram_tensor("out", inputs["x"].shape, F32, kind="ExternalOutput").ap()
    decoder(nc, x, ctx, out, params, cols, consts)
    r = run_bass_kernel_spmd(nc, [arrays], core_ids=[0])
    return r.results[0]["out"]
```

```python
from contextlib import ExitStack

import concourse.bass as bass
from concourse import mybir

F32 = mybir.dt.float32
BF16 = mybir.dt.bfloat16
I32 = mybir.dt.int32
U8 = mybir.dt.uint8
ALU = mybir.AluOpType
ACT = mybir.ActivationFunctionType
AX_X = mybir.AxisListType.X

P = 128
NB = 4
D = 256
FT = D // P
T = NB * P
NH, DH = 16, 16
SLOT = 32
SHIFT_ROW = 16
EPS = 1e-5
BIG = float(2.0 ** 100)
EXPERTS = 8
SEQUENCES = 16
PAIR_DONE = [2, 2, 4, 4]


class Chain:

    def __init__(self, eng, sem):
        self.eng, self.sem, self.n = eng, sem, 0

    def step(self, ins):
        self.n += 1
        ins.then_inc(self.sem, 1)

    def settle(self):
        self.eng.wait_ge(self.sem, self.n)

    def __call__(self, ins):
        self.step(ins)
        self.settle()


class Net:

    def __init__(self, nc, cx, params, cols, consts):
        self.nc, self.cx, self.params, self.cols = nc, cx, params, cols

        def sb(name, shape, dt=F32):
            return cx.enter_context(nc.sbuf_tensor(name, shape, dt))

        self.x = sb("x_tokens", [P, NB, D])
        self.xT = sb("x_features", [P, FT, T])
        self.ctx = sb("ctx_tokens", [P, NB, D])
        self.ctxT = sb("ctx_features", [P, FT, T])
        self.r = sb("residual_sum", [P, NB, D])
        self.stats = sb("ln_stats", [P, NB, 6])
        self.mv = sb("ln_mean_var", [P, NB, 2])
        self.var = sb("ln_var_eps", [P, NB])
        self.rvar = sb("ln_inverse_var", [P, NB])
        self.rstd = sb("ln_rstd", [P, NB])
        self.spare = sb("table_load_output", [P, 8])
        self.table_loads = 0
        self.turn_next = False
        self.ident = sb("identity", [P, P])
        self.identb = sb("identity_bf16", [P, P], BF16)
        self.mates_qk = sb("mates_bias_qk", [P, 4, P], BF16)
        self.mates_kq = sb("mates_bias_kq", [P, 4, P], BF16)
        self.keep_kq = sb("causal_keep_kq", [P, P])
        self.causal_qk = sb("causal_bias_qk", [P, 4, P], BF16)
        self.causal_kq = sb("causal_bias_kq", [P, 4, P], BF16)
        self.inside = sb("inside_places", [P, NB * (P + 2)])
        self.before = sb("earlier_expert", [P, EXPERTS * EXPERTS])
        self.negmax = [sb(f"negmax_slots{i}", [P, NH, SLOT]) for i in range(2)]
        self.v1 = sb("values_and_one", [P, NB, NH, DH + 1])
        self.w_room = [sb(f"weights{i}", [P, max(cols["room"])]) for i in range(2)]
        self.e_room = sb("expert_weights", [P, cols["expert_room"]])
        self.banks = [cx.enter_context(nc.psum_tensor(f"bank{i}", [P, 512], F32)) for i in range(8)]
        self.pool = [cx.enter_context(nc.semaphore(f"signal{i}")) for i in range(40)]
        self.consts = consts

    def scratch(self, sub):
        return lambda name, shape, dt=F32: sub.enter_context(
            self.nc.sbuf_tensor(f"{self.stage}_{name}", shape, dt))

    def signals(self, n):
        assert n <= len(self.pool)
        return self.pool[:n]

    def end_sublayer(self):
        nums = [s.num for s in self.pool]
        self.nc.all_engine_barrier(sems_to_clear=range(min(nums), max(nums) + 1))

    def weights(self, sub):
        self.stage = sub
        at, out = 0, {}
        for name, n in self.cols[sub]:
            out[name] = self.w_room[SUBLAYERS.index(sub) % 2][:, at:at + n]
            at += n
        return out


def tiles(ap, k):
    return ap.rearrange("p (k n) -> p k n", k=k)


def seq(b):
    return slice(b * P, (b + 1) * P)



def transposes(pe, net, src, banks, done, src_ready=None):
    for b in range(NB):
        if src_ready is not None:
            pe.wait_ge(src_ready, b + 1)
        for f in range(FT):
            mm = pe.transpose(net.banks[banks[f]][:, seq(b)], src[:, b, f * P:(f + 1) * P], net.ident[:])
            if b == NB - 1:
                mm.then_inc(done, 1)


def project(pe, out, w, src, m, start=True, stop=True):
    k = w.shape[1]
    for f in range(k):
        mm = pe.matmul(out, w[:, f, m * P:(m + 1) * P], src[:, f, :], start=start and f == 0,
                       stop=stop and f == k - 1)
    return mm


def project_tokens(pe, out, srcT, b, w, start=True, stop=True):
    k = w.shape[1]
    for f in range(k):
        mm = pe.matmul(out, srcT[:, f, seq(b)], w[:, f, :], start=start and f == 0,
                       stop=stop and f == k - 1)
    return mm


def half(net, banks, b):
    return net.banks[banks[b // 2]][:, (b % 2) * D:(b % 2 + 1) * D]


class Finish:

    def __init__(self, net, signals, banks=(0, 1)):
        self.net, self.banks = net, banks
        self.var_ready, self.rstd_ready, self.x_ready, self.xT_in_psum = signals

    def run_dve(self, dve, chain, add):
        net, nc = self.net, self.net.nc
        for b in range(NB):
            chain(add(b))
            chain.step(nc.vector.bn_stats(net.stats[:, b, :], net.r[:, b, :]))
        chain.settle()
        aggregate_dve(net, chain)
        nc.vector.reciprocal(net.rvar[:], net.var[:]).then_inc(self.var_ready, 1)
        dve.wait_ge(self.rstd_ready, 1)
        for b in range(NB):
            nc.vector.tensor_scalar(net.x[:, b, :], net.r[:, b, :], net.mv[:, b, 0:1],
                                    net.rstd[:, b:b + 1], ALU.subtract, ALU.mult).then_inc(self.x_ready, 1)
        if net.turn_next:
            dve.wait_ge(self.xT_in_psum, 2)
            nc.vector.tensor_copy(net.xT[:, 1, :], net.banks[self.banks[1]][:])

    def run_act(self, act):
        net, nc = self.net, self.net.nc
        load_table(net, ACT.Sqrt)
        act.wait_ge(self.var_ready, 1)
        nc.scalar.activation(net.rstd[:], net.rvar[:], ACT.Sqrt).then_inc(self.rstd_ready, 1)
        if net.turn_next:
            act.wait_ge(self.xT_in_psum, 1)
            nc.scalar.copy(net.xT[:, 0, :], net.banks[self.banks[0]][:])

    def run_pe(self, pe):
        net = self.net
        if net.turn_next:
            transposes(pe, net, net.x, self.banks, self.xT_in_psum, self.x_ready)


def load_table(net, func):
    net.table_loads += 1
    at = net.table_loads % 8
    net.nc.scalar.activation(net.spare[:, at:at + 1], net.ident[:, 0:1], func)


def aggregate_dve(net, chain):
    nc = net.nc
    for b in range(NB):
        chain.step(nc.vector.bn_aggr(net.mv[:, b, :], net.stats[:, b, :]))
    chain.settle()
    chain(nc.vector.tensor_scalar(net.var[:], net.mv[:, :, 1], EPS, None, ALU.add))



class Heads16:

    SCORES, SHIFTED, MAXT, CONTEXT = (0, 1), (2, 3), 4, (5, 6)

    def __init__(self, net, sub, signals, masked, scale):
        self.net, self.masked, self.scale = net, masked, scale
        (self.scores_ready, self.max_ready, self.negmax_ready, self.negmaxT_ready,
         self.shift_ready, self.shifted_ready, self.exp_ready, self.sums_ready,
         self.context_ready) = signals
        nc = net.nc

        sb = net.scratch(sub)

        self.qT = sb("q_slots", [P, 4, T])
        self.kT = sb("k_slots", [P, 4, T])
        self.probs = [sb(f"probs{i}", [P, 4, 4, P]) for i in range(2)]
        self.mx = [sb(f"score_max{i}", [P, 4, 4]) for i in range(2)]
        self.rec = [sb(f"inverse_sum{i}", [P, NH]) for i in range(2)]
        self.context = sb("context", [P, NB, D])

    def run_pe(self, pe):
        net = self.net

        def four_tiles(out_banks, lhs, rhs, b, u, mask, done):
            if self.masked:
                for s in range(2):
                    pe.matmul(net.banks[out_banks[s]][:], net.identb[:],
                              mask[:].rearrange("p a k -> p (a k)"), start=True, stop=True)
            for t in range(4):
                for s in range(2):
                    at = SLOT * (2 * u + s)
                    mm = pe.matmul(net.banks[out_banks[s]][:, seq(t)], lhs[at:at + SLOT, t, seq(b)],
                                   rhs[at:at + SLOT, t, seq(b)], start=not self.masked, stop=True,
                                   skip_group_check=True, tile_position=(at, 0))
                    if t == 3:
                        mm.then_inc(done, 1)

        def scores(b, u):
            n = 2 * b + u
            if n:
                pe.wait_ge(self.max_ready, 2 * n)
            four_tiles(self.SCORES, self.qT, self.kT, b, u, net.mates_qk, self.scores_ready)

        def negmax_transposes(b):
            pe.wait_ge(self.negmax_ready, b + 1)
            if b:
                pe.wait_ge(self.shift_ready, b)
            for t in range(4):
                mm = pe.transpose(net.banks[self.MAXT][:, seq(t)],
                                  net.negmax[b % 2][:, 4 * t:4 * t + 4, :].rearrange("p h s -> p (h s)"),
                                  net.ident[:])
            mm.then_inc(self.negmaxT_ready, 1)

        def shifted(b, u):
            n = 2 * b + u
            pe.wait_ge(self.shift_ready, b + 1)
            if n:
                pe.wait_ge(self.exp_ready, 2 * n)
            four_tiles(self.SHIFTED, self.kT, self.qT, b, u, net.mates_kq, self.shifted_ready)

        def context(b):
            pe.wait_ge(self.exp_ready, 4 * (b + 1))
            if b >= 2:
                pe.wait_ge(self.context_ready, b - 1)
            for h in range(NH):
                mm = pe.matmul(net.banks[self.CONTEXT[b % 2]][:, h * (DH + 1):(h + 1) * (DH + 1)],
                               self.probs[b % 2][:, h % 4, h // 4, :], net.v1[:, b, h, :], start=True, stop=True)
            mm.then_inc(self.sums_ready, 1)

        scores(0, 0)
        scores(0, 1)
        for b in range(NB):
            if b + 1 < NB:
                scores(b + 1, 0)
            negmax_transposes(b)
            shifted(b, 0)
            if b + 1 < NB:
                scores(b + 1, 1)
            shifted(b, 1)
            if b:
                context(b - 1)
        context(NB - 1)

    def run_act(self, act):
        for b in range(NB):
            for s in range(4):
                act.wait_ge(self.shifted_ready, 4 * b + s + 1)
                if b >= 2 and s == 0:
                    act.wait_ge(self.sums_ready, b - 1)
                self.net.nc.scalar.activation(
                    self.probs[b % 2][:, s, :, :].rearrange("p t q -> p (t q)"),
                    self.net.banks[self.SHIFTED[s % 2]][:], ACT.Exp,
                    scale=self.scale).then_inc(self.exp_ready, 1)

    def run_dve(self, dve, chain):
        net, nc = self.net, self.net.nc

        def maxima(b, u):
            if u == 0 and b >= 2:
                dve.wait_ge(self.negmax_ready, b - 1)
            for s in (2 * u, 2 * u + 1):
                dve.wait_ge(self.scores_ready, 4 * b + s + 1)
                nc.vector.reduce_max(self.mx[b % 2][:, :, s],
                                     net.banks[self.SCORES[s % 2]][:].rearrange("p (t k) -> p t k", t=4),
                                     AX_X).then_inc(self.max_ready, 1)

        def negate(b):
            dve.wait_ge(self.max_ready, 4 * (b + 1))
            if b >= 2:
                dve.wait_ge(self.negmaxT_ready, b - 1)
            nc.vector.tensor_scalar(net.negmax[b % 2][:, :, SHIFT_ROW],
                                    self.mx[b % 2][:].rearrange("p t s -> p (t s)"), -1.0, None,
                                    ALU.mult).then_inc(self.negmax_ready, 1)

        def shift(b):
            dve.wait_ge(self.negmaxT_ready, b + 1)
            dve.wait_ge(self.scores_ready, 4 * (b + 1))
            nc.vector.tensor_tensor(self.qT[:, :, seq(b)], self.qT[:, :, seq(b)],
                                    net.banks[self.MAXT][:].rearrange("p (t q) -> p t q", t=4),
                                    ALU.add).then_inc(self.shift_ready, 1)

        def normalise(b):
            dve.wait_ge(self.sums_ready, b + 1)
            got = net.banks[self.CONTEXT[b % 2]][:, 0:NH * (DH + 1)].rearrange("p (h d) -> p h d", h=NH)
            chain(nc.vector.reciprocal(self.rec[b % 2][:], got[:, :, DH]))
            nc.vector.tensor_tensor(self.context[:, b, :].rearrange("p (h d) -> p h d", h=NH),
                                    got[:, :, 0:DH],
                                    self.rec[b % 2][:].unsqueeze(2).broadcast_to([P, NH, DH]),
                                    ALU.mult).then_inc(self.context_ready, 1)

        maxima(0, 0)
        maxima(0, 1)
        negate(0)
        for b in range(NB):
            if b + 1 < NB:
                maxima(b + 1, 0)
            shift(b)
            if b + 1 < NB:
                maxima(b + 1, 1)
                negate(b + 1)
            if b:
                normalise(b - 1)
        normalise(NB - 1)



def l0_attn(net, prefetch):
    nc = net.nc
    w = net.weights("l0_attn")
    wqk, wv, wo = tiles(w["wqk"], FT), tiles(w["wv"], FT), tiles(w["wo"], FT)
    proj = tiles(w["proj"], 8)
    with ExitStack() as sub:
        sb = net.scratch(sub)

        qk = sb("qk", [P, 4, T])
        prime = net.e_room[:, 0:16 * T].rearrange("p (t m n) -> p t m n", t=2, m=8)
        scores = [sb(f"scores{i}", [P, 2, 8, P]) for i in range(2)]
        den = sb("denominator", [P, NH])
        context = sb("context", [P, NB, D])
        contextT = sb("contextT", [P, FT, T])
        xb = sb("x_plus_bias", [P, NB, D])
        (qk_in_psum, qk_ready, v_in_psum, v_ready, prime_in_psum,
         qprime_ready, kprime_ready, scores_in_psum, scores_ready, sums_ready, context_ready,
         cT_in_psum, cT0_ready, cT1_ready, y_ready, xb_ready, dve_steps) = net.signals(21)[4:]
        finish = Finish(net, net.signals(4))
        Y = (4, 5, 6, 7)
        with nc.Block() as block:
            @block.sync
            def _(sp):
                prefetch(sp)

            @block.tensor
            def _(pe):
                pe.wait_ge(net.ready["l0_attn"], 16)
                for m in range(4):
                    project(pe, net.banks[2 + m][:], wqk, net.xT, m).then_inc(qk_in_psum, 1)
                for b in range(NB):
                    project_tokens(pe, half(net, (6, 7), b), net.xT, b, wv).then_inc(v_in_psum, 1)
                pe.wait_ge(qk_ready, 4)
                for j in range(16):
                    pair, t = j // 2, j % 2
                    if j >= 4:
                        pe.wait_ge((qprime_ready, kprime_ready)[t], pair - 1)
                    pe.matmul(net.banks[2 + j % 4][:], proj[:, pair, :], qk[:, 2 * t + pair // 4, :],
                              start=True, stop=True).then_inc(prime_in_psum, 1)
                pe.wait_ge(qprime_ready, 8)
                pe.wait_ge(kprime_ready, 8)
                pe.wait_ge(v_ready, NB)

                def score(b):
                    for u in range(2):
                        n = 2 * b + u
                        if n >= 2:
                            pe.wait_ge(scores_ready, 2 * (n - 1))
                        for i in range(4):
                            for j in range(2):
                                rows = slice(64 * j, 64 * j + 64)
                                mm = pe.matmul(net.banks[2 * (n % 2) + j][:, seq(i)],
                                               prime[rows, 1, 4 * u + i, seq(b)],
                                               prime[rows, 0, 4 * u + i, seq(b)], start=True, stop=True,
                                               tile_position=(64 * j, 0))
                                if i == 3:
                                    mm.then_inc(scores_in_psum, 1)

                def context_of(b):
                    pe.wait_ge(scores_ready, 4 * (b + 1))
                    if b >= 2:
                        pe.wait_ge(context_ready, b - 1)
                    for h in range(NH):
                        mm = pe.matmul(net.banks[6 + b % 2][:, h * (DH + 1):(h + 1) * (DH + 1)],
                                       scores[b % 2][:, h % 2, h // 2, :], net.v1[:, b, h, :], start=True, stop=True)
                    mm.then_inc(sums_ready, 1)

                for b in range(NB):
                    score(b)
                    if b:
                        context_of(b - 1)
                context_of(NB - 1)
                transposes(pe, net, context, (2, 3), cT_in_psum, context_ready)
                pe.wait_ge(cT0_ready, 1)
                pe.wait_ge(cT1_ready, 1)
                for b in range(NB):
                    project_tokens(pe, net.banks[Y[b]][:, 0:D], contextT, b, wo).then_inc(y_ready, 1)
                finish.run_pe(pe)

            @block.scalar
            def _(act):
                act.wait_ge(net.ready["l0_attn"], 16)
                for m in range(4):
                    act.wait_ge(qk_in_psum, m + 1)
                    nc.scalar.activation(qk[:, m, :], net.banks[2 + m][:], ACT.Identity,
                                         bias=w["bqk"][:, m:m + 1]).then_inc(qk_ready, 1)
                for pair in range(8):
                    act.wait_ge(prime_in_psum, 2 * pair + 1)
                    nc.scalar.activation(prime[:, 0, pair, :], net.banks[2 + (2 * pair) % 4][:],
                                         ACT.Relu).then_inc(qprime_ready, 1)
                act.wait_ge(cT_in_psum, 1)
                nc.scalar.copy(contextT[:, 0, :], net.banks[2][:]).then_inc(cT0_ready, 1)
                finish.run_act(act)

            @block.vector
            def _(dve):
                chain = Chain(dve, dve_steps)
                dve.wait_ge(net.ready["l0_attn"], 16)
                for b in range(NB):
                    dve.wait_ge(v_in_psum, PAIR_DONE[b])
                    nc.vector.tensor_tensor(net.v1[:, b, :, 0:DH],
                                            half(net, (6, 7), b).rearrange("p (h d) -> p h d", h=NH),
                                            w["bv"].rearrange("p (h d) -> p h d", h=NH),
                                            ALU.add).then_inc(v_ready, 1)
                for pair in range(8):
                    dve.wait_ge(prime_in_psum, 2 * pair + 2)
                    nc.vector.tensor_scalar(prime[:, 1, pair, :], net.banks[2 + (2 * pair + 1) % 4][:], 0.0,
                                            None, ALU.max).then_inc(kprime_ready, 1)

                def mask(b):
                    if b >= 2:
                        dve.wait_ge(sums_ready, b - 1)
                    for n in (2 * b, 2 * b + 1):
                        for j in range(2):
                            dve.wait_ge(scores_in_psum, 2 * n + j + 1)
                            pairs = slice(4 * (n % 2), 4 * (n % 2) + 4)
                            nc.vector.tensor_tensor(scores[b % 2][:, j, pairs, :],
                                                    net.banks[2 * (n % 2) + j][:].rearrange(
                                                        "p (h q) -> p h q", h=4),
                                                    net.keep_kq[:].unsqueeze(1).broadcast_to([P, 4, P]),
                                                    ALU.mult).then_inc(scores_ready, 1)

                def divide(b):
                    dve.wait_ge(sums_ready, b + 1)
                    got = net.banks[6 + b % 2][:, 0:NH * (DH + 1)].rearrange("p (h d) -> p h d", h=NH)
                    chain(nc.vector.tensor_scalar(den[:], got[:, :, DH], 1e-6, None, ALU.add))
                    chain(nc.vector.reciprocal(den[:], den[:]))
                    nc.vector.tensor_tensor(context[:, b, :].rearrange("p (h d) -> p h d", h=NH),
                                            got[:, :, 0:DH], den[:].unsqueeze(2).broadcast_to([P, NH, DH]),
                                            ALU.mult).then_inc(context_ready, 1)
                    dve.wait_ge(context_ready, b + 1)

                for b in range(NB):
                    mask(b)
                    if b:
                        divide(b - 1)
                divide(NB - 1)
                dve.wait_ge(cT_in_psum, 2)
                nc.vector.tensor_copy(contextT[:, 1, :], net.banks[3][:]).then_inc(cT1_ready, 1)
                dve.wait_ge(xb_ready, 1)

                def add(b):
                    dve.wait_ge(y_ready, b + 1)
                    return nc.vector.tensor_tensor(net.r[:, b, :], xb[:, b, :], net.banks[Y[b]][:, 0:D],
                                                   ALU.add)

                finish.run_dve(dve, chain, add)

            @block.gpsimd
            def _(pool):
                pool.wait_ge(net.ready["l0_attn"], 16)
                nc.gpsimd.tensor_tensor(xb[:], net.x[:], w["bo"].unsqueeze(1).broadcast_to([P, NB, D]),
                                        ALU.add).then_inc(xb_ready, 1)
    net.end_sublayer()



def l0_xattn(net, prefetch):
    nc = net.nc
    w = net.weights("l0_xattn")
    wq, wk, wv = (tiles(w[n], FT) for n in ("wq", "wk", "wv"))
    with ExitStack() as sub:
        sig = net.signals(19)
        qk_in_psum, q_ready, k_ready, v_in_psum, v_ready, dve_steps = sig[13:]
        finish = Finish(net, sig[9:13])
        heads = Heads16(net, sub, sig[:9], masked=False, scale=DH ** -0.5)
        with nc.Block() as block:
            @block.sync
            def _(sp):
                prefetch(sp)

            @block.tensor
            def _(pe):
                pe.wait_ge(net.ready["l0_xattn"], 16)
                for m in range(4):
                    project(pe, net.banks[2 + m][:], wk, net.ctxT, m).then_inc(qk_in_psum, 1)
                for b in range(NB):
                    project_tokens(pe, half(net, (6, 7), b), net.ctxT, b, wv).then_inc(v_in_psum, 1)
                for m in range(4):
                    pe.wait_ge(k_ready, m + 1)
                    project(pe, net.banks[2 + m][:], wq, net.xT, m).then_inc(qk_in_psum, 1)
                pe.wait_ge(q_ready, 4)
                pe.wait_ge(v_ready, NB)
                heads.run_pe(pe)
                finish.run_pe(pe)

            @block.scalar
            def _(act):
                act.wait_ge(net.ready["l0_xattn"], 16)
                load_table(net, ACT.Exp)
                for m in range(4):
                    act.wait_ge(qk_in_psum, m + 1)
                    nc.scalar.activation(heads.kT[:, m, :], net.banks[2 + m][:], ACT.Relu,
                                         bias=w["one_rows"][:, 0:1]).then_inc(k_ready, 1)
                for m in range(4):
                    act.wait_ge(qk_in_psum, m + 5)
                    nc.scalar.activation(heads.qT[:, m, :], net.banks[2 + m][:],
                                         ACT.Relu).then_inc(q_ready, 1)
                heads.run_act(act)
                finish.run_act(act)

            @block.vector
            def _(dve):
                chain = Chain(dve, dve_steps)
                for b in range(NB):
                    dve.wait_ge(v_in_psum, PAIR_DONE[b])
                    nc.vector.tensor_scalar(net.v1[:, b, :, 0:DH],
                                            half(net, (6, 7), b).rearrange("p (h d) -> p h d", h=NH),
                                            0.0, None, ALU.max).then_inc(v_ready, 1)
                heads.run_dve(dve, chain)

                def add(b):
                    dve.wait_ge(heads.context_ready, b + 1)
                    return nc.vector.tensor_tensor(net.r[:, b, :], net.x[:, b, :],
                                                   heads.context[:, b, :], ALU.add)

                finish.run_dve(dve, chain, add)
    net.end_sublayer()



class OutputProjection:

    Y = (2, 3, 4, 7)

    def __init__(self, net, sub, heads, wo, signals):
        self.net, self.heads, self.wo = net, heads, wo
        self.cT_in_psum, self.cT0_ready, self.cT1_ready, self.y_ready = signals
        self.contextT = net.scratch(sub)("contextT", [P, FT, T])

    def y(self, b):
        return self.net.banks[self.Y[b]][:, 0:D]

    def run_pe(self, pe):
        transposes(pe, self.net, self.heads.context, (0, 1), self.cT_in_psum, self.heads.context_ready)
        pe.wait_ge(self.cT0_ready, 1)
        pe.wait_ge(self.cT1_ready, 1)
        for b in range(NB):
            project_tokens(pe, self.y(b), self.contextT, b, self.wo).then_inc(self.y_ready, 1)

    def run_act(self, act):
        act.wait_ge(self.cT_in_psum, 1)
        self.net.nc.scalar.copy(self.contextT[:, 0, :], self.net.banks[0][:]).then_inc(self.cT0_ready, 1)

    def run_dve(self, dve):
        dve.wait_ge(self.cT_in_psum, 2)
        self.net.nc.vector.tensor_copy(self.contextT[:, 1, :],
                                       self.net.banks[1][:]).then_inc(self.cT1_ready, 1)



def l0_ffn_attention(net, prefetch):
    nc = net.nc
    w = net.weights("l0_ffn_attention")
    wq, wk, wv, wo = (tiles(w[n], FT) for n in ("wq", "wk", "wv", "wo"))
    with ExitStack() as sub:
        sig = net.signals(39)
        (h_ready, hT_in_psum, hT0_ready, hT1_ready, qk_in_psum, q_ready, k_ready, v_in_psum, v_ready,
         xb_ready, x1_ready, base_ready, h2_ready, h2T_in_psum, h2T_ready, var_ready, rstd_ready,
         dve_steps) = sig[13:31]
        heads = Heads16(net, sub, sig[:9], masked=True, scale=DH ** -0.5)
        back = OutputProjection(net, sub, heads, wo, sig[9:13])
        normed = net.scratch(sub)("normed", [P, NB, D])
        xb = net.scratch(sub)("x_plus_bias", [P, NB, D])
        with nc.Block() as block:
            @block.sync
            def _(sp):
                prefetch(sp)

            @block.tensor
            def _(pe):
                pe.wait_ge(net.ready["l0_ffn_attention"], 16)
                transposes(pe, net, normed, (0, 1), hT_in_psum, h_ready)
                pe.wait_ge(hT0_ready, 1)
                pe.wait_ge(hT1_ready, 1)
                for m in range(4):
                    project(pe, net.banks[2 + m][:], wk, net.xT, m).then_inc(qk_in_psum, 1)
                for b in range(NB):
                    project_tokens(pe, half(net, (6, 7), b), net.xT, b, wv).then_inc(v_in_psum, 1)
                for m in range(4):
                    pe.wait_ge(k_ready, m + 1)
                    project(pe, net.banks[2 + m][:], wq, net.xT, m).then_inc(qk_in_psum, 1)
                pe.wait_ge(q_ready, 4)
                pe.wait_ge(v_ready, NB)
                heads.run_pe(pe)
                back.run_pe(pe)
                transposes(pe, net, normed, (0, 1), h2T_in_psum, h2_ready)

            @block.scalar
            def _(act):
                act.wait_ge(net.ready["l0_ffn_attention"], 16)
                load_table(net, ACT.Sqrt)
                act.wait_ge(var_ready, 1)
                nc.scalar.activation(net.rstd[:], net.rvar[:], ACT.Sqrt).then_inc(rstd_ready, 1)
                load_table(net, ACT.Exp)
                act.wait_ge(hT_in_psum, 1)
                nc.scalar.activation(net.xT[:, 0, :], net.banks[0][:], ACT.Identity,
                                     scale=w["ln1_w"][:, 0:1],
                                     bias=w["ln1_b"][:, 0:1]).then_inc(hT0_ready, 1)
                for m in range(4):
                    act.wait_ge(qk_in_psum, m + 1)
                    nc.scalar.activation(heads.kT[:, m, :], net.banks[2 + m][:], ACT.Identity,
                                         bias=w["bk"][:, m:m + 1]).then_inc(k_ready, 1)
                for m in range(4):
                    act.wait_ge(qk_in_psum, m + 5)
                    nc.scalar.activation(heads.qT[:, m, :], net.banks[2 + m][:], ACT.Identity,
                                         bias=w["bq"][:, m:m + 1]).then_inc(q_ready, 1)
                heads.run_act(act)
                back.run_act(act)
                load_table(net, ACT.Sqrt)
                act.wait_ge(var_ready, 2)
                nc.scalar.activation(net.rstd[:], net.rvar[:], ACT.Sqrt).then_inc(rstd_ready, 1)
                act.wait_ge(h2T_in_psum, 1)
                nc.scalar.activation(net.xT[:, 0, :], net.banks[0][:], ACT.Identity,
                                     scale=w["ln2_w"][:, 0:1],
                                     bias=w["ln2_b"][:, 0:1]).then_inc(h2T_ready, 1)

            @block.vector
            def _(dve):
                chain = Chain(dve, dve_steps)

                def norm(src, n, done):
                    for b in range(NB):
                        if n == 2:
                            dve.wait_ge(back.y_ready, b + 1)
                            nc.vector.tensor_tensor(net.r[:, b, :], xb[:, b, :], back.y(b),
                                                    ALU.add).then_inc(x1_ready, 1)
                            dve.wait_ge(x1_ready, b + 1)
                        chain.step(nc.vector.bn_stats(net.stats[:, b, :], src[:, b, :]))
                    chain.settle()
                    aggregate_dve(net, chain)
                    nc.vector.reciprocal(net.rvar[:], net.var[:]).then_inc(var_ready, 1)
                    dve.wait_ge(rstd_ready, n)
                    for b in range(NB):
                        nc.vector.tensor_scalar(normed[:, b, :], src[:, b, :], net.mv[:, b, 0:1],
                                                net.rstd[:, b:b + 1], ALU.subtract,
                                                ALU.mult).then_inc(done, 1)

                dve.wait_ge(net.ready["l0_ffn_attention"], 16)
                norm(net.x, 1, h_ready)
                dve.wait_ge(hT_in_psum, 2)
                nc.vector.tensor_scalar(net.xT[:, 1, :], net.banks[1][:], w["ln1_w"][:, 1:2],
                                        w["ln1_b"][:, 1:2], ALU.mult, ALU.add).then_inc(hT1_ready, 1)
                for b in range(NB):
                    dve.wait_ge(v_in_psum, PAIR_DONE[b])
                    nc.vector.tensor_tensor(net.v1[:, b, :, 0:DH],
                                            half(net, (6, 7), b).rearrange("p (h d) -> p h d", h=NH),
                                            w["bv"].rearrange("p (h d) -> p h d", h=NH),
                                            ALU.add).then_inc(v_ready, 1)
                heads.run_dve(dve, chain)
                back.run_dve(dve)
                dve.wait_ge(xb_ready, 1)
                norm(net.r, 2, h2_ready)
                dve.wait_ge(h2T_in_psum, 2)
                nc.vector.tensor_scalar(net.xT[:, 1, :], net.banks[1][:], w["ln2_w"][:, 1:2],
                                        w["ln2_b"][:, 1:2], ALU.mult, ALU.add).then_inc(h2T_ready, 1)

            @block.gpsimd
            def _(pool):
                pool.wait_ge(net.ready["l0_ffn_attention"], 16)
                nc.gpsimd.tensor_tensor(xb[:], net.x[:], w["bo"].unsqueeze(1).broadcast_to([P, NB, D]),
                                        ALU.add).then_inc(xb_ready, 1)
                pool.wait_ge(x1_ready, NB)
                nc.gpsimd.tensor_tensor(net.x[:], net.x[:], net.r[:], ALU.add).then_inc(base_ready, 1)
                pool.wait_ge(base_ready, 1)
    net.end_sublayer()



class Experts:

    HIDDEN, OUT = (1, 2, 3), ((4, 5), (6, 7))

    def __init__(self, net, sub, name, signals, n_hidden, func, bias=None, slots=EXPERTS):
        self.net, self.n, self.func, self.bias, self.slots = net, n_hidden, func, bias, slots
        (self.hidden_in_psum, self.hidden_ready, self.out_in_psum, self.out_taken) = signals
        self.hidden = [net.scratch(sub)(f"hidden{i}", [P, n_hidden, T])
                       for i in range(2)]
        loop = next(part for part in LOOPS if name in part)
        self.loads = 16 * (1 + [s for s in loop if s in RUN and s in EXPERT_NETS].index(name))

    def w1(self, e):
        at = (e % self.slots) * self.n * 2 * D
        return tiles(self.net.e_room[:, at:at + self.n * D], FT)

    def w2(self, e):
        at = (e % self.slots) * self.n * 2 * D + self.n * D
        return tiles(self.net.e_room[:, at:at + self.n * D], self.n)

    def run_pe(self, pe, before_out=None):
        net = self.net

        def hidden(e):
            pe.wait_ge(net.expert_ready[e], self.loads)
            for m in range(self.n):
                n = e * self.n + m
                if n >= 3:
                    pe.wait_ge(self.hidden_ready, n - 2)
                project(pe, net.banks[self.HIDDEN[n % 3]][:], self.w1(e), net.xT,
                        m).then_inc(self.hidden_in_psum, 1)

        def out(e):
            pe.wait_ge(self.hidden_ready, self.n * (e + 1))
            if e >= 2:
                pe.wait_ge(self.out_taken, NB * (e - 1))
            for b in range(NB):
                project_tokens(pe, half(net, self.OUT[e % 2], b), self.hidden[e % 2], b,
                               self.w2(e)).then_inc(self.out_in_psum, 1)

        hidden(0)
        for e in range(EXPERTS):
            if e + 1 < EXPERTS:
                hidden(e + 1)
            if e == 0 and before_out:
                before_out()
            out(e)

    def run_act(self, act):
        for e in range(EXPERTS):
            if e >= 2:
                act.wait_ge(self.out_in_psum, NB * (e - 1))
            for m in range(self.n):
                n = e * self.n + m
                act.wait_ge(self.hidden_in_psum, n + 1)
                kw = {"bias": self.bias[:, n:n + 1]} if self.bias is not None else {}
                self.net.nc.scalar.activation(self.hidden[e % 2][:, m, :],
                                              self.net.banks[self.HIDDEN[n % 3]][:], self.func,
                                              **kw).then_inc(self.hidden_ready, 1)

    def run_dve(self, dve, gates, base):
        net = self.net

        def add(e, b):
            dve.wait_ge(self.out_in_psum, NB * e + PAIR_DONE[b])
            if e:
                dve.wait_ge(self.out_taken, NB * (e - 1) + b + 1)
            return net.nc.vector.scalar_tensor_tensor(
                out=net.r[:, b, :], in0=half(net, self.OUT[e % 2], b), scalar=gates[:, b, e:e + 1],
                in1=base[:, b, :] if e == 0 else net.r[:, b, :], op0=ALU.mult, op1=ALU.add)

        for e in range(EXPERTS - 1):
            for b in range(NB):
                add(e, b).then_inc(self.out_taken, 1)
        return lambda b: add(EXPERTS - 1, b)


def top2_dve(net, chain, key, chosen, greater, equal, rank):
    nc = net.nc
    shape = [P, NB, EXPERTS, EXPERTS]
    other = key[:].unsqueeze(2).broadcast_to(shape)
    own = key[:].unsqueeze(3).broadcast_to(shape)
    chain.step(nc.vector.tensor_tensor(greater[:], other, own, ALU.is_gt))
    chain(nc.vector.tensor_tensor(equal[:], other, own, ALU.is_equal))
    chain(nc.vector.tensor_tensor(equal[:].rearrange("p b e o -> p b (e o)"),
                                  equal[:].rearrange("p b e o -> p b (e o)"),
                                  net.before[:].unsqueeze(1).broadcast_to([P, NB, EXPERTS * EXPERTS]),
                                  ALU.mult))
    chain(nc.vector.tensor_tensor(greater[:], greater[:], equal[:], ALU.add))
    chain(nc.vector.reduce_sum(rank[:], greater[:], AX_X))
    chain(nc.vector.tensor_scalar(chosen[:], rank[:], 2.0, None, ALU.is_lt))


def load_experts(sub):
    def load(net, sp):
        per = EXPERT_COLS[sub]
        for e in range(min(EXPERTS, EXPERT_ROOM // per)):
            sp.dma_start(net.e_room[:, e * per:(e + 1) * per],
                         net.params[sub + "_experts"][:, e * per:(e + 1) * per]).then_inc(
                             net.expert_ready[e], 16)
    return load



def l0_ffn_experts(net, prefetch):
    nc = net.nc
    w = net.weights("l0_ffn_experts")
    router = tiles(w["router"], FT)
    with ExitStack() as sub:
        sb = net.scratch(sub)

        logits_in_psum, shifted_ready, exp_ready, dve_steps = net.signals(12)[8:]
        finish = Finish(net, net.signals(8)[4:])
        experts = Experts(net, sub, "l0_ffn_experts", net.signals(4), 4, ACT.Gelu)
        mx, total = sb("logit_max", [P, NB]), sb("exp_sum", [P, NB])
        prob, gates, chosen, rank = (sb(n, [P, NB, EXPERTS]) for n in ("prob", "gates", "chosen", "rank"))
        greater, equal = (sb(n, [P, NB, EXPERTS, EXPERTS]) for n in ("greater", "equal"))
        logits = net.banks[0][:, 0:NB * EXPERTS].rearrange("p (b e) -> p b e", b=NB)
        with nc.Block() as block:
            @block.sync
            def _(sp):
                prefetch(sp)

            @block.tensor
            def _(pe):
                pe.wait_ge(net.ready["l0_ffn_experts"], 16)
                for b in range(NB):
                    mm = project_tokens(pe, logits[:, b, :], net.xT, b, router)
                mm.then_inc(logits_in_psum, 1)
                experts.run_pe(pe)
                finish.run_pe(pe)

            @block.scalar
            def _(act):
                act.wait_ge(shifted_ready, 1)
                nc.scalar.activation(prob[:], prob[:], ACT.Exp).then_inc(exp_ready, 1)
                experts.run_act(act)
                finish.run_act(act)

            @block.vector
            def _(dve):
                chain = Chain(dve, dve_steps)
                wide = [P, NB, EXPERTS]
                dve.wait_ge(logits_in_psum, 1)
                chain(nc.vector.reduce_max(mx[:], logits, AX_X))
                nc.vector.tensor_tensor(prob[:], logits, mx[:].unsqueeze(2).broadcast_to(wide),
                                        ALU.subtract).then_inc(shifted_ready, 1)
                dve.wait_ge(exp_ready, 1)
                chain(nc.vector.reduce_sum(total[:], prob[:], AX_X))
                chain(nc.vector.reciprocal(total[:], total[:]))
                chain(nc.vector.tensor_tensor(prob[:], prob[:], total[:].unsqueeze(2).broadcast_to(wide),
                                              ALU.mult))
                top2_dve(net, chain, prob, chosen, greater, equal, rank)
                chain(nc.vector.tensor_tensor(gates[:], prob[:], chosen[:], ALU.mult))
                finish.run_dve(dve, chain, experts.run_dve(dve, gates, net.x))
    net.end_sublayer()



Q_HEADS, KV_HEADS, HD = 4, 2, 64


def l1_attn(net, prefetch):
    nc = net.nc
    w = net.weights("l1_attn")
    wq, wkv, wo = (tiles(w[n], FT) for n in ("wq", "wkv", "wo"))
    with ExitStack() as sub:
        sb = net.scratch(sub)
        normed = sb("normed", [P, NB, D])
        doubled = sb("x_twice", [P, NB, D])
        msq, unit, temp = sb("mean_square", [P, NB]), sb("inverse_length", [P, NB, 6]), sb("temperature", [P, 1])
        squares = sb("squares", [P, NB, 6, HD])
        qk = sb("unit_qk", [P, NB, 6, HD])
        v = sb("values", [P, NB, KV_HEADS, HD + 1])
        qkT = sb("unit_qkT", [P, 3, T])
        mx = sb("score_max", [P, NB, 2, 2])
        negT = sb("negmaxT", [P, P])
        probs = sb("probs", [P, 2, NB, 2, P])
        rec = sb("inverse_sum", [P, NB, Q_HEADS])
        context = sb("context", [P, NB, D])
        contextT = sb("contextT", [P, FT, T])
        (var_ready, rstd_ready, h_ready, hT_in_psum, hT0_ready, hT1_ready, qkv_in_psum, squares_ready,
         v_ready, ones_ready, length_ready, root_ready, unit_ready, unitT_in_psum, unitT_ready,
         unitT_ready_dve, scores_ready, max_ready, neg_ready, negT_in_psum, negT_ready, shifted_ready,
         exp_ready, sums_ready, context_ready, cT_in_psum, cT0_ready, cT1_ready, y_ready, temp_ready,
         doubled_ready, dve_steps) = net.signals(36)[4:]
        finish = Finish(net, net.signals(4))
        HT, QKV, UNIT_T, SCORES, NEG_T = (0, 1), (2, 3, 4, 5), (6, 7, 0), ((2, 3), (4, 5)), 1
        SHIFTED, SUMS, CT, Y = ((6, 7), (2, 3)), (4, 5, 0, 1), (6, 7), (2, 3, 4, 5)
        with nc.Block() as block:
            @block.sync
            def _(sp):
                prefetch(sp)

            @block.tensor
            def _(pe):
                pe.wait_ge(net.ready["l1_attn"], 16)
                transposes(pe, net, normed, HT, hT_in_psum, h_ready)
                pe.wait_ge(hT0_ready, 1)
                pe.wait_ge(hT1_ready, 1)
                for b in range(NB):
                    bank = net.banks[QKV[b]]
                    project_tokens(pe, bank[:, 0:D], net.xT, b, wq)
                    project_tokens(pe, bank[:, D:2 * D], net.xT, b, wkv).then_inc(qkv_in_psum, 1)
                for k, bank in enumerate(UNIT_T):
                    pe.wait_ge(unit_ready, NB)
                    for b in range(NB):
                        mm = pe.transpose(net.banks[bank][:, seq(b)],
                                          qk[:, b, 2 * k:2 * k + 2, :].rearrange("p h d -> p (h d)"),
                                          net.ident[:])
                    mm.then_inc(unitT_in_psum, 1)
                pe.wait_ge(unitT_ready, 2)
                pe.wait_ge(unitT_ready_dve, 1)
                pe.wait_ge(v_ready, NB)

                def four(out_banks, u, lhs_tile, rhs_tile, mask, done, shift):
                    for j in range(2):
                        pe.matmul(net.banks[out_banks[j]][:], net.identb[:],
                                  mask[:].rearrange("p a k -> p (a k)"), start=True, stop=True)
                    for a in range(4):
                        b, i = 2 * u + a // 2, a % 2
                        if shift:
                            for j in range(2):
                                r = 4 * b + 2 * i + j
                                pe.matmul(net.banks[out_banks[j]][:, seq(a)],
                                          net.ident[0:16, r:r + 1].broadcast_to([16, P]), negT[0:16, :],
                                          start=False, stop=True, skip_group_check=True)
                    for a in range(4):
                        b, i = 2 * u + a // 2, a % 2
                        for j in range(2):
                            rows = slice(HD * j, HD * (j + 1))
                            lt, rt = (i if x == "q" else 2 for x in (lhs_tile, rhs_tile))
                            mm = pe.matmul(net.banks[out_banks[j]][:, seq(a)], qkT[rows, lt, seq(b)],
                                           qkT[rows, rt, seq(b)], start=False, stop=True,
                                           skip_group_check=True, tile_position=(HD * j, 0))
                            if a == 3:
                                mm.then_inc(done, 1)

                for u in range(2):
                    four(SCORES[u], u, "q", "k", net.causal_qk, scores_ready, False)
                pe.wait_ge(neg_ready, 1)
                pe.transpose(net.banks[NEG_T][0:16, 0:P], mx[:].rearrange("p b i j -> p (b i j)"),
                             net.ident[:]).then_inc(negT_in_psum, 1)
                pe.wait_ge(negT_ready, 1)
                for u in range(2):
                    four(SHIFTED[u], u, "k", "q", net.causal_kq, shifted_ready, True)
                pe.wait_ge(ones_ready, 1)
                for b in range(NB):
                    if b % 2 == 0:
                        pe.wait_ge(exp_ready, 2 * (b // 2 + 1))
                    for h in range(Q_HEADS):
                        mm = pe.matmul(net.banks[SUMS[b]][:, h * (HD + 1):(h + 1) * (HD + 1)],
                                       probs[:, h // 2, b, h % 2, :], v[:, b, h // 2, :], start=True, stop=True)
                    mm.then_inc(sums_ready, 1)
                transposes(pe, net, context, CT, cT_in_psum, context_ready)
                pe.wait_ge(cT0_ready, 1)
                pe.wait_ge(cT1_ready, 1)
                for b in range(NB):
                    project_tokens(pe, net.banks[Y[b]][:, 0:D], contextT, b, wo).then_inc(y_ready, 1)
                finish.run_pe(pe)

            @block.scalar
            def _(act):
                act.wait_ge(net.ready["l1_attn"], 16)
                nc.scalar.activation(temp[:], w["log_temperature"], ACT.Exp).then_inc(temp_ready, 1)
                load_table(net, ACT.Sqrt)
                act.wait_ge(var_ready, 1)
                nc.scalar.activation(net.rstd[:], net.rvar[:], ACT.Sqrt).then_inc(rstd_ready, 1)
                act.wait_ge(hT_in_psum, 1)
                nc.scalar.activation(net.xT[:, 0, :], net.banks[HT[0]][:], ACT.Copy,
                                     scale=w["norm_w"][:, 0:1]).then_inc(hT0_ready, 1)
                for b in range(NB):
                    act.wait_ge(qkv_in_psum, b + 1)
                    nc.scalar.activation(squares[:, b, :, :].rearrange("p h d -> p (h d)"),
                                         net.banks[QKV[b]][:, 0:6 * HD], ACT.Square).then_inc(squares_ready, 1)
                act.wait_ge(length_ready, 1)
                nc.scalar.activation(unit[:], unit[:], ACT.Sqrt).then_inc(root_ready, 1)
                load_table(net, ACT.Exp)
                for k in range(2):
                    act.wait_ge(unitT_in_psum, k + 1)
                    nc.scalar.copy(qkT[:, k, :], net.banks[UNIT_T[k]][:]).then_inc(unitT_ready, 1)
                act.wait_ge(temp_ready, 1)
                for u in range(2):
                    for j in range(2):
                        act.wait_ge(shifted_ready, 2 * u + j + 1)
                        nc.scalar.activation(
                            probs[:, j, 2 * u:2 * u + 2, :, :].rearrange("p b i q -> p (b i q)"),
                            net.banks[SHIFTED[u][j]][:], ACT.Exp, scale=temp[:, 0:1]).then_inc(exp_ready, 1)
                act.wait_ge(cT_in_psum, 1)
                nc.scalar.copy(contextT[:, 0, :], net.banks[CT[0]][:]).then_inc(cT0_ready, 1)
                finish.run_act(act)

            @block.vector
            def _(dve):
                chain = Chain(dve, dve_steps)
                dve.wait_ge(net.ready["l1_attn"], 16)
                for b in range(NB):
                    chain.step(nc.vector.bn_stats(net.stats[:, b, :], net.x[:, b, :]))
                chain.settle()
                for b in range(NB):
                    chain.step(nc.vector.bn_aggr(net.mv[:, b, :], net.stats[:, b, :]))
                chain.settle()
                chain(nc.vector.tensor_tensor(msq[:], net.mv[:, :, 0], net.mv[:, :, 0], ALU.mult))
                chain(nc.vector.tensor_tensor(msq[:], msq[:], net.mv[:, :, 1], ALU.add))
                chain(nc.vector.tensor_scalar(net.var[:], msq[:], 1e-6, None, ALU.add))
                nc.vector.reciprocal(net.rvar[:], net.var[:]).then_inc(var_ready, 1)
                dve.wait_ge(rstd_ready, 1)
                for b in range(NB):
                    nc.vector.tensor_scalar(normed[:, b, :], net.x[:, b, :], net.rstd[:, b:b + 1], None,
                                            ALU.mult).then_inc(h_ready, 1)
                dve.wait_ge(hT_in_psum, 2)
                nc.vector.tensor_scalar(net.xT[:, 1, :], net.banks[HT[1]][:], w["norm_w"][:, 1:2], None,
                                        ALU.mult).then_inc(hT1_ready, 1)
                for b in range(NB):
                    dve.wait_ge(squares_ready, b + 1)
                    chain.step(nc.vector.reduce_sum(unit[:, b, :], squares[:, b, :, :], AX_X))
                chain.settle()
                chain(nc.vector.tensor_scalar(unit[:], unit[:], 1e-24, None, ALU.max))
                nc.vector.reciprocal(unit[:], unit[:]).then_inc(length_ready, 1)
                dve.wait_ge(root_ready, 1)
                for b in range(NB):
                    nc.vector.tensor_tensor(qk[:, b, :, :],
                                            net.banks[QKV[b]][:, 0:6 * HD].rearrange("p (h d) -> p h d", h=6),
                                            unit[:, b, :].unsqueeze(2).broadcast_to([P, 6, HD]),
                                            ALU.mult).then_inc(unit_ready, 1)
                dve.wait_ge(ones_ready, 1)
                for b in range(NB):
                    nc.vector.tensor_copy(v[:, b, :, 0:HD],
                                          net.banks[QKV[b]][:, 6 * HD:].rearrange("p (h d) -> p h d", h=2)
                                          ).then_inc(v_ready, 1)
                dve.wait_ge(unitT_in_psum, 3)
                nc.vector.tensor_copy(qkT[:, 2, :], net.banks[UNIT_T[2]][:]).then_inc(unitT_ready_dve, 1)
                for u in range(2):
                    for j in range(2):
                        dve.wait_ge(scores_ready, 2 * u + j + 1)
                        nc.vector.reduce_max(mx[:, 2 * u:2 * u + 2, :, j],
                                             net.banks[SCORES[u][j]][:].rearrange(
                                                 "p (b i k) -> p b i k", b=2, i=2),
                                             AX_X).then_inc(max_ready, 1)
                dve.wait_ge(max_ready, 4)
                nc.vector.tensor_scalar(mx[:], mx[:], -1.0, None, ALU.mult).then_inc(neg_ready, 1)
                dve.wait_ge(negT_in_psum, 1)
                nc.vector.tensor_copy(negT[0:16, :], net.banks[NEG_T][0:16, 0:P]).then_inc(negT_ready, 1)
                for b in range(NB):
                    dve.wait_ge(sums_ready, b + 1)
                    got = net.banks[SUMS[b]][:, 0:Q_HEADS * (HD + 1)].rearrange("p (h d) -> p h d", h=Q_HEADS)
                    chain(nc.vector.reciprocal(rec[:, b, :], got[:, :, HD]))
                    nc.vector.tensor_tensor(context[:, b, :].rearrange("p (h d) -> p h d", h=Q_HEADS),
                                            got[:, :, 0:HD],
                                            rec[:, b, :].unsqueeze(2).broadcast_to([P, Q_HEADS, HD]),
                                            ALU.mult).then_inc(context_ready, 1)
                dve.wait_ge(cT_in_psum, 2)
                nc.vector.tensor_copy(contextT[:, 1, :], net.banks[CT[1]][:]).then_inc(cT1_ready, 1)
                dve.wait_ge(doubled_ready, 1)

                def add(b):
                    dve.wait_ge(y_ready, b + 1)
                    return nc.vector.scalar_tensor_tensor(
                        out=net.r[:, b, :], in0=net.banks[Y[b]][:, 0:D], scalar=w["gate"],
                        in1=doubled[:, b, :], op0=ALU.mult, op1=ALU.add)

                finish.run_dve(dve, chain, add)

            @block.gpsimd
            def _(pool):
                nc.gpsimd.memset(v[:], 1.0).then_inc(ones_ready, 1)
                nc.gpsimd.tensor_tensor(doubled[:], net.x[:], net.x[:], ALU.add).then_inc(doubled_ready, 1)
    net.end_sublayer()



PAD = P + 2


def l1_xattn(net, prefetch):
    nc = net.nc
    w = net.weights("l1_xattn")
    with ExitStack() as sub:
        sb = net.scratch(sub)
        decay = sb("decay", [P, FT])
        decays = sb("decays", [P, FT, NB * PAD])
        ek = sb("exp_k", [P, FT, NB, PAD])
        ekv = sb("exp_k_v", [P, FT, NB, PAD])
        cur = sb("exp_u_k", [P, FT, T])
        gate = sb("sigmoid_r", [P, FT, T])
        scans = sb("scans", [P, 4, NB, PAD])
        num, den = sb("numerator", [P, FT, T]), sb("denominator", [P, FT, T])
        (gate_ready, decay_ready, zeros_ready, ek_ready, cur_ready, ekv_ready, curv_ready,
         scans_ready, sums_ready, out_ready, out_in_psum, dve_steps, pool_steps) = net.signals(17)[4:]
        finish = Finish(net, net.signals(4))

        def by_seq(ap):
            return ap.rearrange("p (b t) -> p b t", b=NB)

        with nc.Block() as block:
            @block.sync
            def _(sp):
                prefetch(sp)

            @block.tensor
            def _(pe):
                pe.wait_ge(out_ready, 2)
                for half_ in range(2):
                    for b in (2 * half_, 2 * half_ + 1):
                        for f in range(FT):
                            mm = pe.transpose(half(net, (2, 3), b)[:, f * P:(f + 1) * P],
                                              num[:, f, seq(b)], net.ident[:])
                        mm.then_inc(out_in_psum, 1)
                finish.run_pe(pe)

            @block.scalar
            def _(act):
                act.wait_ge(net.ready["l1_xattn"], 16)
                nc.scalar.activation(decay[:], w["w"], ACT.Exp).then_inc(decay_ready, 1)
                act.wait_ge(zeros_ready, 1)
                for f in range(FT):
                    nc.scalar.activation(ek[:, f, :, 1:P + 1], by_seq(net.ctxT[:, f, :]),
                                         ACT.Exp).then_inc(ek_ready, 1)
                for f in range(FT):
                    nc.scalar.activation(cur[:, f, :], net.ctxT[:, f, :], ACT.Exp,
                                         bias=w["u"][:, f:f + 1]).then_inc(cur_ready, 1)
                for f in range(FT):
                    nc.scalar.activation(gate[:, f, :], net.xT[:, f, :], ACT.Sigmoid).then_inc(gate_ready, 1)
                finish.run_act(act)

            @block.vector
            def _(dve):
                chain = Chain(dve, dve_steps)
                dve.wait_ge(net.ready["l1_xattn"], 16)
                dve.wait_ge(decay_ready, 1)
                for f in range(FT):
                    chain.step(nc.vector.tensor_scalar(decays[:, f, :], net.inside[:], decay[:, f:f + 1],
                                                       None, ALU.mult))
                chain.settle()
                for f in range(FT):
                    dve.wait_ge(ek_ready, f + 1)
                    dve.wait_ge(ekv_ready, f + 1)
                    if f:
                        dve.wait_ge(scans_ready, 4 * f)
                        dve.wait_ge(sums_ready, 2 * f)
                    for k, (src, back) in enumerate(((ekv, False), (ek, False), (ekv, True), (ek, True))):
                        data = src[:, f, :, :].rearrange("p b t -> p (b t)")
                        mult = decays[:, f, :]
                        dst = scans[:, k, :, :].rearrange("p b t -> p (b t)")
                        if back:
                            data, mult, dst = data[:, ::-1], mult[:, ::-1], dst[:, ::-1]
                        nc.vector.tensor_tensor_scan(dst, mult, data, 0.0, ALU.mult,
                                                     ALU.add).then_inc(scans_ready, 1)
                    dve.wait_ge(scans_ready, 4 * (f + 1))
                    dve.wait_ge(curv_ready, f + 1)
                    for k, (out, own) in enumerate(((num, num), (den, cur))):
                        chain(nc.vector.tensor_tensor(scans[:, k, :, 0:P], scans[:, k, :, 0:P],
                                                      scans[:, 2 + k, :, 2:P + 2], ALU.add))
                        if k == 1:
                            dve.wait_ge(cur_ready, f + 1)
                        nc.vector.tensor_tensor(by_seq(out[:, f, :]), scans[:, k, :, 0:P],
                                                by_seq(own[:, f, :]), ALU.add).then_inc(sums_ready, 1)
                    dve.wait_ge(sums_ready, 2 * (f + 1))
                    dve.wait_ge(gate_ready, f + 1)
                    chain(nc.vector.reciprocal(den[:, f, :], den[:, f, :]))
                    chain(nc.vector.tensor_tensor(num[:, f, :], num[:, f, :], den[:, f, :], ALU.mult))
                    nc.vector.tensor_tensor(num[:, f, :], num[:, f, :], gate[:, f, :],
                                            ALU.mult).then_inc(out_ready, 1)

                def add(b):
                    dve.wait_ge(out_in_psum, PAIR_DONE[b])
                    return nc.vector.tensor_tensor(net.r[:, b, :], net.x[:, b, :], half(net, (2, 3), b),
                                                   ALU.add)

                finish.run_dve(dve, chain, add)

            @block.gpsimd
            def _(pool):
                nc.gpsimd.memset(ek[:], 0.0).then_inc(pool_steps, 1)
                nc.gpsimd.memset(ekv[:], 0.0).then_inc(pool_steps, 1)
                pool.wait_ge(pool_steps, 2)
                nc.gpsimd.engine_nop().then_inc(zeros_ready, 1)
                for f in range(FT):
                    pool.wait_ge(ek_ready, f + 1)
                    nc.gpsimd.tensor_tensor(ekv[:, f, :, 1:P + 1], ek[:, f, :, 1:P + 1],
                                            by_seq(net.ctxT[:, f, :]), ALU.mult).then_inc(ekv_ready, 1)
                for f in range(FT):
                    pool.wait_ge(cur_ready, f + 1)
                    nc.gpsimd.tensor_tensor(num[:, f, :], cur[:, f, :], net.ctxT[:, f, :],
                                            ALU.mult).then_inc(curv_ready, 1)
    net.end_sublayer()



def floor_dve(nc, chain, out, src, whole, above):
    chain(nc.vector.tensor_copy(whole, src))
    chain(nc.vector.tensor_copy(out, whole))
    chain(nc.vector.tensor_tensor(above, out, src, ALU.is_gt))
    chain(nc.vector.tensor_tensor(out, out, above, ALU.subtract))


def l1_ffn(net, prefetch):
    nc = net.nc
    w = net.weights("l1_ffn")
    b2 = tiles(w["b2"], EXPERTS)
    with ExitStack() as sub:
        sb = net.scratch(sub)
        dve_steps = net.signals(9)[8]
        finish = Finish(net, net.signals(8)[4:])
        experts = Experts(net, sub, "l1_ffn", net.signals(4), 8, ACT.Relu, bias=w["b1"],
                          slots=EXPERT_ROOM // EXPERT_COLS["l1_ffn"])
        keys, octave, fl = (sb(n, [P, NB]) for n in ("keys", "octave", "floor"))
        above, whole = sb("above", [P, NB]), sb("whole", [P, NB], I32)
        gates = sb("gates", [P, NB, EXPERTS])
        with nc.Block() as block:
            @block.sync
            def _(sp):
                for e in range(experts.slots, EXPERTS):
                    sp.wait_ge(experts.out_in_psum, NB * (e - experts.slots + 1))
                    at = (e % experts.slots) * EXPERT_COLS["l1_ffn"]
                    sp.dma_start(net.e_room[:, at:at + EXPERT_COLS["l1_ffn"]],
                                 net.params["l1_ffn_experts"][:, e * EXPERT_COLS["l1_ffn"]:
                                                              (e + 1) * EXPERT_COLS["l1_ffn"]]
                                 ).then_inc(net.expert_ready[e], 16)
                prefetch(sp)

            @block.tensor
            def _(pe):
                experts.run_pe(pe)
                finish.run_pe(pe)

            @block.scalar
            def _(act):
                act.wait_ge(net.ready["l1_ffn"], 16)
                experts.run_act(act)
                finish.run_act(act)

            @block.vector
            def _(dve):
                chain = Chain(dve, dve_steps)
                dve.wait_ge(net.ready["l1_ffn"], 16)
                chain(nc.vector.tensor_tensor(net.r[:], net.x[:], w["wr"].unsqueeze(1).broadcast_to([P, NB, D]),
                                              ALU.mult))
                chain(nc.vector.reduce_sum(keys[:], net.r[:], AX_X))
                chain(nc.vector.tensor_scalar(keys[:], keys[:], w["br"], None, ALU.add))
                floor_dve(nc, chain, fl[:], keys[:], whole[:], above[:])
                chain(nc.vector.tensor_scalar(keys[:], fl[:], 1.0 / EXPERTS, None, ALU.mult))
                floor_dve(nc, chain, octave[:], keys[:], whole[:], above[:])
                chain(nc.vector.tensor_scalar(octave[:], octave[:], float(-EXPERTS), None, ALU.mult))
                chain(nc.vector.tensor_tensor(fl[:], fl[:], octave[:], ALU.add))
                for e in range(EXPERTS):
                    chain.step(nc.vector.tensor_scalar(gates[:, :, e], fl[:], float(e), None, ALU.is_equal))
                chain.settle()
                for e in range(EXPERTS):
                    for b in range(NB):
                        chain.step(nc.vector.scalar_tensor_tensor(
                            out=net.r[:, b, :], in0=b2[:, e, :], scalar=gates[:, b, e:e + 1],
                            in1=net.x[:, b, :] if e == 0 else net.r[:, b, :], op0=ALU.mult, op1=ALU.add))
                    chain.settle()
                finish.run_dve(dve, chain, experts.run_dve(dve, gates, net.r))
    net.end_sublayer()



CONV = 4
CT_ = CONV * NB


def l2_attn(net, prefetch):
    nc = net.nc
    w = net.weights("l2_attn")
    wqk, wv, wo, ch_w1 = (tiles(w[n], FT) for n in ("wqk", "wv", "wo", "ch_w1"))
    c1, c2, conv2_b = w["c1"], w["c2"], w["conv2_b"]
    ROWS = slice(0, CT_)
    with ExitStack() as sub:
        sb = net.scratch(sub)
        dq, dqk = sb("q_less_mean", [P, NB, D]), sb("products", [P, NB, D])
        qstats, qmv = sb("qk_stats", [P, NB, 2, 6]), sb("qk_mean_var", [P, NB, 2, 2])
        cov = sb("covariance", [P, NB])
        num, den, tmp = (sb(n, [P, NB]) for n in ("numerator", "denominator", "partial"))
        base = sb("attn_base", [P, CONV, NB])
        rows_in = sb("rows", [CT_, P + 2])
        h, hh = sb("conv1", [CT_, P]), sb("conv1_less_mean", [CT_, P])
        act_in = sb("conv2_input", [CT_, P + 2])
        z = sb("conv2", [CT_, P])
        one = {n: sb(n, [CT_, 1]) for n in ("row_sum", "group_mean", "square_sum", "group_var", "scale")}
        final, weight_rows = sb("final", [NB, P]), sb("weight_rows", [NB, P])
        total = sb("exp_sum", [NB, 1])
        weights = sb("token_weights", [P, NB])
        mean = sb("feature_sums", [P, FT, NB])
        ch_h, ch = sb("channel_hidden", [64, NB]), sb("channel_weights", [P, FT, NB])
        vT = sb("weighted_vT", [P, FT, T])
        xb = sb("x_plus_bias", [P, NB, D])
        (qk_in_psum, base_ready, rows_in_psum, rows_ready,
         sum_ready, mean_in_psum, centred_ready, squares_ready, var_in_psum, gvar_ready, groot_ready,
         scale_ready, relu_ready, z_ready, z_in_psum, final_ready, sig_ready, exp_ready, weight_ready,
         weights_in_psum, v_in_psum, fmean_ready, ch1_in_psum, ch1_ready, ch2_in_psum, ch_ready,
         vT_ready, y_ready, xb_ready, dve_steps, zeros_ready) = net.signals(35)[4:]
        finish = Finish(net, net.signals(4))
        QK, V, SMALL, CHANNEL, Y = (2, 3, 4, 5), (6, 7), 0, 1, (2, 3, 4, 5)
        small, channel = net.banks[SMALL], net.banks[CHANNEL]
        with nc.Block() as block:
            @block.sync
            def _(sp):
                prefetch(sp)

            @block.tensor
            def _(pe):
                pe.wait_ge(net.ready["l2_attn"], 16)
                for b in range(NB):
                    project_tokens(pe, net.banks[QK[b]][:], net.xT, b, wqk).then_inc(qk_in_psum, 1)
                for m in range(FT):
                    project(pe, net.banks[V[m]][:], wv, net.xT, m).then_inc(v_in_psum, 1)
                pe.wait_ge(fmean_ready, 1)
                for f in range(FT):
                    mm = pe.matmul(channel[0:64, 0:NB], ch_w1[:, f, :], mean[:, f, :],
                                   start=f == 0, stop=f == FT - 1)
                mm.then_inc(ch1_in_psum, 1)
                pe.wait_ge(ch1_ready, 1)
                for f in range(FT):
                    mm = pe.matmul(channel[:, f * NB:(f + 1) * NB], w["ch_w2"][0:64, f * P:(f + 1) * P],
                                   ch_h[:], start=True, stop=True)
                mm.then_inc(ch2_in_psum, 1)
                pe.wait_ge(base_ready, 1)
                pe.transpose(small[ROWS, 0:P], base[:].rearrange("p c b -> p (c b)"),
                             net.ident[:]).then_inc(rows_in_psum, 1)
                pe.wait_ge(sum_ready, 1)
                pe.wait_ge(rows_ready, 1)
                pe.matmul(small[ROWS, 0:1], w["groups"][ROWS, 0:CT_], one["row_sum"][:],
                          start=True, stop=True).then_inc(mean_in_psum, 1)
                pe.wait_ge(squares_ready, 1)
                pe.wait_ge(centred_ready, 1)
                pe.matmul(small[ROWS, 1:2], w["groups"][ROWS, 0:CT_], one["square_sum"][:],
                          start=True, stop=True).then_inc(var_in_psum, 1)
                pe.wait_ge(z_ready, 1)
                pe.matmul(small[0:NB, 0:P], w["channels"][ROWS, 0:NB], z[:],
                          start=True, stop=True).then_inc(z_in_psum, 1)
                pe.wait_ge(weight_ready, 1)
                pe.transpose(small[:, 0:NB], weight_rows[:], net.ident[0:NB, 0:NB]).then_inc(weights_in_psum, 1)
                pe.wait_ge(vT_ready, FT)
                for b in range(NB):
                    project_tokens(pe, net.banks[Y[b]][:, 0:D], vT, b, wo).then_inc(y_ready, 1)
                finish.run_pe(pe)

            @block.scalar
            def _(act):
                act.wait_ge(net.ready["l2_attn"], 16)
                act.wait_ge(ch1_in_psum, 1)
                nc.scalar.activation(ch_h[:], channel[0:64, 0:NB], ACT.Relu, scale=1.0 / P,
                                     bias=w["ch_b1"][0:64, 0:1]).then_inc(ch1_ready, 1)
                act.wait_ge(ch2_in_psum, 1)
                for f in range(FT):
                    nc.scalar.activation(ch[:, f, :], channel[:, f * NB:(f + 1) * NB], ACT.Sigmoid,
                                         bias=w["ch_b2"][:, f:f + 1]).then_inc(ch_ready, 1)
                act.wait_ge(gvar_ready, 1)
                nc.scalar.activation(one["group_var"][:], one["group_var"][:], ACT.Sqrt).then_inc(groot_ready, 1)
                act.wait_ge(scale_ready, 1)
                act.wait_ge(zeros_ready, 1)
                nc.scalar.activation(act_in[:, 1:P + 1], hh[:], ACT.Relu, scale=one["scale"][:, 0:1],
                                     bias=w["gn_b"][ROWS, 0:1]).then_inc(relu_ready, 1)
                act.wait_ge(final_ready, 1)
                nc.scalar.activation(final[:], final[:], ACT.Sigmoid).then_inc(sig_ready, 1)
                act.wait_ge(sig_ready, 1)
                nc.scalar.activation(weight_rows[:], final[:], ACT.Exp,
                                     accum_out=total[:]).then_inc(exp_ready, 1)
                finish.run_act(act)

            @block.vector
            def _(dve):
                chain = Chain(dve, dve_steps)
                tt, ts, stt = nc.vector.tensor_tensor, nc.vector.tensor_scalar, nc.vector.scalar_tensor_tensor
                dve.wait_ge(net.ready["l2_attn"], 16)
                nc.vector.reduce_sum(mean[:], net.xT[:].rearrange("p f (b t) -> p f b t", b=NB),
                                     AX_X).then_inc(fmean_ready, 1)
                for b in range(NB):
                    dve.wait_ge(qk_in_psum, b + 1)
                    for s in range(2):
                        chain.step(nc.vector.bn_stats(qstats[:, b, s, :],
                                                      net.banks[QK[b]][:, s * D:(s + 1) * D]))
                    chain.settle()
                    for s in range(2):
                        chain.step(nc.vector.bn_aggr(qmv[:, b, s, :], qstats[:, b, s, :]))
                    chain.settle()
                    chain(ts(dq[:, b, :], net.banks[QK[b]][:, 0:D], qmv[:, b, 0, 0:1], None, ALU.subtract))
                    chain.step(stt(out=dqk[:, b, :], in0=net.banks[QK[b]][:, D:2 * D],
                                   scalar=qmv[:, b, 1, 0:1], in1=dq[:, b, :], op0=ALU.subtract,
                                   op1=ALU.mult, accum_out=cov[:, b:b + 1]))
                chain.settle()
                mq, mk, vq, vk = (qmv[:, :, s, k] for s, k in ((0, 0), (1, 0), (0, 1), (1, 1)))
                chain(tt(num[:], mq, mk, ALU.mult))
                chain(ts(num[:], num[:], 2.0, c1, ALU.mult, ALU.add))
                chain(ts(tmp[:], cov[:], 2.0 / (D - 1), c2, ALU.mult, ALU.add))
                chain(tt(num[:], num[:], tmp[:], ALU.mult))
                chain(tt(den[:], mq, mq, ALU.mult))
                chain(tt(tmp[:], mk, mk, ALU.mult))
                chain(stt(out=den[:], in0=den[:], scalar=c1, in1=tmp[:], op0=ALU.add, op1=ALU.add))
                chain(tt(tmp[:], vq, vk, ALU.add))
                chain(ts(tmp[:], tmp[:], D / (D - 1), c2, ALU.mult, ALU.add))
                chain(tt(den[:], den[:], tmp[:], ALU.mult))
                chain(ts(den[:], den[:], 1e-7, None, ALU.add))
                chain(nc.vector.reciprocal(den[:], den[:]))
                chain(tt(num[:], num[:], den[:], ALU.mult))
                chain(tt(base[:], num[:].unsqueeze(1).broadcast_to([P, CONV, NB]),
                         num[:].unsqueeze(1).broadcast_to([P, CONV, NB]), ALU.mult))
                nc.vector.engine_nop().then_inc(base_ready, 1)
                for f in range(FT):
                    dve.wait_ge(v_in_psum, f + 1)
                    dve.wait_ge(ch_ready, f + 1)
                    tt(vT[:, f, :].rearrange("p (b t) -> p b t", b=NB),
                       net.banks[V[f]][:].rearrange("p (b t) -> p b t", b=NB),
                       ch[:, f, :].unsqueeze(2).broadcast_to([P, NB, P]), ALU.mult).then_inc(vT_ready, 1)
                dve.wait_ge(rows_in_psum, 1)
                dve.wait_ge(zeros_ready, 1)
                nc.vector.tensor_copy(rows_in[:, 1:P + 1], small[ROWS, 0:P]).then_inc(rows_ready, 1)
                dve.wait_ge(rows_ready, 1)
                conv1, conv2 = w["conv1"], w["conv2"]
                chain(ts(h[:], rows_in[:, 0:P], conv1[ROWS, 0:1], None, ALU.mult))
                chain(stt(out=h[:], in0=rows_in[:, 1:P + 1], scalar=conv1[ROWS, 1:2], in1=h[:],
                          op0=ALU.mult, op1=ALU.add))
                chain(stt(out=h[:], in0=rows_in[:, 2:P + 2], scalar=conv1[ROWS, 2:3], in1=h[:],
                          op0=ALU.mult, op1=ALU.add))
                nc.vector.reduce_sum(one["row_sum"][:], h[:], AX_X).then_inc(sum_ready, 1)
                dve.wait_ge(mean_in_psum, 1)
                chain(ts(one["group_mean"][:], small[ROWS, 0:1], 1.0 / (2 * P), None, ALU.mult))
                chain(ts(hh[:], h[:], one["group_mean"][:, 0:1], None, ALU.subtract))
                nc.vector.engine_nop().then_inc(centred_ready, 1)
                chain(tt(h[:], hh[:], hh[:], ALU.mult))
                nc.vector.reduce_sum(one["square_sum"][:], h[:], AX_X).then_inc(squares_ready, 1)
                dve.wait_ge(var_in_psum, 1)
                chain(ts(one["group_var"][:], small[ROWS, 1:2], 1.0 / (2 * P), EPS, ALU.mult, ALU.add))
                nc.vector.reciprocal(one["group_var"][:], one["group_var"][:]).then_inc(gvar_ready, 1)
                dve.wait_ge(groot_ready, 1)
                tt(one["scale"][:], one["group_var"][:], w["gn_g"][ROWS, :], ALU.mult).then_inc(scale_ready, 1)
                dve.wait_ge(relu_ready, 1)
                chain(ts(z[:], act_in[:, 0:P], conv2[ROWS, 0:1], None, ALU.mult))
                chain(stt(out=z[:], in0=act_in[:, 1:P + 1], scalar=conv2[ROWS, 1:2], in1=z[:],
                          op0=ALU.mult, op1=ALU.add))
                stt(out=z[:], in0=act_in[:, 2:P + 2], scalar=conv2[ROWS, 2:3], in1=z[:],
                    op0=ALU.mult, op1=ALU.add).then_inc(z_ready, 1)
                dve.wait_ge(z_in_psum, 1)
                stt(out=final[:], in0=small[0:NB, 0:P], scalar=conv2_b[0:NB, 0:1],
                    in1=rows_in[0:NB, 1:P + 1], op0=ALU.add, op1=ALU.add).then_inc(final_ready, 1)
                dve.wait_ge(exp_ready, 1)
                chain(nc.vector.reciprocal(total[:], total[:]))
                ts(weight_rows[:], weight_rows[:], total[:, 0:1], None, ALU.mult).then_inc(weight_ready, 1)
                dve.wait_ge(weights_in_psum, 1)
                chain(nc.vector.tensor_copy(weights[:], small[:, 0:NB]))
                dve.wait_ge(xb_ready, 1)

                def add(b):
                    dve.wait_ge(y_ready, b + 1)
                    return stt(out=net.r[:, b, :], in0=net.banks[Y[b]][:, 0:D], scalar=weights[:, b:b + 1],
                               in1=xb[:, b, :], op0=ALU.mult, op1=ALU.add)

                finish.run_dve(dve, chain, add)

            @block.gpsimd
            def _(pool):
                nc.gpsimd.memset(rows_in[:], 0.0)
                nc.gpsimd.memset(act_in[:], 0.0).then_inc(zeros_ready, 1)
                pool.wait_ge(net.ready["l2_attn"], 16)
                nc.gpsimd.tensor_tensor(xb[:], net.x[:], w["bo"].unsqueeze(1).broadcast_to([P, NB, D]),
                                        ALU.add).then_inc(xb_ready, 1)
    net.end_sublayer()



def l2_xattn(net, prefetch):
    nc = net.nc
    w = net.weights("l2_xattn")
    wq, wk, wv, wo = (tiles(w[n], FT) for n in ("wq", "wk", "wv", "wo"))
    with ExitStack() as sub:
        sig = net.signals(24)
        qk_in_psum, q_ready, k_ready, v_in_psum, v_ready, xb_ready, dve_steps = sig[17:]
        finish = Finish(net, sig[13:17])
        heads = Heads16(net, sub, sig[:9], masked=False, scale=DH ** -0.5)
        back = OutputProjection(net, sub, heads, wo, sig[9:13])
        xb = net.scratch(sub)("x_plus_bias", [P, NB, D])
        with nc.Block() as block:
            @block.sync
            def _(sp):
                prefetch(sp)

            @block.tensor
            def _(pe):
                pe.wait_ge(net.ready["l2_xattn"], 16)
                for m in range(4):
                    project(pe, net.banks[2 + m][:], wk, net.ctxT, m).then_inc(qk_in_psum, 1)
                for b in range(NB):
                    project_tokens(pe, half(net, (6, 7), b), net.ctxT, b, wv).then_inc(v_in_psum, 1)
                for m in range(4):
                    pe.wait_ge(k_ready, m + 1)
                    project(pe, net.banks[2 + m][:], wq, net.xT, m).then_inc(qk_in_psum, 1)
                pe.wait_ge(q_ready, 4)
                pe.wait_ge(v_ready, NB)
                heads.run_pe(pe)
                back.run_pe(pe)
                finish.run_pe(pe)

            @block.scalar
            def _(act):
                load_table(net, ACT.Exp)
                act.wait_ge(net.ready["l2_xattn"], 16)
                for m in range(4):
                    act.wait_ge(qk_in_psum, m + 1)
                    nc.scalar.activation(heads.kT[:, m, :], net.banks[2 + m][:], ACT.Identity,
                                         bias=w["bk"][:, m:m + 1]).then_inc(k_ready, 1)
                for m in range(4):
                    act.wait_ge(qk_in_psum, m + 5)
                    nc.scalar.activation(heads.qT[:, m, :], net.banks[2 + m][:], ACT.Identity,
                                         bias=w["bq"][:, m:m + 1]).then_inc(q_ready, 1)
                heads.run_act(act)
                back.run_act(act)
                finish.run_act(act)

            @block.vector
            def _(dve):
                chain = Chain(dve, dve_steps)
                dve.wait_ge(net.ready["l2_xattn"], 16)
                for b in range(NB):
                    dve.wait_ge(v_in_psum, PAIR_DONE[b])
                    nc.vector.tensor_tensor(net.v1[:, b, :, 0:DH],
                                            half(net, (6, 7), b).rearrange("p (h d) -> p h d", h=NH),
                                            w["bv"].rearrange("p (h d) -> p h d", h=NH),
                                            ALU.add).then_inc(v_ready, 1)
                heads.run_dve(dve, chain)
                back.run_dve(dve)
                dve.wait_ge(xb_ready, 1)

                def add(b):
                    dve.wait_ge(back.y_ready, b + 1)
                    return nc.vector.tensor_tensor(net.r[:, b, :], xb[:, b, :], back.y(b), ALU.add)

                finish.run_dve(dve, chain, add)

            @block.gpsimd
            def _(pool):
                pool.wait_ge(net.ready["l2_xattn"], 16)
                nc.gpsimd.tensor_tensor(xb[:], net.x[:], w["bo"].unsqueeze(1).broadcast_to([P, NB, D]),
                                        ALU.add).then_inc(xb_ready, 1)
    net.end_sublayer()



def l2_ffn(net, prefetch):
    nc = net.nc
    w = net.weights("l2_ffn")
    router, sw1, sw3, sw2 = tiles(w["router"], FT), tiles(w["sw1"], FT), tiles(w["sw3"], FT), tiles(w["sw2"], 4)
    with ExitStack() as sub:
        sb = net.scratch(sub)
        (logits_in_psum, sigmoid_ready, gate_in_psum, silu_ready, up_in_psum, swiglu_ready,
         shared_in_psum, shared_taken, dve_steps) = net.signals(17)[8:]
        finish = Finish(net, net.signals(8)[4:])
        experts = Experts(net, sub, "l2_ffn", net.signals(4), 2, ACT.Gelu)
        s, gates, chosen, rank = (sb(n, [P, NB, EXPERTS]) for n in ("sigmoid", "gates", "chosen", "rank"))
        greater, equal = (sb(n, [P, NB, EXPERTS, EXPERTS]) for n in ("greater", "equal"))
        total, usable, spare = (sb(n, [P, NB]) for n in ("gate_sum", "usable", "spare"))
        silu, swiglu = sb("silu", [P, 4, T]), sb("swiglu", [P, 4, T])
        logits = net.banks[0][:, 0:NB * EXPERTS].rearrange("p (b e) -> p b e", b=NB)
        GATE, UP, SHARED = (2, 3), (4, 5), (6, 7)
        with nc.Block() as block:
            @block.sync
            def _(sp):
                prefetch(sp)

            @block.tensor
            def _(pe):
                pe.wait_ge(net.ready["l2_ffn"], 16)
                for b in range(NB):
                    mm = project_tokens(pe, logits[:, b, :], net.xT, b, router)
                mm.then_inc(logits_in_psum, 1)
                for m in range(4):
                    if m >= 2:
                        pe.wait_ge(swiglu_ready, m - 1)
                    project(pe, net.banks[GATE[m % 2]][:], sw1, net.xT, m).then_inc(gate_in_psum, 1)
                    project(pe, net.banks[UP[m % 2]][:], sw3, net.xT, m).then_inc(up_in_psum, 1)
                pe.wait_ge(swiglu_ready, 4)
                for b in range(NB):
                    project_tokens(pe, half(net, SHARED, b), swiglu, b, sw2).then_inc(shared_in_psum, 1)
                experts.run_pe(pe, before_out=lambda: pe.wait_ge(shared_taken, NB))
                finish.run_pe(pe)

            @block.scalar
            def _(act):
                act.wait_ge(logits_in_psum, 1)
                nc.scalar.activation(s[:], logits, ACT.Sigmoid).then_inc(sigmoid_ready, 1)
                for m in range(4):
                    act.wait_ge(gate_in_psum, m + 1)
                    nc.scalar.activation(silu[:, m, :], net.banks[GATE[m % 2]][:],
                                         ACT.Silu).then_inc(silu_ready, 1)
                experts.run_act(act)
                finish.run_act(act)

            @block.vector
            def _(dve):
                chain = Chain(dve, dve_steps)
                tt, ts = nc.vector.tensor_tensor, nc.vector.tensor_scalar
                wide = [P, NB, EXPERTS]
                dve.wait_ge(net.ready["l2_ffn"], 16)
                for m in range(4):
                    dve.wait_ge(silu_ready, m + 1)
                    dve.wait_ge(up_in_psum, m + 1)
                    tt(swiglu[:, m, :], silu[:, m, :], net.banks[UP[m % 2]][:], ALU.mult).then_inc(swiglu_ready, 1)
                dve.wait_ge(sigmoid_ready, 1)
                chain(tt(rank[:], s[:], w["router_bias"].unsqueeze(1).broadcast_to(wide), ALU.add))
                chain(nc.vector.tensor_copy(gates[:], rank[:]))
                top2_dve(net, chain, gates, chosen, greater, equal, rank)
                chain(tt(gates[:], s[:], chosen[:], ALU.mult))
                chain(nc.vector.reduce_sum(total[:], gates[:], AX_X))
                chain(ts(usable[:], total[:], 1e-9, None, ALU.is_gt))
                chain(ts(total[:], total[:], 1e-9, None, ALU.add))
                chain(nc.vector.reciprocal(total[:], total[:]))
                chain(tt(total[:], total[:], usable[:], ALU.mult))
                chain(tt(gates[:], gates[:], total[:].unsqueeze(2).broadcast_to(wide), ALU.mult))
                chain(ts(spare[:], usable[:], -0.5, 0.5, ALU.mult, ALU.add))
                chain(tt(chosen[:], chosen[:], spare[:].unsqueeze(2).broadcast_to(wide), ALU.mult))
                chain(tt(gates[:], gates[:], chosen[:], ALU.add))
                for b in range(NB):
                    dve.wait_ge(shared_in_psum, PAIR_DONE[b])
                    tt(net.r[:, b, :], net.x[:, b, :], half(net, SHARED, b), ALU.add).then_inc(shared_taken, 1)
                dve.wait_ge(shared_taken, NB)
                finish.run_dve(dve, chain, experts.run_dve(dve, gates, net.r))
    net.end_sublayer()



DI, STATES, TAPS = 512, 16, 4
DT_ = DI // P


def l3_attn(net, prefetch):
    nc = net.nc
    w = net.weights("l3_attn")
    w_in, w_x, w_dt, w_out = tiles(w["w_in"], FT), tiles(w["w_x"], DT_), tiles(w["w_dt"], DT_), tiles(w["w_out"], DT_)
    conv_w = w["conv_w"].rearrange("p (m k) -> p m k", m=DT_)
    with ExitStack() as sub:
        sb = net.scratch(sub)
        u = sb("conv_silu", [P, DT_, T])
        zs = sb("silu_z", [P, DT_, T])
        dt = sb("step", [P, DT_, T])
        dtu = sb("step_times_input", [P, DT_, T])
        bc_rest = [sb(f"b_and_c_rest{i}", [2 * STATES, T]) for i in range(2)]
        PARTS = 6 * STATES
        part = sb("b_and_c_part", [2 * STATES, T], BF16)
        bc, pick = sb("b_and_c_parts", [PARTS, T], BF16), sb("pick_row", [PARTS, 2 * STATES], BF16)
        a = sb("minus_exp_a_log", [P, DT_ * STATES])
        c_row = [sb(f"c_on_all_rows{i}", [P, T]) for i in range(2)]
        room = net.e_room
        padded = room[:, 0:DT_ * NB * (P + 3)].rearrange("p (m b t) -> p m b t", m=DT_, b=NB)
        at = DT_ * NB * (P + 3)
        conv, delta, ex, one_ex, lost, positive = (
            room[:, at + k * DT_ * T:at + (k + 1) * DT_ * T].rearrange("p (m t) -> p m t", m=DT_)
            for k in range(6))
        ring = [room[:, k * DT_ * T:(k + 1) * DT_ * T].rearrange("p (m t) -> p m t", m=DT_)
                for k in range(8)]
        Y = (4, 5, 6, 7)
        decay, drive, state, out = ring[0:2], ring[2:4], ring[4:6], ring[6:8]
        (zeros_ready, in_in_psum, in_taken, conv_ready, u_ready,
         x_in_psum, delta_ready, bc_ready, dt_in_psum, positive_ready, exp_ready, log_ready, dt_ready, a_ready, b_in_psum, c_in_psum, drive_ready,
         c_ready, decay_ready, state_ready, out_ready, summed, yz_ready, y_ready,
         dve_steps, act_steps) = net.signals(30)[4:]
        finish = Finish(net, net.signals(4), banks=(2, 3))
        with nc.Block() as block:
            @block.sync
            def _(sp):
                prefetch(sp)

            @block.tensor
            def _(pe):
                pe.wait_ge(net.ready["l3_attn"], 16)
                for m in range(2 * DT_):
                    if m >= 4:
                        pe.wait_ge(in_taken, m - 3)
                    project(pe, net.banks[2 + m % 4][:], w_in, net.xT, m).then_inc(in_in_psum, 1)
                pe.wait_ge(in_taken, 2 * DT_)
                pe.wait_ge(u_ready, DT_)
                for m in range(DT_):
                    project(pe, net.banks[2 + m][:], w_x, u, m).then_inc(x_in_psum, 1)
                for k in range(DT_):
                    mm = pe.matmul(net.banks[6][0:2 * STATES, :], w_x[:, k, DI:DI + 2 * STATES], u[:, k, :],
                                   start=k == 0, stop=k == DT_ - 1)
                mm.then_inc(x_in_psum, 1)
                pe.wait_ge(delta_ready, DT_)
                for m in range(DT_):
                    project(pe, net.banks[2 + m][:], w_dt, delta, m).then_inc(dt_in_psum, 1)
                pe.wait_ge(bc_ready, 1)
                pe.wait_ge(positive_ready, DT_)
                pe.wait_ge(exp_ready, DT_)

                def add_up(s):
                    pe.wait_ge(out_ready, s + 1)
                    for m in range(DT_):
                        mm = pe.matmul(net.banks[m][:], net.ident[:], out[s % 2][:, m, :],
                                       start=s == 0, stop=s == STATES - 1)
                    mm.then_inc(summed, 1)

                def spread_out(s):
                    if s >= 2:
                        pe.wait_ge(drive_ready, s - 1)
                        pe.wait_ge(c_ready, s - 1)
                    for bank, col, done in ((4, s, b_in_psum), (6, STATES + s, c_in_psum)):
                        pe.matmul(net.banks[bank + s % 2][:],
                                  pick[:, col:col + 1].broadcast_to([PARTS, P]),
                                  bc[:], start=True, stop=True).then_inc(done, 1)

                spread_out(0)
                spread_out(1)
                for s in range(STATES):
                    add_up(s)
                    if s + 2 < STATES:
                        spread_out(s + 2)
                pe.wait_ge(yz_ready, DT_)
                for b in range(NB):
                    project_tokens(pe, net.banks[Y[b]][:, 0:D], dtu, b, w_out).then_inc(y_ready, 1)
                finish.run_pe(pe)

            @block.scalar
            def _(act):
                chain = Chain(act, act_steps)
                act.wait_ge(net.ready["l3_attn"], 16)
                chain(nc.scalar.activation(a[:], w["a_log"], ACT.Exp))
                nc.scalar.mul(a[:], a[:], -1.0).then_inc(a_ready, 1)
                act.wait_ge(zeros_ready, 1)
                for m in range(DT_):
                    act.wait_ge(in_in_psum, m + 1)
                    nc.scalar.copy(padded[:, m, :, 3:P + 3],
                                   net.banks[2 + m][:].rearrange("p (b t) -> p b t", b=NB)).then_inc(in_taken, 1)
                for m in range(DT_):
                    act.wait_ge(in_in_psum, DT_ + m + 1)
                    nc.scalar.activation(zs[:, m, :], net.banks[2 + m][:], ACT.Silu).then_inc(in_taken, 1)
                for m in range(DT_):
                    act.wait_ge(conv_ready, m + 1)
                    nc.scalar.activation(u[:, m, :], conv[:, m, :], ACT.Silu,
                                         bias=w["conv_b"][:, m:m + 1]).then_inc(u_ready, 1)
                for m in range(DT_):
                    act.wait_ge(x_in_psum, m + 1)
                    nc.scalar.copy(delta[:, m, :], net.banks[2 + m][:]).then_inc(delta_ready, 1)
                for m in range(DT_):
                    act.wait_ge(dt_in_psum, m + 1)
                    chain(nc.scalar.activation(ex[:, m, :], net.banks[2 + m][:], ACT.Abs,
                                               bias=w["dt_b"][:, m:m + 1]))
                    nc.scalar.activation(ex[:, m, :], ex[:, m, :], ACT.Exp, scale=-1.0).then_inc(exp_ready, 1)
                act.wait_ge(exp_ready, DT_)
                nc.scalar.activation(dt[:], ex, ACT.Ln, bias=1.0).then_inc(log_ready, 1)
                load_table(net, ACT.Exp)
                act.wait_ge(dt_ready, 1)
                act.wait_ge(a_ready, 1)
                for s in range(STATES):
                    if s >= 2:
                        act.wait_ge(state_ready, s - 1)
                        act.wait_ge(out_ready, s - 1)
                    for m in range(DT_):
                        nc.scalar.activation(decay[s % 2][:, m, :], dt[:, m, :], ACT.Exp,
                                             scale=a[:, m * STATES + s:m * STATES + s + 1]).then_inc(decay_ready, 1)
                    act.wait_ge(c_in_psum, s + 1)
                    nc.scalar.copy(c_row[s % 2][:], net.banks[6 + s % 2][:]).then_inc(c_ready, 1)
                finish.run_act(act)

            @block.vector
            def _(dve):
                chain = Chain(dve, dve_steps)
                tt, ts, stt = nc.vector.tensor_tensor, nc.vector.tensor_scalar, nc.vector.scalar_tensor_tensor
                dve.wait_ge(net.ready["l3_attn"], 16)
                for m in range(DT_):
                    dve.wait_ge(in_taken, m + 1)
                    acc = conv[:, m, :].rearrange("p (b t) -> p b t", b=NB)
                    chain(ts(acc, padded[:, m, :, 0:P], conv_w[:, m, 0:1], None, ALU.mult))
                    for k in range(1, TAPS):
                        ins = stt(out=acc, in0=padded[:, m, :, k:k + P], scalar=conv_w[:, m, k:k + 1],
                                  in1=acc, op0=ALU.mult, op1=ALU.add)
                        if k < TAPS - 1:
                            chain(ins)
                    ins.then_inc(conv_ready, 1)
                dve.wait_ge(x_in_psum, DT_ + 1)
                n = 2 * STATES
                chain(nc.vector.tensor_copy(bc_rest[0][:], net.banks[6][0:n, :]))
                for k in range(3):
                    chain.step(nc.vector.tensor_copy(pick[n * k:n * (k + 1), :], net.ident[0:n, 0:n]))
                    chain(nc.vector.tensor_copy(bc[0:n, :] if k == 0 else part[:], bc_rest[k % 2][:]))
                    if k:
                        chain.step(nc.vector.tensor_copy(bc[n * k:n * (k + 1), :], part[:]))
                    if k < 2:
                        chain(tt(bc_rest[(k + 1) % 2][:], bc_rest[k % 2][:],
                                 bc[0:n, :] if k == 0 else part[:], ALU.subtract))
                chain.settle()
                nc.vector.engine_nop().then_inc(bc_ready, 1)
                for m in range(DT_):
                    dve.wait_ge(dt_in_psum, m + 1)
                    dve.wait_ge(exp_ready, m + 1)
                    ts(positive[:, m, :], net.banks[2 + m][:], w["dt_b"][:, m:m + 1], 0.0, ALU.add,
                       ALU.max).then_inc(positive_ready, 1)
                chain(ts(one_ex, ex, 1.0, None, ALU.add))
                chain(stt(out=lost, in0=one_ex, scalar=-1.0, in1=ex, op0=ALU.add, op1=ALU.subtract))
                dve.wait_ge(log_ready, 1)
                dve.wait_ge(positive_ready, DT_)
                chain(tt(dt[:], dt[:], positive, ALU.add))
                chain(tt(dt[:], dt[:], lost, ALU.subtract))
                nc.vector.engine_nop().then_inc(dt_ready, 1)
                chain(tt(dtu[:], dt[:], u[:], ALU.mult))
                for s in range(STATES):
                    dve.wait_ge(b_in_psum, s + 1)
                    if s >= 2:
                        dve.wait_ge(state_ready, s - 1)
                    tt(drive[s % 2], dtu[:],
                       net.banks[4 + s % 2][:].unsqueeze(1).broadcast_to([P, DT_, T]),
                       ALU.mult).then_inc(drive_ready, 1)
                    dve.wait_ge(decay_ready, DT_ * (s + 1))
                    chain(nc.vector.memset(decay[s % 2].rearrange("p m (b t) -> p (m b) t", b=NB)[:, :, 0],
                                           0.0))
                    dve.wait_ge(drive_ready, s + 1)
                    if s >= 2:
                        dve.wait_ge(out_ready, s - 1)
                    nc.vector.tensor_tensor_scan(state[s % 2].rearrange("p m t -> p (m t)"),
                                                 decay[s % 2].rearrange("p m t -> p (m t)"),
                                                 drive[s % 2].rearrange("p m t -> p (m t)"),
                                                 0.0, ALU.mult, ALU.add).then_inc(state_ready, 1)
                dve.wait_ge(summed, STATES)
                for m in range(DT_):
                    chain(stt(out=u[:, m, :], in0=u[:, m, :], scalar=w["d"][:, m:m + 1],
                              in1=net.banks[m][:], op0=ALU.mult, op1=ALU.add))
                    tt(dtu[:, m, :], u[:, m, :], zs[:, m, :], ALU.mult).then_inc(yz_ready, 1)

                def add(b):
                    dve.wait_ge(y_ready, b + 1)
                    return tt(net.r[:, b, :], net.x[:, b, :], net.banks[Y[b]][:, 0:D], ALU.add)

                finish.run_dve(dve, chain, add)

            @block.gpsimd
            def _(pool):
                nc.gpsimd.memset(padded, 0.0).then_inc(zeros_ready, 1)
                for s in range(STATES):
                    pool.wait_ge(state_ready, s + 1)
                    pool.wait_ge(c_ready, s + 1)
                    if s >= 2:
                        pool.wait_ge(summed, s - 1)
                    nc.gpsimd.tensor_tensor(out[s % 2], state[s % 2],
                                            c_row[s % 2][:].unsqueeze(1).broadcast_to([P, DT_, T]),
                                            ALU.mult).then_inc(out_ready, 1)
    net.end_sublayer()



def l3_xattn(net, prefetch):
    nc = net.nc
    net.stage = "l3_xattn"
    with ExitStack() as sub:
        kv = net.scratch(sub)("kv", [P, NB, FT, D])
        kv_in_psum, kv_ready, y_ready, dve_steps = net.signals(8)[4:]
        finish = Finish(net, net.signals(4))
        with nc.Block() as block:
            @block.sync
            def _(sp):
                prefetch(sp)

            @block.tensor
            def _(pe):
                for b in range(NB):
                    for m in range(FT):
                        mm = pe.matmul(net.banks[2 + b][:, m * D:(m + 1) * D], net.ctx[:, b, m * P:(m + 1) * P],
                                       net.ctx[:, b, :], start=True, stop=True)
                    mm.then_inc(kv_in_psum, 1)
                for b in range(NB):
                    pe.wait_ge(kv_ready, b + 1)
                    project_tokens(pe, half(net, (6, 7), b), net.xT, b, kv[:, b, :, :]).then_inc(y_ready, 1)
                finish.run_pe(pe)

            @block.scalar
            def _(act):
                for b in range(NB):
                    act.wait_ge(kv_in_psum, b + 1)
                    nc.scalar.activation(kv[:, b, :, :].rearrange("p f d -> p (f d)"), net.banks[2 + b][:],
                                         ACT.Copy, scale=1.0 / P).then_inc(kv_ready, 1)
                finish.run_act(act)

            @block.vector
            def _(dve):
                chain = Chain(dve, dve_steps)

                def add(b):
                    dve.wait_ge(y_ready, PAIR_DONE[b])
                    return nc.vector.tensor_tensor(net.r[:, b, :], net.x[:, b, :], half(net, (6, 7), b),
                                                   ALU.add)

                finish.run_dve(dve, chain, add)
    net.end_sublayer()



BITS = 4 * 1024 + 8 * 1024 + 8 * D
BITS_AT = (2 * 1024 + 8 * 1024 + 8 * D)


def load_bits(net, sp):
    room = net.e_room[:, BITS_AT:BITS_AT + BITS // 4].bitcast(I32)
    sp.dma_start(room, net.params["l3_ffn_bits"]).then_inc(net.expert_ready[0], 16)


def l3_ffn(net, prefetch):
    nc = net.nc
    w = net.weights("l3_ffn")
    with ExitStack() as sub:
        sb = net.scratch(sub)
        scale = sb("scales", [P, 2])
        h0, h1 = sb("hidden0", [P, 8, T]), sb("hidden1", [P, 8, T])
        room = net.e_room
        w0 = tiles(room[:, 0:2048], 2)
        w1 = tiles(room[:, 2048:2048 + 8192], 8)
        w2 = tiles(room[:, 2048 + 8192:BITS_AT], 8)
        bits = room[:, BITS_AT:BITS_AT + BITS // 4].bitcast(U8)
        k0, k1, k2 = tiles(bits[:, 0:4096], 4), tiles(bits[:, 4096:4096 + 8192], 8), tiles(bits[:, 4096 + 8192:BITS], 8)
        (w0_ready, w1_ready, w2_ready, scale_ready, h0_in_psum, h0_ready, h1_in_psum, h1_ready, y_ready,
         dve_steps) = net.signals(14)[4:]
        finish = Finish(net, net.signals(4))
        loads = 16 * (1 + sum(s in EXPERT_NETS for s in LAST_LOOP if s in RUN))
        with nc.Block() as block:
            @block.sync
            def _(sp):
                prefetch(sp)

            @block.tensor
            def _(pe):
                pe.wait_ge(w0_ready, 1)
                for m in range(8):
                    if m >= 4:
                        pe.wait_ge(h0_ready, m - 3)
                    project(pe, net.banks[2 + m % 4][:], w0, net.xT, m).then_inc(h0_in_psum, 1)
                pe.wait_ge(h0_ready, 8)
                pe.wait_ge(w1_ready, 8)
                for m in range(8):
                    if m >= 4:
                        pe.wait_ge(h1_ready, m - 3)
                    project(pe, net.banks[2 + m % 4][:], w1, h0, m).then_inc(h1_in_psum, 1)
                pe.wait_ge(h1_ready, 8)
                pe.wait_ge(w2_ready, 1)
                for b in range(NB):
                    project_tokens(pe, half(net, (6, 7), b), h1, b, w2).then_inc(y_ready, 1)

            @block.scalar
            def _(act):
                act.wait_ge(scale_ready, 1)
                for m in range(8):
                    act.wait_ge(h0_in_psum, m + 1)
                    nc.scalar.activation(h0[:, m, :], net.banks[2 + m % 4][:], ACT.Relu,
                                         scale=scale[:, 0:1]).then_inc(h0_ready, 1)
                for m in range(8):
                    act.wait_ge(h1_in_psum, m + 1)
                    nc.scalar.activation(h1[:, m, :], net.banks[2 + m % 4][:], ACT.Relu,
                                         scale=scale[:, 1:2]).then_inc(h1_ready, 1)
                finish.run_act(act)

            @block.vector
            def _(dve):
                chain = Chain(dve, dve_steps)
                dve.wait_ge(net.expert_ready[0], loads)
                nc.vector.tensor_tensor(w0, k0[:, 0:2, :], k0[:, 2:4, :], ALU.subtract).then_inc(w0_ready, 1)
                dve.wait_ge(net.ready["l3_ffn"], 16)
                chain(nc.vector.tensor_scalar(scale[:, 0:1], w["s0"], 4.0, None, ALU.mult))
                nc.vector.tensor_scalar(scale[:, 1:2], w["s1"], 2.0, None, ALU.mult).then_inc(scale_ready, 1)
                for k in range(8):
                    nc.vector.tensor_scalar(w1[:, k, :], k1[:, k, :], 2.0, -1.0, ALU.mult,
                                            ALU.add).then_inc(w1_ready, 1)

                def add(b):
                    dve.wait_ge(y_ready, PAIR_DONE[b])
                    return nc.vector.scalar_tensor_tensor(
                        out=net.r[:, b, :], in0=half(net, (6, 7), b), scalar=w["s2"], in1=net.x[:, b, :],
                        op0=ALU.mult, op1=ALU.add)

                finish.run_dve(dve, chain, add)

            @block.gpsimd
            def _(pool):
                pool.wait_ge(net.expert_ready[0], loads)
                nc.gpsimd.tensor_scalar(w2, k2, 2.0, -1.0, ALU.mult, ALU.add).then_inc(w2_ready, 1)
    net.end_sublayer()


EXPERT_COLS = {"l0_ffn_experts": 2048, "l1_ffn": 4096, "l2_ffn": 1024}
EXPERT_NETS = tuple(EXPERT_COLS)
EXPERT_LOADS = {s: load_experts(s) for s in EXPERT_NETS}
EXPERT_LOADS["l3_ffn"] = load_bits
EXPERT_ROOM = 16384
BODIES = {"l0_attn": l0_attn, "l0_xattn": l0_xattn, "l0_ffn_attention": l0_ffn_attention,
          "l0_ffn_experts": l0_ffn_experts,
          "l1_attn": l1_attn, "l1_xattn": l1_xattn, "l1_ffn": l1_ffn,
          "l2_attn": l2_attn, "l2_xattn": l2_xattn, "l2_ffn": l2_ffn,
          "l3_attn": l3_attn, "l3_xattn": l3_xattn, "l3_ffn": l3_ffn}
RUN = list(BODIES)


def expert_parameters(i):
    import numpy as np

    def blocks(w1, w2):
        return np.concatenate([p for e in range(EXPERTS) for p in (rows(w1[e]), rows(w2[e]))], axis=1)

    bits = [rows(i[f"L3_ffn_k{k}"].view(np.uint8)) for k in range(3)]
    return {"l3_ffn_bits": np.concatenate(bits, axis=1).view(np.int32),
            "l0_ffn_experts_experts": blocks(i["L0_ffn_w1"], i["L0_ffn_w2"]),
            "l1_ffn_experts": blocks(i["L1_ffn_W1"], i["L1_ffn_W2"]),
            "l2_ffn_experts": blocks(i["L2_ffn_ew1"], i["L2_ffn_ew2"])}



SUBLAYERS = ["l0_attn", "l0_xattn", "l0_ffn_attention", "l0_ffn_experts", "l1_attn", "l1_xattn", "l1_ffn",
             "l2_attn", "l2_xattn", "l2_ffn", "l3_attn", "l3_xattn", "l3_ffn"]
LOOPS = [SUBLAYERS[:2], SUBLAYERS[2:4], SUBLAYERS[4:]]
LAST_LOOP = LOOPS[2]
WANTS_XT = ("l0_attn", "l0_xattn", "l1_xattn", "l1_ffn", "l2_attn", "l2_xattn", "l2_ffn", "l3_attn",
            "l3_xattn", "l3_ffn")
ACROSS = ("l0_ffn_attention", "l0_ffn_experts")
GROUPS = 4


def decoder(nc, x, ctx, out, params, cols, consts):
    with ExitStack() as cx:
        net = Net(nc, cx, params, cols, consts)
        io_done = cx.enter_context(nc.semaphore("io_done"))
        constants_ready = cx.enter_context(nc.semaphore("constants_ready"))
        ctxT_in_psum = cx.enter_context(nc.semaphore("ctxT_in_psum"))
        xT_in_psum = cx.enter_context(nc.semaphore("xT_in_psum"))
        net.ready = {s: cx.enter_context(nc.semaphore(f"{s}_weights_ready")) for s in SUBLAYERS}
        net.expert_ready = [cx.enter_context(nc.semaphore(f"expert{e}_weights_ready"))
                            for e in range(EXPERTS)]
        net.out_stored = cx.enter_context(nc.semaphore("out_stored"))
        between = [nc.dram_tensor(f"stream{i}", x.shape, F32).ap() for i in range(2)]

        def load_weights(sp, sub):
            n = sum(c for _, c in cols.get(sub, []))
            if not n:
                return
            room = net.w_room[SUBLAYERS.index(sub) % 2]
            sp.dma_start(room[:, 0:n], params[sub]).then_inc(net.ready[sub], 16)

        with nc.Block() as block:
            @block.sync
            def _(sp):
                for name, dst in (("ident", net.ident), ("identb", net.identb),
                                  ("mates_qk", net.mates_qk), ("mates_kq", net.mates_kq),
                                  ("keep_kq", net.keep_kq), ("before", net.before),
                                  ("causal_qk", net.causal_qk), ("causal_kq", net.causal_kq),
                                  ("inside", net.inside)):
                    sp.dma_start(dst[:].rearrange("p a k -> p (a k)") if len(dst.shape) == 3 else dst[:],
                                 consts[name]).then_inc(constants_ready, 16)
                sp.wait_ge(constants_ready, 16 * 9)

            @block.gpsimd
            def _(pool):
                for buf in net.negmax:
                    nc.gpsimd.memset(buf[:], 0.0)
                nc.gpsimd.memset(net.v1[:], 1.0)

        loops = [names for names in ([n for n in part if n in RUN] for part in LOOPS) if names]
        for k, names in enumerate(loops):
            src = x if k == 0 else between[k - 1]
            dst = out if k == len(loops) - 1 else between[k]
            group_loop(net, names, src, dst, ctx, load_weights, io_done, ctxT_in_psum, xT_in_psum)


def group_loop(net, names, src, dst, ctx, load_weights, io_done, ctxT_in_psum, xT_in_psum):
    nc = net.nc
    across = names[0] in ACROSS
    ctx_g = ctx.rearrange("(g b) t d -> g t b d", b=NB)

    def group_views(a, g):
        if across:
            v = a.rearrange("s (g b p) d -> g b p s d", b=NB, p=P // SEQUENCES)[g]
        else:
            v = a.rearrange("(g b) t d -> g b t d", b=NB)[g]
        return [v[b] for b in range(NB)]

    with nc.Fori(0, GROUPS) as g:
        with nc.Block() as block:
            @block.sync
            def _(sp):
                if not across:
                    sp.dma_start(net.ctx[:], ctx_g[g]).then_inc(io_done, 16)
                for b, view in enumerate(group_views(src, g)):
                    sp.dma_start(net.x[:, b, :], view).then_inc(io_done, 16)
                load_weights(sp, names[0])
                if names[0] in EXPERT_LOADS:
                    EXPERT_LOADS[names[0]](net, sp)
                sp.wait_ge(io_done, 16 * (NB + (not across)))

            @block.tensor
            def _(pe):
                pe.wait_ge(io_done, 16 * (NB + (not across)))
                if not across:
                    transposes(pe, net, net.ctx, (0, 1), ctxT_in_psum)
                if names[0] in WANTS_XT:
                    transposes(pe, net, net.x, (2, 3), xT_in_psum)

            @block.scalar
            def _(act):
                if not across:
                    act.wait_ge(ctxT_in_psum, 1)
                    nc.scalar.copy(net.ctxT[:, 0, :], net.banks[0][:])
                if names[0] in WANTS_XT:
                    act.wait_ge(xT_in_psum, 1)
                    nc.scalar.copy(net.xT[:, 0, :], net.banks[2][:])

            @block.vector
            def _(dve):
                if not across:
                    dve.wait_ge(ctxT_in_psum, 2)
                    nc.vector.tensor_copy(net.ctxT[:, 1, :], net.banks[1][:])
                if names[0] in WANTS_XT:
                    dve.wait_ge(xT_in_psum, 2)
                    nc.vector.tensor_copy(net.xT[:, 1, :], net.banks[3][:])

        for i, name in enumerate(names):
            def prefetch(sp, i=i):
                if i + 1 < len(names):
                    load_weights(sp, names[i + 1])
                    if names[i + 1] in EXPERT_LOADS:
                        EXPERT_LOADS[names[i + 1]](net, sp)
            net.turn_next = i + 1 < len(names) and names[i + 1] in WANTS_XT
            BODIES[name](net, prefetch)

        with nc.Block() as block:
            @block.sync
            def _(sp):
                for b, view in enumerate(group_views(dst, g)):
                    sp.dma_start(view, net.x[:, b, :]).then_inc(net.out_stored, 16)
                sp.wait_ge(net.out_stored, 16 * NB)
        nums = [s.num for s in [io_done, ctxT_in_psum, xT_in_psum, net.out_stored,
                                *net.ready.values(), *net.expert_ready]]
        nc.all_engine_barrier(sems_to_clear=range(min(nums), max(nums) + 1))



def rows(a):
    import numpy as np
    k, n = a.shape
    return np.ascontiguousarray(a.reshape(k // P, P, n).transpose(1, 0, 2)).reshape(P, -1)


def spread(v):
    import numpy as np
    v = np.asarray(v).reshape(1, -1)
    return np.broadcast_to(v, (P, v.shape[1]))


def column(v):
    return v.reshape(-1, P).T


def slots(a, row=0.0):
    import numpy as np
    out = np.zeros((*a.shape[:-1], NH, SLOT), a.dtype)
    out[..., 0:DH] = a.reshape(*a.shape[:-1], NH, DH)
    out[..., SHIFT_ROW] = row
    return out.reshape(*a.shape[:-1], NH * SLOT)


def parameters(i):
    import numpy as np
    proj = np.zeros((8, P, P), np.float32)
    for h in range(NH):
        at = (h % 8) * DH
        proj[h // 2, at:at + DH, (h % 2) * 64:(h % 2) * 64 + 64] = i["L0_attn_proj"][h]
    out = {
        "l0_attn": [
            ("wqk", rows(i["L0_attn_qkv_w"][:, :2 * D])), ("wv", rows(i["L0_attn_qkv_w"][:, 2 * D:])),
            ("wo", rows(i["L0_attn_out_w"])), ("bqk", column(i["L0_attn_qkv_b"][:2 * D])),
            ("bv", spread(i["L0_attn_qkv_b"][2 * D:])), ("bo", spread(i["L0_attn_out_b"])),
            ("proj", proj.transpose(1, 0, 2).reshape(P, -1))],
        "l0_xattn": [
            ("wq", rows(slots(i["L0_xattn_Wq"].T))), ("wk", rows(slots(i["L0_xattn_Wk"].T))),
            ("wv", rows(i["L0_xattn_Wv"].T)),
            ("one_rows", column(slots(np.zeros(D, np.float32), 1.0)))],
    }
    i0 = {k[len("L0_ffn_"):]: v for k, v in i.items() if k.startswith("L0_ffn_")}
    w0, b0 = i0["in_proj_w"], i0["in_proj_b"]
    out["l0_ffn_attention"] = [
        ("wq", rows(slots(w0[:D].T))), ("wk", rows(slots(w0[D:2 * D].T))), ("wv", rows(w0[2 * D:].T)),
        ("wo", rows(i0["out_proj_w"].T)), ("bq", column(slots(b0[:D]))), ("bk", column(slots(b0[D:2 * D], 1.0))),
        ("bv", spread(b0[2 * D:])), ("bo", spread(i0["out_proj_b"])),
        ("ln1_w", column(i0["ln1_w"])), ("ln1_b", column(i0["ln1_b"])),
        ("ln2_w", column(i0["ln2_w"])), ("ln2_b", column(i0["ln2_b"]))]
    out["l0_ffn_experts"] = [("router", rows(i0["router_w"].T))]
    order = [0, 2, 1, 3]
    wq = i["L1_attn_Wq"].reshape(D, Q_HEADS, HD)[:, order].reshape(D, D)
    out["l1_attn"] = [
        ("wq", rows(wq)), ("wkv", rows(np.concatenate([i["L1_attn_Wk"], i["L1_attn_Wv"]], axis=1))),
        ("wo", rows(i["L1_attn_Wo"])), ("norm_w", column(i["L1_attn_norm_w"])),
        ("gate", spread(i["L1_attn_gate"])), ("log_temperature", spread(i["L1_attn_log_temperature"]))]
    out["l1_xattn"] = [("w", column(i["L1_xattn_w"].reshape(-1))), ("u", column(i["L1_xattn_u"].reshape(-1)))]
    out["l1_ffn"] = [
        ("wr", spread(i["L1_ffn_wr"])), ("br", spread(i["L1_ffn_br"])),
        ("b1", column(i["L1_ffn_b1"].reshape(-1))), ("b2", spread(i["L1_ffn_b2"].reshape(-1)))]
    i2 = {k[len("L2_attn_"):]: v for k, v in i.items() if k.startswith("L2_attn_")}

    def down(a):
        full = np.zeros((P, a.shape[1]), np.float32)
        full[:a.shape[0]] = a
        return full

    channel = np.repeat(np.arange(CONV), NB)
    sequence = np.tile(np.arange(NB), CONV)
    groups = (sequence[:, None] == sequence) & (channel[:, None] // 2 == channel // 2)
    out["l2_attn"] = [
        ("wqk", rows(i2["qkv_w"][:, :2 * D])), ("wv", rows(i2["qkv_w"][:, 2 * D:])),
        ("wo", rows(i2["proj_w"])), ("bo", spread(i2["proj_b"])), ("c1", spread(i2["c1"])),
        ("c2", spread(i2["c2"])), ("conv2_b", spread(i2["conv2_b"])), ("ch_w1", rows(i2["ch_w1"])),
        ("ch_w2", down(i2["ch_w2"])), ("ch_b1", down(i2["ch_b1"].reshape(-1, 1))),
        ("ch_b2", column(i2["ch_b2"])), ("groups", down(groups.astype(np.float32))),
        ("channels", down((sequence[:, None] == np.arange(NB)).astype(np.float32))),
        ("conv1", down(i2["conv1_w"].reshape(CONV, 3)[channel])),
        ("conv2", down(i2["conv2_w"].reshape(CONV, 3)[channel])),
        ("gn_g", down(i2["gn_g"][channel].reshape(-1, 1))), ("gn_b", down(i2["gn_b"][channel].reshape(-1, 1)))]
    out["l2_xattn"] = [
        ("wq", rows(slots(i["L2_xattn_Wq"]))), ("wk", rows(slots(i["L2_xattn_Wk"]))),
        ("wv", rows(i["L2_xattn_Wv"])), ("wo", rows(i["L2_xattn_Wo"])),
        ("bq", column(slots(i["L2_xattn_bq"]))), ("bk", column(slots(i["L2_xattn_bk"], 1.0))),
        ("bv", spread(i["L2_xattn_bv"])), ("bo", spread(i["L2_xattn_bo"]))]
    out["l2_ffn"] = [
        ("router", rows(i["L2_ffn_router_w"].T)), ("router_bias", spread(i["L2_ffn_router_bias"])),
        ("sw1", rows(i["L2_ffn_sw1"])), ("sw3", rows(i["L2_ffn_sw3"])), ("sw2", rows(i["L2_ffn_sw2"]))]
    i3 = {k[len("L3_attn_"):]: v for k, v in i.items() if k.startswith("L3_attn_")}

    def by_tile(a):
        return a.reshape(-1, P, a.shape[1]).transpose(1, 0, 2).reshape(P, -1)

    out["l3_attn"] = [
        ("w_in", rows(i3["in_proj_w"].T)), ("w_x", rows(i3["x_proj_w"].T)), ("w_dt", rows(i3["dt_proj_w"].T)),
        ("w_out", rows(i3["out_proj_w"].T)), ("conv_w", by_tile(i3["conv_w"][:, 0, :])),
        ("conv_b", column(i3["conv_b"])), ("dt_b", column(i3["dt_proj_b"])),
        ("a_log", by_tile(i3["A_log"])), ("d", column(i3["D"]))]
    out["l3_ffn"] = [(s, spread(i["L3_ffn_" + s])) for s in ("s0", "s1", "s2")]
    return out


def kernel(**inputs):
    import ml_dtypes
    import numpy as np
    import concourse.bacc as bacc
    from concourse.bass_utils import run_bass_kernel_spmd

    inputs = {k: np.asarray(v) for k, v in inputs.items()}
    nc = bacc.Bacc("TRN2", target_bir_lowering=False, num_devices=1)
    arrays = {}

    def dram(name, a):
        a = np.ascontiguousarray(a)
        arrays[name] = a
        return nc.dram_tensor(name, a.shape, mybir.dt.from_np(a.dtype), kind="ExternalInput").ap()

    pieces = parameters(inputs)
    experts = expert_parameters(inputs)
    cols = {s: [(n, a.shape[1]) for n, a in p] for s, p in pieces.items()}
    cols["room"] = [sum(c for _, c in cols[s]) for s in pieces]
    cols["expert_room"] = EXPERT_ROOM
    params = {s: dram(s, np.concatenate([a for _, a in p], axis=1)) for s, p in pieces.items()}
    params.update({s: dram(s, a) for s, a in experts.items()})
    key, query = np.arange(P)[:, None], np.arange(P)[None, :]
    later = np.where(key <= query, 0.0, -BIG)
    mates = (key <= query) & (key // SEQUENCES == query // SEQUENCES)
    below = np.where(mates, 0.0, -BIG)
    consts = {n: dram(n, a) for n, a in {
        "ident": np.eye(P, dtype=np.float32), "identb": np.eye(P).astype(ml_dtypes.bfloat16),
        "mates_qk": np.tile(below.T, 4).astype(ml_dtypes.bfloat16),
        "mates_kq": np.tile(below, 4).astype(ml_dtypes.bfloat16),
        "causal_qk": np.tile(later.T, 4).astype(ml_dtypes.bfloat16),
        "causal_kq": np.tile(later, 4).astype(ml_dtypes.bfloat16),
        "inside": np.tile(np.pad(np.ones(P, np.float32), 1), (P, NB)),
        "before": np.tile(np.tril(np.ones((EXPERTS, EXPERTS), np.float32), -1).reshape(1, -1), (P, 1)),
        "keep_kq": (key <= query).astype(np.float32)}.items()}
    x, ctx = dram("x", inputs["x"]), dram("ctx", inputs["ctx_1024"])
    out = nc.dram_tensor("out", inputs["x"].shape, F32, kind="ExternalOutput").ap()
    decoder(nc, x, ctx, out, params, cols, consts)
    r = run_bass_kernel_spmd(nc, [arrays], core_ids=[0])
    return r.results[0]["out"]
```
